# Optimizing a Trainium2 kernel written in Bass

```python
import numpy as np
import jax
import jax.numpy as jnp

def _softmax(x, axis=-1):
    return jax.nn.softmax(x, axis=axis)

def _gelu(x):
    return jax.nn.gelu(x, approximate=True)

def _silu(x):
    return jax.nn.silu(x)

def _sigmoid(x):
    return jax.nn.sigmoid(x)

def _layernorm(x, axis=-1, eps=1e-05):
    m = jnp.mean(x, axis=axis, keepdims=True)
    v = jnp.var(x, axis=axis, keepdims=True)
    return (x - m) / jnp.sqrt(v + eps)

def _scatter_add(tgt, idx, src, axis=0):
    return tgt.at[idx].add(src)

def _segment_sum(src, seg, n):
    return jax.ops.segment_sum(src, seg, n)
kernel_name = 'mk_decoder_preln_d4_seqx_r8_53f82c'

def setup_inputs(seed: int=0):
    np.random.seed(seed)
    _w = jnp.asarray

    def _rec_inputs():
        import jax
        import jax.numpy as jnp
        _rk = jax.random.key(seed)
        x = 7.22e-05 + 1 * jax.random.normal(jax.random.fold_in(_rk, 1), (16, 128, 128), jnp.float32)
        _lenS = 128 - jax.random.randint(jax.random.fold_in(_rk, 7), (16,), 0, max(1, 128 // 4) + 1, jnp.int32)
        _lenS2 = 128 - jax.random.randint(jax.random.fold_in(_rk, 8), (16,), 0, max(1, 128 // 4) + 1, jnp.int32)
        _ctx_1024P = jax.random.normal(jax.random.fold_in(_rk, 11), (16, 16, 128), jnp.float32)
        _ctx_1024c = jax.random.dirichlet(jax.random.fold_in(_rk, 511), 0.3 * jnp.ones((16,), jnp.float32), (16, 128))
        _ctx_1024t = jnp.einsum('bsk,bkd->bsd', _ctx_1024c, _ctx_1024P)
        _ctx_1024t = _ctx_1024t * jax.lax.rsqrt(jnp.mean(jnp.square(_ctx_1024t)) + 1e-12) * 0.953939
        ctx_1024 = 4.13588e-05 + 0.999923 * (_ctx_1024t + 0.3 * jax.random.normal(jax.random.fold_in(_rk, 611), (16, 128, 128), jnp.float32))
        _validS = jnp.arange(128)[None, :] < _lenS[:, None]
        _validS2 = jnp.arange(128)[None, :] < _lenS2[:, None]
        _causal = jnp.tril(jnp.ones((128, 128), dtype=bool))
        mask_Bx1xSxS2_bk1 = jnp.broadcast_to(_validS2[:, None, None, :], (16, 1, 128, 128))
        mask_SxS2_ik0 = jnp.where(jnp.broadcast_to(_validS2[0:1, :], (128, 128)), 0, 1).astype(jnp.int32)
        return (x, ctx_1024, mask_Bx1xSxS2_bk1, mask_SxS2_ik0)
    x, ctx_1024, mask_Bx1xSxS2_bk1, mask_SxS2_ik0 = _rec_inputs()

    def _L0_attn_setup():
        import jax, jax.numpy as jnp
        import numpy as np
        import math
        B, S, D = (4, 256, 128)
        H = 16
        HD = D // H
        R = 128
        P = 2 * R
        key = jax.random.key(seed)
        ks = jax.random.split(key, 6)
        x = jax.random.normal(ks[0], (B, S, D), dtype=jnp.float32)
        s = 0.02
        Wk = jax.random.normal(ks[1], (D, D), dtype=jnp.float32) * s
        Wq = jax.random.normal(ks[2], (D, D), dtype=jnp.float32) * s
        Wv = jax.random.normal(ks[3], (D, D), dtype=jnp.float32) * s
        Wp = jax.random.normal(ks[4], (D, D), dtype=jnp.float32) * s
        pos_emb_k = jax.random.normal(ks[5], (P, HD), dtype=jnp.float32) * 0.02
        return {'x': x, 'Wq': Wq, 'Wk': Wk, 'Wv': Wv, 'Wp': Wp, 'pos_emb_k': pos_emb_k}
    _L0_attn_all = _L0_attn_setup()
    _L0_attn_in = {k: v for k, v in _L0_attn_all.items() if k in ('Wq', 'Wk', 'Wv', 'Wp', 'pos_emb_k')}
    del _L0_attn_all

    def _L0_xattn_setup():
        import jax, jax.numpy as jnp
        import numpy as np
        BETA = 128
        NUM_HEADS = 16
        NORM = (BETA // NUM_HEADS) ** (-0.5)
        key = jax.random.key(seed)
        ks = jax.random.split(key, 6)
        B, N = (4, 256)
        D_in_q = D_in_k = D_in_v = 128
        D_out_k = D_out_v = 128
        q = jax.random.normal(ks[0], (B, N, D_in_q), dtype=jnp.float32)
        k = jax.random.normal(ks[1], (B, N, D_in_k), dtype=jnp.float32)
        v = jax.random.normal(ks[2], (B, N, D_in_v), dtype=jnp.float32)
        Wq = jax.random.normal(ks[3], (D_out_k, D_in_q), dtype=jnp.float32) * D_in_q ** (-0.5)
        Wk = jax.random.normal(ks[4], (D_out_k, D_in_k), dtype=jnp.float32) * D_in_k ** (-0.5)
        Wv = jax.random.normal(ks[5], (D_out_v, D_in_v), dtype=jnp.float32) * D_in_v ** (-0.5)
        return {'q': q, 'k': k, 'v': v, 'Wq': Wq, 'Wk': Wk, 'Wv': Wv}
    _L0_xattn_all = _L0_xattn_setup()
    _L0_xattn_in = {k: v for k, v in _L0_xattn_all.items() if k in ('Wq', 'Wk', 'Wv')}
    del _L0_xattn_all

    def _L0_ffn_setup():
        import jax, jax.numpy as jnp
        import numpy as np
        HIDDEN = 128
        INNER = 512

        def _weight_quant(w):
            scale = 1.0 / jnp.clip(jnp.mean(jnp.abs(w)), 1e-05)
            wq = jnp.clip(jnp.round(w * scale), -1.0, 1.0) / scale
            return w + jax.lax.stop_gradient(wq - w)

        def _act_quant(x):
            scale = 127.0 / jnp.clip(jnp.max(jnp.abs(x), axis=-1, keepdims=True), 1e-05)
            xq = jnp.clip(jnp.round(x * scale), -128.0, 127.0) / scale
            return x + jax.lax.stop_gradient(xq - x)

        def _bitlinear(x, w):
            return jnp.einsum('bsi,oi->bso', _act_quant(x), _weight_quant(w))
        key = jax.random.key(seed)
        k0, k1, k2, k3 = jax.random.split(key, 4)
        x = jax.random.normal(k0, (4, 256, HIDDEN), dtype=jnp.float32)
        w_gate = jax.random.normal(k1, (INNER, HIDDEN), dtype=jnp.float32) / np.sqrt(HIDDEN)
        w_up = jax.random.normal(k2, (INNER, HIDDEN), dtype=jnp.float32) / np.sqrt(HIDDEN)
        w_down = jax.random.normal(k3, (HIDDEN, INNER), dtype=jnp.float32) / np.sqrt(INNER)
        return {'x': x, 'w_gate': w_gate, 'w_up': w_up, 'w_down': w_down}
    _L0_ffn_all = _L0_ffn_setup()
    _L0_ffn_in = {k: v for k, v in _L0_ffn_all.items() if k in ('w_gate', 'w_up', 'w_down')}
    del _L0_ffn_all

    def _L1_attn_setup():
        import jax, jax.numpy as jnp
        import numpy as np
        B, S, D = (4, 256, 128)
        H, K = (16, 64)
        EPS = 0.001
        key = jax.random.key(seed)
        ks = jax.random.split(key, 11)
        s = 0.02
        return {'x': jax.random.normal(ks[0], (B, S, D), jnp.float32), 'Wq': jax.random.normal(ks[1], (D, H, K), jnp.float32) * s, 'bq': jnp.zeros((H, K), jnp.float32), 'Wk': jax.random.normal(ks[2], (D, H, K), jnp.float32) * s, 'bk': jnp.zeros((H, K), jnp.float32), 'Wv': jax.random.normal(ks[3], (D, H, K), jnp.float32) * s, 'bv': jnp.zeros((H, K), jnp.float32), 'Wo': jax.random.normal(ks[4], (H, K, D), jnp.float32) * s, 'bo': jnp.zeros((D,), jnp.float32), 'gamma': jnp.ones((D,), jnp.float32), 'beta': jnp.zeros((D,), jnp.float32)}
    _L1_attn_all = _L1_attn_setup()
    _L1_attn_in = {k: v for k, v in _L1_attn_all.items() if k in ('Wq', 'bq', 'Wk', 'bk', 'Wv', 'bv', 'Wo', 'bo', 'gamma', 'beta')}
    del _L1_attn_all

    def _L1_xattn_setup():
        import jax, jax.numpy as jnp
        import numpy as np
        EMBED = 128
        HEADS = 16
        HEAD_DIM = EMBED // HEADS
        B, S = (4, 256)

        def _split_heads(x):
            b, s, _ = x.shape
            return x.reshape(b, s, HEADS, HEAD_DIM).transpose(0, 2, 1, 3)
        key = jax.random.key(seed)
        ks = jax.random.split(key, 13)
        scale = 1.0 / np.sqrt(EMBED)
        inp = {'query': jax.random.normal(ks[0], (B, S, EMBED), dtype=jnp.float32), 'key': jax.random.normal(ks[1], (B, S, EMBED), dtype=jnp.float32), 'value': jax.random.normal(ks[2], (B, S, EMBED), dtype=jnp.float32), 'mask': jax.random.randint(ks[3], (B, 1, S, S), 0, 2) > 0, 'Wq': jax.random.normal(ks[4], (EMBED, EMBED), dtype=jnp.float32) * scale, 'bq': jnp.zeros((EMBED,), dtype=jnp.float32), 'Wk': jax.random.normal(ks[5], (EMBED, EMBED), dtype=jnp.float32) * scale, 'bk': jnp.zeros((EMBED,), dtype=jnp.float32), 'Wv': jax.random.normal(ks[6], (EMBED, EMBED), dtype=jnp.float32) * scale, 'bv': jnp.zeros((EMBED,), dtype=jnp.float32), 'Wo': jax.random.normal(ks[7], (EMBED, EMBED), dtype=jnp.float32) * scale, 'bo': jnp.zeros((EMBED,), dtype=jnp.float32)}
        return inp
    _L1_xattn_all = _L1_xattn_setup()
    _L1_xattn_in = {k: v for k, v in _L1_xattn_all.items() if k in ('Wq', 'bq', 'Wk', 'bk', 'Wv', 'bv', 'Wo', 'bo')}
    del _L1_xattn_all

    def _L1_ffn_setup():
        import jax, jax.numpy as jnp
        import numpy as np
        EPS = 1e-05

        def rmsnorm(x):
            var = jnp.mean(jnp.square(x), axis=-1, keepdims=True)
            return x * jax.lax.rsqrt(var + 1e-06)

        def activation_quant(x):
            scale = 127.0 / jnp.clip(jnp.max(jnp.abs(x), axis=-1, keepdims=True), EPS, None)
            return jnp.clip(jnp.round(x * scale), -128, 127) / scale

        def weight_quant(w):
            scale = 1.0 / jnp.clip(jnp.mean(jnp.abs(w)), EPS, None)
            return jnp.clip(jnp.round(w * scale), -1, 1) / scale

        def bitlinear(x, w, b):
            xn = rmsnorm(x)
            xq = xn + jax.lax.stop_gradient(activation_quant(xn) - xn)
            wq = w + jax.lax.stop_gradient(weight_quant(w) - w)
            return jnp.einsum('bsi,oi->bso', xq, wq) + b
        key = jax.random.key(seed)
        k1, k2, k3 = jax.random.split(key, 3)
        B, S, D, H = (4, 256, 128, 512)
        x = jax.random.normal(k1, (B, S, D), dtype=jnp.float32)
        w1 = jax.random.normal(k2, (H, D), dtype=jnp.float32) * D ** (-0.5)
        b1 = jnp.zeros((H,), dtype=jnp.float32)
        w2 = jax.random.normal(k3, (D, H), dtype=jnp.float32) * H ** (-0.5)
        b2 = jnp.zeros((D,), dtype=jnp.float32)
        return {'x': x, 'w1': w1, 'b1': b1, 'w2': w2, 'b2': b2}
    _L1_ffn_all = _L1_ffn_setup()
    _L1_ffn_in = {k: v for k, v in _L1_ffn_all.items() if k in ('w1', 'b1', 'w2', 'b2')}
    del _L1_ffn_all

    def _L2_attn_setup():
        import jax, jax.numpy as jnp
        import numpy as np
        NUM_HEADS = 8
        BETA_MIN, BETA_MAX = (0.85, 0.999)
        ROPE_BASE = 10000.0

        def _rope_cache(L, d):
            half = d // 2
            inv_freq = 1.0 / ROPE_BASE ** (jnp.arange(half, dtype=jnp.float32) / half)
            freqs = jnp.arange(L, dtype=jnp.float32)[:, None] * inv_freq[None, :]
            return (jnp.cos(freqs), jnp.sin(freqs))

        def _apply_rope(x, cos, sin):
            B, H, L, D = x.shape
            xp = x.reshape(B, H, L, D // 2, 2)
            x1, x2 = (xp[..., 0], xp[..., 1])
            c = cos[None, None]
            s = sin[None, None]
            r1 = x1 * c - x2 * s
            r2 = x2 * c + x1 * s
            return jnp.stack([r1, r2], axis=-1).reshape(B, H, L, D)

        def _delta_scan(q, k, v, alpha, beta):
            B, H, L, Dh = q.shape
            qm = q.transpose(2, 0, 1, 3)
            km = k.transpose(2, 0, 1, 3)
            vm = v.transpose(2, 0, 1, 3)
            am = alpha.transpose(2, 0, 1)
            bm = beta.transpose(2, 0, 1)

            def step(state, inp):
                qt, kt, vt, at, bt = inp
                state = state * bt[..., None, None] + at[..., None, None] * (kt[..., :, None] * vt[..., None, :])
                ot = jnp.einsum('bhd,bhde->bhe', qt, state)
                return (state, ot)
            state0 = jnp.zeros((B, H, Dh, Dh), dtype=q.dtype)
            _, outs = jax.lax.scan(step, state0, (qm, km, vm, am, bm))
            return outs.transpose(1, 2, 0, 3)
        key = jax.random.key(seed)
        B, L, D, H = (2, 256, 128, NUM_HEADS)
        ks = jax.random.split(key, 8)
        scale = np.sqrt(6.0 / (D + D)).astype(np.float32)
        Wq = jax.random.uniform(ks[0], (D, D), jnp.float32, -scale, scale)
        Wk = jax.random.uniform(ks[1], (D, D), jnp.float32, -scale, scale)
        Wv = jax.random.uniform(ks[2], (D, D), jnp.float32, -scale, scale)
        Wo = jax.random.uniform(ks[3], (D, D), jnp.float32, -scale, scale)
        bo = jnp.zeros((D,), jnp.float32)
        Wbeta = jax.random.normal(ks[4], (H, D), jnp.float32) * 0.02
        bbeta = jnp.full((H,), float(np.log(0.97 / 0.03)), jnp.float32)
        Walpha = jax.random.normal(ks[5], (H, D), jnp.float32) * 0.02
        balpha = jnp.zeros((H,), jnp.float32)
        x = jax.random.normal(ks[6], (B, L, D), jnp.float32)
        return {'x': x, 'Wq': Wq, 'Wk': Wk, 'Wv': Wv, 'Wbeta': Wbeta, 'bbeta': bbeta, 'Walpha': Walpha, 'balpha': balpha, 'Wo': Wo, 'bo': bo}
    _L2_attn_all = _L2_attn_setup()
    _L2_attn_in = {k: v for k, v in _L2_attn_all.items() if k in ('Wq', 'Wk', 'Wv', 'Wbeta', 'bbeta', 'Walpha', 'balpha', 'Wo', 'bo')}
    del _L2_attn_all

    def _L2_xattn_setup():
        import jax, jax.numpy as jnp
        import numpy as np
        EMBED = 128
        HEADS = 16
        HEAD_DIM = EMBED // HEADS

        def _split_heads(x):
            b, n, c = x.shape
            return x.reshape(b, n, HEADS, c // HEADS).transpose(0, 2, 1, 3)
        key = jax.random.key(seed)
        ks = jax.random.split(key, 11)
        B, S, D = (2, 256, EMBED)
        scale = 1.0 / np.sqrt(D)
        inp = {'q': jax.random.normal(ks[0], (B, S, D), jnp.float32), 'k': jax.random.normal(ks[1], (B, S, D), jnp.float32), 'v': jax.random.normal(ks[2], (B, S, D), jnp.float32), 'Wq': jax.random.normal(ks[3], (D, D), jnp.float32) * scale, 'bq': jnp.zeros((D,), jnp.float32), 'Wk': jax.random.normal(ks[4], (D, D), jnp.float32) * scale, 'bk': jnp.zeros((D,), jnp.float32), 'Wv': jax.random.normal(ks[5], (D, D), jnp.float32) * scale, 'bv': jnp.zeros((D,), jnp.float32), 'Wo': jax.random.normal(ks[6], (D, D), jnp.float32) * scale, 'bo': jnp.zeros((D,), jnp.float32)}
        return inp
    _L2_xattn_all = _L2_xattn_setup()
    _L2_xattn_in = {k: v for k, v in _L2_xattn_all.items() if k in ('Wq', 'bq', 'Wk', 'bk', 'Wv', 'bv', 'Wo', 'bo')}
    del _L2_xattn_all

    def _L2_ffn_setup():
        import jax, jax.numpy as jnp
        import numpy as np
        D_MODEL = 128
        H_SHARED = 256
        H_ROUTED = 128
        N_EXPERTS = 8
        TOP_K = 2
        key = jax.random.key(seed)
        ks = jax.random.split(key, 8)
        B, T = (2, 256)
        sc_d = 1.0 / np.sqrt(D_MODEL)
        sc_hs = 1.0 / np.sqrt(H_SHARED)
        sc_hr = 1.0 / np.sqrt(H_ROUTED)
        return {'x': jax.random.normal(ks[0], (B, T, D_MODEL), dtype=jnp.float32), 'router_w': jax.random.normal(ks[1], (N_EXPERTS, D_MODEL), dtype=jnp.float32) * sc_d, 'router_bias': jnp.zeros((N_EXPERTS,), dtype=jnp.float32), 'sw1': jax.random.normal(ks[2], (D_MODEL, H_SHARED), dtype=jnp.float32) * sc_d, 'sw3': jax.random.normal(ks[3], (D_MODEL, H_SHARED), dtype=jnp.float32) * sc_d, 'sw2': jax.random.normal(ks[4], (H_SHARED, D_MODEL), dtype=jnp.float32) * sc_hs, 'ew1': jax.random.normal(ks[5], (N_EXPERTS, D_MODEL, H_ROUTED), dtype=jnp.float32) * sc_d, 'ew2': jax.random.normal(ks[6], (N_EXPERTS, H_ROUTED, D_MODEL), dtype=jnp.float32) * sc_hr}
    _L2_ffn_all = _L2_ffn_setup()
    _L2_ffn_in = {k: v for k, v in _L2_ffn_all.items() if k in ('router_w', 'router_bias', 'sw1', 'sw3', 'sw2', 'ew1', 'ew2')}
    del _L2_ffn_all

    def _L3_attn_setup():
        import jax, jax.numpy as jnp
        import numpy as np
        N_HIDDEN = 128
        N_HEADS = 16
        HEAD_DIM = N_HIDDEN // N_HEADS
        KERNEL = 4
        GN_EPS = 1e-05

        def _short_conv_1d(x, weight):
            F, K = weight.shape
            xp = jnp.pad(x, ((0, 0), (K - 1, 0), (0, 0)))
            shifts = jnp.stack([xp[:, i:i + x.shape[1], :] for i in range(K)], axis=-1)
            return jnp.sum(shifts * weight[None, None, :, :], axis=-1)
        key = jax.random.key(seed)
        ks = jax.random.split(key, 16)
        B, S = (4, 512)
        H, Hd = (N_HEADS, N_HIDDEN)
        sc = 0.02
        inp = {'x': jax.random.normal(ks[0], (B, S, Hd), dtype=jnp.float32), 'Wq': jax.random.normal(ks[1], (Hd, Hd), dtype=jnp.float32) * sc, 'bq': jnp.zeros((Hd,), jnp.float32), 'Wk': jax.random.normal(ks[2], (Hd, Hd), dtype=jnp.float32) * sc, 'bk': jnp.zeros((Hd,), jnp.float32), 'Wv': jax.random.normal(ks[3], (Hd, Hd), dtype=jnp.float32) * sc, 'bv': jnp.zeros((Hd,), jnp.float32), 'q_conv': jax.random.normal(ks[4], (Hd, KERNEL), dtype=jnp.float32) * sc, 'k_conv': jax.random.normal(ks[5], (Hd, KERNEL), dtype=jnp.float32) * sc, 'v_conv': jax.random.normal(ks[6], (Hd, KERNEL), dtype=jnp.float32) * sc, 'Wa': jax.random.normal(ks[7], (Hd, H), dtype=jnp.float32) * sc, 'ba': jnp.zeros((H,), jnp.float32), 'Wb': jax.random.normal(ks[8], (Hd, H), dtype=jnp.float32) * sc, 'bb': jnp.zeros((H,), jnp.float32), 'Wg': jax.random.normal(ks[9], (Hd, Hd), dtype=jnp.float32) * sc, 'bg': jnp.zeros((Hd,), jnp.float32), 'gn_scale': jnp.ones((Hd,), jnp.float32), 'gn_bias': jnp.zeros((Hd,), jnp.float32), 'Wo': jax.random.normal(ks[10], (Hd, Hd), dtype=jnp.float32) * sc, 'bo': jnp.zeros((Hd,), jnp.float32)}
        return inp
    _L3_attn_all = _L3_attn_setup()
    _L3_attn_in = {k: v for k, v in _L3_attn_all.items() if k in ('Wq', 'bq', 'Wk', 'bk', 'Wv', 'bv', 'q_conv', 'k_conv', 'v_conv', 'Wa', 'ba', 'Wb', 'bb', 'Wg', 'bg', 'gn_scale', 'gn_bias', 'Wo', 'bo')}
    del _L3_attn_all

    def _L3_xattn_setup():
        import jax, jax.numpy as jnp
        import numpy as np
        B, S, D = (4, 512, 128)
        NUM_Q_HEADS = 16
        D_K = D // NUM_Q_HEADS
        INIT_SCALE = 0.02
        key = jax.random.key(seed)
        ks = jax.random.split(key, 11)
        s = INIT_SCALE
        return {'Q': jax.random.normal(ks[0], (B, S, D), dtype=jnp.float32), 'K': jax.random.normal(ks[1], (B, S, D), dtype=jnp.float32), 'V': jax.random.normal(ks[2], (B, S, D), dtype=jnp.float32), 'Wq': jax.random.normal(ks[3], (D, D), dtype=jnp.float32) * s, 'bq': jnp.zeros((D,), jnp.float32), 'Wk': jax.random.normal(ks[4], (D, D), dtype=jnp.float32) * s, 'bk': jnp.zeros((D,), jnp.float32), 'Wv': jax.random.normal(ks[5], (D, D), dtype=jnp.float32) * s, 'bv': jnp.zeros((D,), jnp.float32), 'Wo': jax.random.normal(ks[6], (D, D), dtype=jnp.float32) * s, 'bo': jnp.zeros((D,), jnp.float32), 'mask': jnp.tril(jnp.ones((S, S), dtype=jnp.int32))}
    _L3_xattn_all = _L3_xattn_setup()
    _L3_xattn_in = {k: v for k, v in _L3_xattn_all.items() if k in ('Wq', 'bq', 'Wk', 'bk', 'Wv', 'bv', 'Wo', 'bo')}
    del _L3_xattn_all

    def _L3_ffn_setup():
        import jax, jax.numpy as jnp
        import numpy as np
        B, S, D, F, E = (2, 256, 128, 512, 8)
        LN_EPS = 1e-05

        def _xavier(key, shape, fan_in, fan_out):
            a = np.sqrt(6.0 / (fan_in + fan_out))
            return jax.random.uniform(key, shape, jnp.float32, -a, a)
        key = jax.random.key(seed)
        ks = jax.random.split(key, 8)
        tgt = jax.random.normal(ks[0], (B, S, D), jnp.float32)
        router_w = _xavier(ks[1], (E, D), D, E)
        router_b = jnp.zeros((E,), jnp.float32)
        w1 = _xavier(ks[2], (E, D, F), D, F)
        b1 = jnp.zeros((E, F), jnp.float32)
        w2 = _xavier(ks[3], (E, F, D), F, D)
        b2 = jnp.zeros((E, D), jnp.float32)
        gamma = jnp.ones((D,), jnp.float32)
        beta = jnp.zeros((D,), jnp.float32)
        return {'tgt': tgt, 'router_w': router_w, 'router_b': router_b, 'w1': w1, 'b1': b1, 'w2': w2, 'b2': b2, 'gamma': gamma, 'beta': beta}
    _L3_ffn_all = _L3_ffn_setup()
    _L3_ffn_in = {k: v for k, v in _L3_ffn_all.items() if k in ('router_w', 'router_b', 'w1', 'b1', 'w2', 'b2', 'gamma', 'beta')}
    del _L3_ffn_all
    return {'x': x, 'ctx_1024': ctx_1024, 'mask_Bx1xSxS2_bk1': mask_Bx1xSxS2_bk1, 'mask_SxS2_ik0': mask_SxS2_ik0, 'L0_attn_Wq': _L0_attn_in['Wq'], 'L0_attn_Wk': _L0_attn_in['Wk'], 'L0_attn_Wv': _L0_attn_in['Wv'], 'L0_attn_Wp': _L0_attn_in['Wp'], 'L0_attn_pos_emb_k': _L0_attn_in['pos_emb_k'], 'L0_xattn_Wq': _L0_xattn_in['Wq'], 'L0_xattn_Wk': _L0_xattn_in['Wk'], 'L0_xattn_Wv': _L0_xattn_in['Wv'], 'L0_ffn_w_gate': _L0_ffn_in['w_gate'], 'L0_ffn_w_up': _L0_ffn_in['w_up'], 'L0_ffn_w_down': _L0_ffn_in['w_down'], 'L1_attn_Wq': _L1_attn_in['Wq'], 'L1_attn_bq': _L1_attn_in['bq'], 'L1_attn_Wk': _L1_attn_in['Wk'], 'L1_attn_bk': _L1_attn_in['bk'], 'L1_attn_Wv': _L1_attn_in['Wv'], 'L1_attn_bv': _L1_attn_in['bv'], 'L1_attn_Wo': _L1_attn_in['Wo'], 'L1_attn_bo': _L1_attn_in['bo'], 'L1_attn_gamma': _L1_attn_in['gamma'], 'L1_attn_beta': _L1_attn_in['beta'], 'L1_xattn_Wq': _L1_xattn_in['Wq'], 'L1_xattn_bq': _L1_xattn_in['bq'], 'L1_xattn_Wk': _L1_xattn_in['Wk'], 'L1_xattn_bk': _L1_xattn_in['bk'], 'L1_xattn_Wv': _L1_xattn_in['Wv'], 'L1_xattn_bv': _L1_xattn_in['bv'], 'L1_xattn_Wo': _L1_xattn_in['Wo'], 'L1_xattn_bo': _L1_xattn_in['bo'], 'L1_ffn_w1': _L1_ffn_in['w1'], 'L1_ffn_b1': _L1_ffn_in['b1'], 'L1_ffn_w2': _L1_ffn_in['w2'], 'L1_ffn_b2': _L1_ffn_in['b2'], 'L2_attn_Wq': _L2_attn_in['Wq'], 'L2_attn_Wk': _L2_attn_in['Wk'], 'L2_attn_Wv': _L2_attn_in['Wv'], 'L2_attn_Wbeta': _L2_attn_in['Wbeta'], 'L2_attn_bbeta': _L2_attn_in['bbeta'], 'L2_attn_Walpha': _L2_attn_in['Walpha'], 'L2_attn_balpha': _L2_attn_in['balpha'], 'L2_attn_Wo': _L2_attn_in['Wo'], 'L2_attn_bo': _L2_attn_in['bo'], 'L2_xattn_Wq': _L2_xattn_in['Wq'], 'L2_xattn_bq': _L2_xattn_in['bq'], 'L2_xattn_Wk': _L2_xattn_in['Wk'], 'L2_xattn_bk': _L2_xattn_in['bk'], 'L2_xattn_Wv': _L2_xattn_in['Wv'], 'L2_xattn_bv': _L2_xattn_in['bv'], 'L2_xattn_Wo': _L2_xattn_in['Wo'], 'L2_xattn_bo': _L2_xattn_in['bo'], 'L2_ffn_router_w': _L2_ffn_in['router_w'], 'L2_ffn_router_bias': _L2_ffn_in['router_bias'], 'L2_ffn_sw1': _L2_ffn_in['sw1'], 'L2_ffn_sw3': _L2_ffn_in['sw3'], 'L2_ffn_sw2': _L2_ffn_in['sw2'], 'L2_ffn_ew1': _L2_ffn_in['ew1'], 'L2_ffn_ew2': _L2_ffn_in['ew2'], 'L3_attn_Wq': _L3_attn_in['Wq'], 'L3_attn_bq': _L3_attn_in['bq'], 'L3_attn_Wk': _L3_attn_in['Wk'], 'L3_attn_bk': _L3_attn_in['bk'], 'L3_attn_Wv': _L3_attn_in['Wv'], 'L3_attn_bv': _L3_attn_in['bv'], 'L3_attn_q_conv': _L3_attn_in['q_conv'], 'L3_attn_k_conv': _L3_attn_in['k_conv'], 'L3_attn_v_conv': _L3_attn_in['v_conv'], 'L3_attn_Wa': _L3_attn_in['Wa'], 'L3_attn_ba': _L3_attn_in['ba'], 'L3_attn_Wb': _L3_attn_in['Wb'], 'L3_attn_bb': _L3_attn_in['bb'], 'L3_attn_Wg': _L3_attn_in['Wg'], 'L3_attn_bg': _L3_attn_in['bg'], 'L3_attn_gn_scale': _L3_attn_in['gn_scale'], 'L3_attn_gn_bias': _L3_attn_in['gn_bias'], 'L3_attn_Wo': _L3_attn_in['Wo'], 'L3_attn_bo': _L3_attn_in['bo'], 'L3_xattn_Wq': _L3_xattn_in['Wq'], 'L3_xattn_bq': _L3_xattn_in['bq'], 'L3_xattn_Wk': _L3_xattn_in['Wk'], 'L3_xattn_bk': _L3_xattn_in['bk'], 'L3_xattn_Wv': _L3_xattn_in['Wv'], 'L3_xattn_bv': _L3_xattn_in['bv'], 'L3_xattn_Wo': _L3_xattn_in['Wo'], 'L3_xattn_bo': _L3_xattn_in['bo'], 'L3_ffn_router_w': _L3_ffn_in['router_w'], 'L3_ffn_router_b': _L3_ffn_in['router_b'], 'L3_ffn_w1': _L3_ffn_in['w1'], 'L3_ffn_b1': _L3_ffn_in['b1'], 'L3_ffn_w2': _L3_ffn_in['w2'], 'L3_ffn_b2': _L3_ffn_in['b2'], 'L3_ffn_gamma': _L3_ffn_in['gamma'], 'L3_ffn_beta': _L3_ffn_in['beta']}

def reference(x, ctx_1024, mask_Bx1xSxS2_bk1, mask_SxS2_ik0, L0_attn_Wq, L0_attn_Wk, L0_attn_Wv, L0_attn_Wp, L0_attn_pos_emb_k, L0_xattn_Wq, L0_xattn_Wk, L0_xattn_Wv, L0_ffn_w_gate, L0_ffn_w_up, L0_ffn_w_down, L1_attn_Wq, L1_attn_bq, L1_attn_Wk, L1_attn_bk, L1_attn_Wv, L1_attn_bv, L1_attn_Wo, L1_attn_bo, L1_attn_gamma, L1_attn_beta, L1_xattn_Wq, L1_xattn_bq, L1_xattn_Wk, L1_xattn_bk, L1_xattn_Wv, L1_xattn_bv, L1_xattn_Wo, L1_xattn_bo, L1_ffn_w1, L1_ffn_b1, L1_ffn_w2, L1_ffn_b2, L2_attn_Wq, L2_attn_Wk, L2_attn_Wv, L2_attn_Wbeta, L2_attn_bbeta, L2_attn_Walpha, L2_attn_balpha, L2_attn_Wo, L2_attn_bo, L2_xattn_Wq, L2_xattn_bq, L2_xattn_Wk, L2_xattn_bk, L2_xattn_Wv, L2_xattn_bv, L2_xattn_Wo, L2_xattn_bo, L2_ffn_router_w, L2_ffn_router_bias, L2_ffn_sw1, L2_ffn_sw3, L2_ffn_sw2, L2_ffn_ew1, L2_ffn_ew2, L3_attn_Wq, L3_attn_bq, L3_attn_Wk, L3_attn_bk, L3_attn_Wv, L3_attn_bv, L3_attn_q_conv, L3_attn_k_conv, L3_attn_v_conv, L3_attn_Wa, L3_attn_ba, L3_attn_Wb, L3_attn_bb, L3_attn_Wg, L3_attn_bg, L3_attn_gn_scale, L3_attn_gn_bias, L3_attn_Wo, L3_attn_bo, L3_xattn_Wq, L3_xattn_bq, L3_xattn_Wk, L3_xattn_bk, L3_xattn_Wv, L3_xattn_bv, L3_xattn_Wo, L3_xattn_bo, L3_ffn_router_w, L3_ffn_router_b, L3_ffn_w1, L3_ffn_b1, L3_ffn_w2, L3_ffn_b2, L3_ffn_gamma, L3_ffn_beta):
    import jax
    import jax.numpy as jnp

    def _L0_attn_ref(x, Wq, Wk, Wv, Wp, pos_emb_k):
        import jax, jax.numpy as jnp
        import numpy as np
        import math
        B, S, D = (4, 256, 128)
        H = 16
        HD = D // H
        R = 128
        P = 2 * R
        batch, ctx, emb = x.shape

        def heads(w):
            return (x @ w.T).reshape(batch, ctx, H, HD).transpose(0, 2, 1, 3)
        q, k, v = (heads(Wq), heads(Wk), heads(Wv))
        att_rel_pos = jnp.einsum('bhsd,pd->bhsp', q, pos_emb_k)
        i = jnp.arange(ctx)
        att_idxs = jnp.clip(i[None, :] - i[:, None], -R, R - 1) % P
        att_pos = jnp.take_along_axis(att_rel_pos, att_idxs[None, None, :, :].astype(jnp.int32), axis=3)
        attn_val = jnp.einsum('bhsd,bhtd->bhst', q, k) + att_pos
        attn_scale = 1.0 / math.sqrt(HD)
        att = jax.nn.softmax((attn_val + att_pos) * attn_scale, axis=-1)
        y = jnp.einsum('bhst,bhtd->bhsd', att, v)
        y = y.transpose(0, 2, 1, 3).reshape(batch, ctx, emb)
        return y @ Wp.T

    def _L0_xattn_ref(q, k, v, Wq, Wk, Wv):
        import jax, jax.numpy as jnp
        import numpy as np
        BETA = 128
        NUM_HEADS = 16
        NORM = (BETA // NUM_HEADS) ** (-0.5)
        qp = jax.nn.relu(jnp.einsum('bnd,od->bno', q, Wq))
        kp = jax.nn.relu(jnp.einsum('bnd,od->bno', k, Wk))
        vp = jax.nn.relu(jnp.einsum('bnd,od->bno', v, Wv))
        B, N, D = qp.shape
        dh = D // NUM_HEADS
        qh = qp.reshape(B, N, NUM_HEADS, dh)
        kh = kp.reshape(B, N, NUM_HEADS, dh)
        vh = vp.reshape(B, N, NUM_HEADS, vp.shape[-1] // NUM_HEADS)
        E = NORM * jnp.einsum('bqhd,bkhd->bhqk', qh, kh)
        A = jax.nn.softmax(E, axis=-1)
        out = jnp.einsum('bhqk,bkhd->bqhd', A, vh)
        return out.reshape(B, N, -1)

    def _L0_ffn_ref(x, w_gate, w_up, w_down):
        import jax, jax.numpy as jnp
        import numpy as np
        HIDDEN = 128
        INNER = 512

        def _weight_quant(w):
            scale = 1.0 / jnp.clip(jnp.mean(jnp.abs(w)), 1e-05)
            wq = jnp.clip(jnp.round(w * scale), -1.0, 1.0) / scale
            return w + jax.lax.stop_gradient(wq - w)

        def _act_quant(x):
            scale = 127.0 / jnp.clip(jnp.max(jnp.abs(x), axis=-1, keepdims=True), 1e-05)
            xq = jnp.clip(jnp.round(x * scale), -128.0, 127.0) / scale
            return x + jax.lax.stop_gradient(xq - x)

        def _bitlinear(x, w):
            return jnp.einsum('bsi,oi->bso', _act_quant(x), _weight_quant(w))
        gate = jax.nn.silu(_bitlinear(x, w_gate))
        up = _bitlinear(x, w_up)
        return _bitlinear(gate * up, w_down)

    def _L1_attn_ref(x, Wq, bq, Wk, bk, Wv, bv, Wo, bo, gamma, beta):
        import jax, jax.numpy as jnp
        import numpy as np
        B, S, D = (4, 256, 128)
        H, K = (16, 64)
        EPS = 0.001
        q = jnp.einsum('bsd,dhk->bshk', x, Wq) + bq
        k = jnp.einsum('bsd,dhk->bshk', x, Wk) + bk
        v = jnp.einsum('bsd,dhk->bshk', x, Wv) + bv
        scale = 1.0 / jnp.sqrt(jnp.asarray(K, x.dtype))
        scores = jnp.einsum('bqhk,bshk->bhqs', q, k) * scale
        attn = jax.nn.softmax(scores, axis=-1)
        ctx = jnp.einsum('bhqs,bshk->bqhk', attn, v)
        attn_out = jnp.einsum('bqhk,hkd->bqd', ctx, Wo) + bo
        y = x + attn_out
        mu = jnp.mean(y, axis=-1, keepdims=True)
        var = jnp.mean(jnp.square(y - mu), axis=-1, keepdims=True)
        return (y - mu) * jax.lax.rsqrt(var + EPS) * gamma + beta

    def _L1_xattn_ref(query, key, value, mask, Wq, bq, Wk, bk, Wv, bv, Wo, bo):
        import jax, jax.numpy as jnp
        import numpy as np
        EMBED = 128
        HEADS = 16
        HEAD_DIM = EMBED // HEADS
        B, S = (4, 256)

        def _split_heads(x):
            b, s, _ = x.shape
            return x.reshape(b, s, HEADS, HEAD_DIM).transpose(0, 2, 1, 3)
        q = _split_heads(query @ Wq.T + bq)
        k = _split_heads(key @ Wk.T + bk)
        v = _split_heads(value @ Wv.T + bv)
        scores = jnp.einsum('bhqd,bhkd->bhqk', q, k) / jnp.sqrt(jnp.float32(HEAD_DIM))
        scores = jnp.where(mask, jnp.float32(-1000000000.0), scores)
        attn = jax.nn.softmax(scores, axis=-1)
        out = jnp.einsum('bhqk,bhkd->bhqd', attn, v)
        out = out.transpose(0, 2, 1, 3).reshape(out.shape[0], -1, EMBED)
        return out @ Wo.T + bo

    def _L1_ffn_ref(x, w1, b1, w2, b2):
        import jax, jax.numpy as jnp
        import numpy as np
        EPS = 1e-05

        def rmsnorm(x):
            var = jnp.mean(jnp.square(x), axis=-1, keepdims=True)
            return x * jax.lax.rsqrt(var + 1e-06)

        def activation_quant(x):
            scale = 127.0 / jnp.clip(jnp.max(jnp.abs(x), axis=-1, keepdims=True), EPS, None)
            return jnp.clip(jnp.round(x * scale), -128, 127) / scale

        def weight_quant(w):
            scale = 1.0 / jnp.clip(jnp.mean(jnp.abs(w)), EPS, None)
            return jnp.clip(jnp.round(w * scale), -1, 1) / scale

        def bitlinear(x, w, b):
            xn = rmsnorm(x)
            xq = xn + jax.lax.stop_gradient(activation_quant(xn) - xn)
            wq = w + jax.lax.stop_gradient(weight_quant(w) - w)
            return jnp.einsum('bsi,oi->bso', xq, wq) + b
        h = bitlinear(x, w1, b1)
        h = jax.nn.gelu(h, approximate=False)
        return bitlinear(h, w2, b2)

    def _L2_attn_ref(x, Wq, Wk, Wv, Wbeta, bbeta, Walpha, balpha, Wo, bo):
        import jax, jax.numpy as jnp
        import numpy as np
        NUM_HEADS = 8
        BETA_MIN, BETA_MAX = (0.85, 0.999)
        ROPE_BASE = 10000.0

        def _rope_cache(L, d):
            half = d // 2
            inv_freq = 1.0 / ROPE_BASE ** (jnp.arange(half, dtype=jnp.float32) / half)
            freqs = jnp.arange(L, dtype=jnp.float32)[:, None] * inv_freq[None, :]
            return (jnp.cos(freqs), jnp.sin(freqs))

        def _apply_rope(x, cos, sin):
            B, H, L, D = x.shape
            xp = x.reshape(B, H, L, D // 2, 2)
            x1, x2 = (xp[..., 0], xp[..., 1])
            c = cos[None, None]
            s = sin[None, None]
            r1 = x1 * c - x2 * s
            r2 = x2 * c + x1 * s
            return jnp.stack([r1, r2], axis=-1).reshape(B, H, L, D)

        def _delta_scan(q, k, v, alpha, beta):
            B, H, L, Dh = q.shape
            qm = q.transpose(2, 0, 1, 3)
            km = k.transpose(2, 0, 1, 3)
            vm = v.transpose(2, 0, 1, 3)
            am = alpha.transpose(2, 0, 1)
            bm = beta.transpose(2, 0, 1)

            def step(state, inp):
                qt, kt, vt, at, bt = inp
                state = state * bt[..., None, None] + at[..., None, None] * (kt[..., :, None] * vt[..., None, :])
                ot = jnp.einsum('bhd,bhde->bhe', qt, state)
                return (state, ot)
            state0 = jnp.zeros((B, H, Dh, Dh), dtype=q.dtype)
            _, outs = jax.lax.scan(step, state0, (qm, km, vm, am, bm))
            return outs.transpose(1, 2, 0, 3)
        B, L, D = x.shape
        H = NUM_HEADS
        Dh = D // H
        split = lambda y: y.reshape(B, L, H, Dh).transpose(0, 2, 1, 3)
        q = split(x @ Wq.T)
        k = split(x @ Wk.T)
        v = split(x @ Wv.T)
        cos, sin = _rope_cache(L, Dh)
        q = _apply_rope(q, cos, sin)
        k = _apply_rope(k, cos, sin)
        beta = BETA_MIN + (BETA_MAX - BETA_MIN) * jax.nn.sigmoid(x @ Wbeta.T + bbeta)
        alpha = jax.nn.sigmoid(x @ Walpha.T + balpha)
        beta = beta.transpose(0, 2, 1)
        alpha = alpha.transpose(0, 2, 1)
        out = _delta_scan(q, k, v, alpha, beta)
        out = out.transpose(0, 2, 1, 3).reshape(B, L, D)
        return out @ Wo.T + bo

    def _L2_xattn_ref(q, k, v, Wq, bq, Wk, bk, Wv, bv, Wo, bo):
        import jax, jax.numpy as jnp
        import numpy as np
        EMBED = 128
        HEADS = 16
        HEAD_DIM = EMBED // HEADS

        def _split_heads(x):
            b, n, c = x.shape
            return x.reshape(b, n, HEADS, c // HEADS).transpose(0, 2, 1, 3)
        qh = _split_heads(q @ Wq + bq)
        kh = _split_heads(k @ Wk + bk)
        vh = _split_heads(v @ Wv + bv)
        scale = 1.0 / jnp.sqrt(jnp.asarray(HEAD_DIM, qh.dtype))
        att = jnp.einsum('bhqd,bhkd->bhqk', qh, kh) * scale
        att = jax.nn.softmax(att, axis=-1)
        out = jnp.einsum('bhqk,bhkd->bhqd', att, vh)
        b, h, n, dh = out.shape
        out = out.transpose(0, 2, 1, 3).reshape(b, n, h * dh)
        return out @ Wo + bo

    def _L2_ffn_ref(x, router_w, router_bias, sw1, sw3, sw2, ew1, ew2):
        import jax, jax.numpy as jnp
        import numpy as np
        D_MODEL = 128
        H_SHARED = 256
        H_ROUTED = 128
        N_EXPERTS = 8
        TOP_K = 2
        B, T, C = x.shape
        xf = x.reshape(-1, C)
        shared_out = jax.nn.silu(xf @ sw1) * (xf @ sw3) @ sw2
        s = jax.nn.sigmoid((xf @ router_w.T).astype(jnp.float32))
        sel_scores = s + router_bias.astype(jnp.float32)
        _, topk_idx = jax.lax.top_k(sel_scores, TOP_K)
        s_sel = jnp.take_along_axis(s, topk_idx, axis=1)
        denom = s_sel.sum(axis=1, keepdims=True)
        gates = jnp.where(denom > 1e-09, s_sel / (denom + 1e-09), 1.0 / TOP_K).astype(x.dtype)
        one_hot = jax.nn.one_hot(topk_idx, N_EXPERTS, dtype=x.dtype)
        comb = jnp.einsum('nke,nk->ne', one_hot, gates)
        h = jax.nn.gelu(jnp.einsum('nd,edh->neh', xf, ew1), approximate=False)
        y = jnp.einsum('neh,ehd->ned', h, ew2)
        routed_out = jnp.einsum('ned,ne->nd', y, comb)
        return (shared_out + routed_out).reshape(B, T, C)

    def _L3_attn_ref(x, Wq, bq, Wk, bk, Wv, bv, q_conv, k_conv, v_conv, Wa, ba, Wb, bb, Wg, bg, gn_scale, gn_bias, Wo, bo):
        import jax, jax.numpy as jnp
        import numpy as np
        N_HIDDEN = 128
        N_HEADS = 16
        HEAD_DIM = N_HIDDEN // N_HEADS
        KERNEL = 4
        GN_EPS = 1e-05

        def _short_conv_1d(x, weight):
            F, K = weight.shape
            xp = jnp.pad(x, ((0, 0), (K - 1, 0), (0, 0)))
            shifts = jnp.stack([xp[:, i:i + x.shape[1], :] for i in range(K)], axis=-1)
            return jnp.sum(shifts * weight[None, None, :, :], axis=-1)
        B, S, _ = x.shape
        h, d = (N_HEADS, HEAD_DIM)
        q = jax.nn.silu(_short_conv_1d(x @ Wq + bq, q_conv)).reshape(B, S, h, d)
        q = q / (jnp.linalg.norm(q, axis=-1, keepdims=True) + 1e-06)
        k = jax.nn.silu(_short_conv_1d(x @ Wk + bk, k_conv)).reshape(B, S, h, d)
        k = k / (jnp.linalg.norm(k, axis=-1, keepdims=True) + 1e-06)
        v = jax.nn.silu(_short_conv_1d(x @ Wv + bv, v_conv)).reshape(B, S, h, d)
        alpha = jax.nn.sigmoid(x @ Wa + ba)
        beta = jax.nn.sigmoid(x @ Wb + bb)
        out_gate = jax.nn.silu(x @ Wg + bg)
        qT = jnp.transpose(q, (1, 0, 2, 3))
        kT = jnp.transpose(k, (1, 0, 2, 3))
        vT = jnp.transpose(v, (1, 0, 2, 3))
        aT = jnp.transpose(alpha, (1, 0, 2))
        bT = jnp.transpose(beta, (1, 0, 2))

        def _step(Sst, inputs):
            q_t, k_t, v_t, a_t, b_t = inputs
            a = a_t[:, :, None, None]
            b = b_t[:, :, None, None]
            Sk = jnp.einsum('bhde,bhe->bhd', Sst, k_t)
            delta_gated = v_t - a_t[:, :, None] * Sk
            update = b * jnp.einsum('bhd,bhe->bhde', delta_gated, k_t)
            Sst = a * Sst + update
            o_t = jnp.einsum('bhde,bhe->bhd', Sst, q_t)
            return (Sst, o_t)
        S0 = jnp.zeros((B, h, d, d), dtype=x.dtype)
        _, outs = jax.lax.scan(_step, S0, (qT, kT, vT, aT, bT))
        outs = jnp.transpose(outs, (1, 0, 2, 3)).reshape(B, S, N_HIDDEN)
        g = outs.reshape(B, S, h, d)
        mu = jnp.mean(g, axis=(1, 3), keepdims=True)
        var = jnp.mean(jnp.square(g), axis=(1, 3), keepdims=True) - jnp.square(mu)
        g = (g - mu) * jax.lax.rsqrt(var + GN_EPS)
        y = g.reshape(B, S, N_HIDDEN) * gn_scale + gn_bias
        return out_gate * y @ Wo + bo

    def _L3_xattn_ref(Q, K, V, Wq, bq, Wk, bk, Wv, bv, Wo, bo, mask):
        import jax, jax.numpy as jnp
        import numpy as np
        B, S, D = (4, 512, 128)
        NUM_Q_HEADS = 16
        D_K = D // NUM_Q_HEADS
        INIT_SCALE = 0.02
        q = Q @ Wq + bq
        k = K @ Wk + bk
        v = V @ Wv + bv
        scale = 1.0 / np.sqrt(D_K).astype(np.float32)
        scores = jnp.einsum('bqd,bkd->bqk', q, k) * scale
        scores = jnp.where(mask == 0, jnp.asarray(-1000000000.0, scores.dtype), scores)
        probs = jax.nn.softmax(scores, axis=-1)
        attn = jnp.einsum('bqk,bkd->bqd', probs, v)
        return attn @ Wo + bo

    def _L3_ffn_ref(tgt, router_w, router_b, w1, b1, w2, b2, gamma, beta):
        import jax, jax.numpy as jnp
        import numpy as np
        B, S, D, F, E = (2, 256, 128, 512, 8)
        LN_EPS = 1e-05

        def _xavier(key, shape, fan_in, fan_out):
            a = np.sqrt(6.0 / (fan_in + fan_out))
            return jax.random.uniform(key, shape, jnp.float32, -a, a)
        logits = jnp.einsum('bsd,ed->bse', tgt, router_w) + router_b
        rw = jax.nn.softmax(logits, axis=-1)
        rw = jnp.zeros_like(rw).at[..., 0].set(1.0)
        h = jax.nn.relu(jnp.einsum('bsd,edf->besf', tgt, w1) + b1[None, :, None, :])
        eo = jnp.einsum('besf,efd->besd', h, w2) + b2[None, :, None, :]
        tgt2 = jnp.einsum('besd,bse->bsd', eo, rw)
        x = tgt + tgt2
        mean = jnp.mean(x, axis=-1, keepdims=True)
        var = jnp.mean(jnp.square(x - mean), axis=-1, keepdims=True)
        return (x - mean) * jax.lax.rsqrt(var + LN_EPS) * gamma + beta
    x = x + _L0_attn_ref(_layernorm(x, axis=-1), L0_attn_Wq, L0_attn_Wk, L0_attn_Wv, L0_attn_Wp, L0_attn_pos_emb_k)
    x = x + _L0_xattn_ref(_layernorm(x, axis=-1), ctx_1024, ctx_1024, L0_xattn_Wq, L0_xattn_Wk, L0_xattn_Wv)
    x = x + _L0_ffn_ref(_layernorm(x, axis=-1), L0_ffn_w_gate, L0_ffn_w_up, L0_ffn_w_down)
    x = x + _L1_attn_ref(_layernorm(x, axis=-1), L1_attn_Wq, L1_attn_bq, L1_attn_Wk, L1_attn_bk, L1_attn_Wv, L1_attn_bv, L1_attn_Wo, L1_attn_bo, L1_attn_gamma, L1_attn_beta)
    x = x + _L1_xattn_ref(_layernorm(x, axis=-1), ctx_1024, ctx_1024, mask_Bx1xSxS2_bk1, L1_xattn_Wq, L1_xattn_bq, L1_xattn_Wk, L1_xattn_bk, L1_xattn_Wv, L1_xattn_bv, L1_xattn_Wo, L1_xattn_bo)
    x = x + _L1_ffn_ref(_layernorm(x, axis=-1), L1_ffn_w1, L1_ffn_b1, L1_ffn_w2, L1_ffn_b2)
    x = x + _L2_attn_ref(_layernorm(x, axis=-1), L2_attn_Wq, L2_attn_Wk, L2_attn_Wv, L2_attn_Wbeta, L2_attn_bbeta, L2_attn_Walpha, L2_attn_balpha, L2_attn_Wo, L2_attn_bo)
    x = x + _L2_xattn_ref(_layernorm(x, axis=-1), ctx_1024, ctx_1024, L2_xattn_Wq, L2_xattn_bq, L2_xattn_Wk, L2_xattn_bk, L2_xattn_Wv, L2_xattn_bv, L2_xattn_Wo, L2_xattn_bo)
    x = x + _L2_ffn_ref(_layernorm(x, axis=-1), L2_ffn_router_w, L2_ffn_router_bias, L2_ffn_sw1, L2_ffn_sw3, L2_ffn_sw2, L2_ffn_ew1, L2_ffn_ew2)
    x = x + _L3_attn_ref(_layernorm(x, axis=-1), L3_attn_Wq, L3_attn_bq, L3_attn_Wk, L3_attn_bk, L3_attn_Wv, L3_attn_bv, L3_attn_q_conv, L3_attn_k_conv, L3_attn_v_conv, L3_attn_Wa, L3_attn_ba, L3_attn_Wb, L3_attn_bb, L3_attn_Wg, L3_attn_bg, L3_attn_gn_scale, L3_attn_gn_bias, L3_attn_Wo, L3_attn_bo)
    x = x + _L3_xattn_ref(_layernorm(x, axis=-1), ctx_1024, ctx_1024, L3_xattn_Wq, L3_xattn_bq, L3_xattn_Wk, L3_xattn_bk, L3_xattn_Wv, L3_xattn_bv, L3_xattn_Wo, L3_xattn_bo, mask_SxS2_ik0)
    x = x + _L3_ffn_ref(_layernorm(x, axis=-1), L3_ffn_router_w, L3_ffn_router_b, L3_ffn_w1, L3_ffn_b1, L3_ffn_w2, L3_ffn_b2, L3_ffn_gamma, L3_ffn_beta)
    return x

_drawn_inputs = setup_inputs


def setup_inputs(seed=0):
    import zlib

    import numpy as np

    out = dict(_drawn_inputs(seed))
    spreads = {'L1_attn_bq': (0.0, 0.8),
     'L1_attn_bk': (0.0, 2.0),
     'L1_attn_bv': (0.0, 0.1),
     'L1_attn_bo': (0.0, 0.1),
     'L1_attn_gamma': (1.0, 0.2),
     'L1_attn_beta': (0.0, 0.1),
     'L1_xattn_bq': (0.0, 0.28),
     'L1_xattn_bk': (0.0, 2.0),
     'L1_xattn_bv': (0.0, 0.1),
     'L1_xattn_bo': (0.0, 0.1),
     'L1_ffn_b1': (0.0, 0.1),
     'L1_ffn_b2': (0.0, 0.1),
     'L2_attn_bbeta': (3.4760987758636475, 0.2),
     'L2_attn_balpha': (0.0, 0.1),
     'L2_attn_bo': (0.0, 0.8),
     'L2_xattn_bq': (0.0, 2.0),
     'L2_xattn_bk': (0.0, 2.0),
     'L2_xattn_bv': (0.0, 0.8),
     'L2_xattn_bo': (0.0, 0.8),
     'L2_ffn_router_bias': (0.0, 0.635),
     'L3_attn_bq': (0.0, 0.8),
     'L3_attn_bk': (0.0, 0.8),
     'L3_attn_bv': (0.0, 0.8),
     'L3_attn_ba': (0.0, 0.8),
     'L3_attn_bb': (0.0, 2.0),
     'L3_attn_bg': (0.0, 0.8),
     'L3_attn_gn_scale': (1.0, 0.6),
     'L3_attn_gn_bias': (0.0, 0.8),
     'L3_attn_bo': (0.0, 0.8),
     'L3_xattn_bq': (0.0, 0.1),
     'L3_xattn_bk': (0.0, 0.1),
     'L3_xattn_bv': (0.0, 0.8),
     'L3_xattn_bo': (0.0, 0.8),
     'L3_ffn_router_b': (0.0, 0.1),
     'L3_ffn_b1': (0.0, 2.0),
     'L3_ffn_b2': (0.0, 2.0),
     'L3_ffn_gamma': (1.0, 0.6),
     'L3_ffn_beta': (0.0, 0.8)}
    factors = {'L0_attn_Wq': 8.0,
     'L0_attn_Wk': 8.0,
     'L0_attn_Wv': 4.364,
     'L0_attn_Wp': 4.392,
     'L0_attn_pos_emb_k': 8.0,
     'L1_attn_Wq': 8.0,
     'L1_attn_Wk': 8.0,
     'L2_attn_Wbeta': 3.661,
     'L2_xattn_Wq': 4.216,
     'L2_xattn_Wk': 3.678,
     'L2_ffn_router_w': 2.944,
     'L2_ffn_ew1': 2.772,
     'L3_attn_Wq': 8.0,
     'L3_attn_Wk': 8.0,
     'L3_attn_Wv': 8.0,
     'L3_attn_q_conv': 8.0,
     'L3_attn_k_conv': 8.0,
     'L3_attn_v_conv': 8.0,
     'L3_attn_Wa': 8.0,
     'L3_attn_Wb': 8.0,
     'L3_attn_Wg': 8.0,
     'L3_attn_Wo': 8.0,
     'L3_xattn_Wv': 8.0,
     'L3_xattn_Wo': 8.0,
     'L3_ffn_w1': 2.831}
    for name, (base, spread) in spreads.items():
        noise = np.random.default_rng([zlib.crc32(name.encode()), seed]).standard_normal(out[name].shape)
        drawn = base * np.exp(spread * noise) if base else spread * noise
        out[name] = jnp.asarray(drawn.astype(out[name].dtype))
    for name, factor in factors.items():
        out[name] = (out[name] * factor).astype(out[name].dtype)
    return out
```

```python
from contextlib import ExitStack

import numpy as np
import concourse.bass as bass
from concourse import mybir

F32 = mybir.dt.float32
BF16 = mybir.dt.bfloat16
I32 = mybir.dt.int32
U8 = mybir.dt.uint8
ALU = mybir.AluOpType
ACT = mybir.ActivationFunctionType
AX_X = mybir.AxisListType.X

P = 128
B = 16
GB = 4
GROUPS = B // GB
T = GB * P
H = 16
HD = 8
STRIP = 32
PAD_ROW = 8
HG = 4
INNER = 512
ROUND = float(1.5 * 2 ** 23)
MASKED = float(-2 ** 30)
NEG = -1e9

SMALL = ("L0a", "L0x", "L1x", "L2x")
CROSS = ("L0x", "L1x", "L2x", "L3x")
PHASES = ("L0a", "L0x", "L0f", "L1a", "L1x", "L1f", "L2a", "L2x", "L2f", "L3a", "scan", "L3o", "L3x", "L3f")
BIT = ("L0f", "L1f")
BEFORE_LOOP = -1
XNT_BANK = {"L2a": 2, "L2f": 4, "L3a": 0, "L3x": 6, "L3f": 5}
LN_PHASES = tuple(p for p in PHASES if p not in ("scan", "L3o"))
CHUNK = 16


def sections(parts):
    at, out = 0, {}
    for name, width in parts:
        out[name] = (at, width)
        at += width
    return out, at


W_PARTS = [
    ("L0a", [("q", 512), ("k", 512), ("v", 128), ("o", 128), ("pe", 256)]),
    ("L0x", [("q", 512), ("k", 512), ("v", 128)]),
    ("L0f", [("gate", 512), ("up", 512), ("down", 512)]),
    ("L1a", [("q", 1024), ("k", 1024), ("v", 1024), ("o", 1024)]),
    ("L1x", [("q", 512), ("k", 512), ("v", 128), ("o", 128)]),
    ("L1f", [("w1", 512), ("w2", 512)]),
    ("L2a", [("q", 256), ("qs", 256), ("k", 256), ("ks", 256), ("v", 128), ("gates", 16), ("o", 128)]),
    ("L2x", [("q", 512), ("k", 512), ("v", 128), ("o", 128)]),
    ("L2f", [("sw1", 256), ("sw3", 256), ("sw2", 256), ("router", 8), ("ew1", 1024), ("ew2", 1024)]),
    ("L3a", [("q", 128), ("k", 128), ("v", 128), ("g", 128), ("a", 16), ("b", 16), ("o", 128)]),
    ("L3x", [("q", 128), ("k", 128), ("v", 128), ("o", 128)]),
    ("L3f", [("w1", 512), ("w2", 512)]),
]
W_AT, W_ALL = sections([(f"{p}.{n}", w) for p, parts in W_PARTS for n, w in parts])
W_PHASE = [p for p, _ in W_PARTS]

C_AT, C_ALL = sections(
    [(f"{p}.{n}", HG) for p in SMALL for n in ("bq", "bk")]
    + [("L1a.bq", 8), ("L1a.bk", 8)]
    + [(f"L3a.{n}", 1) for n in ("bq", "bk", "bv", "bg", "scale", "bias", "ba", "bb")]
    + [(f"L3a.conv{n}", 4) for n in "qkv"]
    + [("L3x.bq", 1), ("L3x.bk", 1), ("L3f.b1", 4)])
R_AT, R_ALL = sections([
    ("L1a.bv", 1024), ("L1a.bo", 128), ("L1a.gamma", 128), ("L1a.beta", 128),
    ("L1x.bv", 128), ("L1x.bo", 128), ("L1f.b1", 512), ("L1f.b2", 128),
    ("L2a.gates", 16), ("L2a.bo", 128), ("L2x.bv", 128), ("L2x.bo", 128), ("L2f.bias", 8),
    ("L3a.bo", 128), ("L3x.bv", 128), ("L3x.bo", 128),
    ("L3f.b2", 128), ("L3f.gamma", 128), ("L3f.beta", 128), ("rank", 8)])
K_AT, K_ALL = sections([("ident", P), ("tri", P), ("cos", P), ("sin", P), ("heads", P), ("sel", 4 * P)])


class Signal:

    def __init__(self, sem, per, phases, pre):
        self.sem, self.per, self.before = sem, per, {}
        total = 0
        for phase in phases:
            total += pre.get(phase, 0)
            self.before[phase] = total
            total += per.get(phase, 0) * passes(phase)

    def at(self, phase, it, k=0):
        return it * self.per[phase] + (self.before[phase] + k + 1)


def passes(phase):
    return P // CHUNK if phase == "scan" else GROUPS


def decoder(nc, x, ctx_t, mask1, mask3, w_all, cols, rows, consts, out, phases=PHASES):
    with ExitStack() as stack:
        def sb(name, shape, dt=F32):
            return stack.enter_context(nc.sbuf_tensor(name, shape, dt))

        def sem(name):
            return stack.enter_context(nc.semaphore(name))

        def signal(name, per, pre={}):
            return Signal(sem(name), per, phases, pre)

        def tile(ap, n=GB):
            return ap.rearrange("p (b d) -> p b d", b=n)

        X = sb("X", [P, B, P])
        W = sb("W", [P, W_ALL])
        COLS = sb("COLS", [P, C_ALL])
        ROWS = sb("ROWS", [P, R_ALL])
        K = sb("K", [P, K_ALL])
        XN = sb("XN", [P, GB, P])
        XNT = sb("XNT", [P, T])
        CTX = sb("CTX", [P, T])
        QK = sb("QK", [P, 2 * HG, T])
        QT = QK[:, 0:HG, :]
        KT = QK[:, HG:2 * HG, :]
        VE = sb("VE", [P, GB, H, HD + 1])
        PR = sb("PR", [P, 2, T])
        ON = sb("ON", [P, GB, P])
        OT = sb("OT", [P, T])
        TMP = sb("TMP", [P, T])
        TMP2 = sb("TMP2", [P, T])
        MEXP = sb("MEXP", [P, HG, 4, STRIP])
        MX = sb("MX", [P, H])
        RD = sb("RD", [P, 64])
        OS = sb("OS", [P, 2, H, HD + 1])
        ST = sb("ST", [P, GB, 6])
        MV = sb("MV", [P, GB, 2])
        VEPS = sb("VEPS", [P, 2, GB])
        RSTD = sb("RSTD", [P, 2, GB])
        MV2 = sb("MV2", [P, GB, 2])
        RES = OT
        HALF = sb("HALF", [P, GB])
        ONES = sb("ONES", [P, P])
        I2 = sb("I2", [P, P])
        NEGI = sb("NEGI", [P, P], BF16)
        MKB = sb("MKB", [P, GB, P], BF16)
        FULL = sb("FULL", [P, 2, GB])
        MASK3 = sb("MASK3", [P, P], I32)
        KEEP = sb("KEEP", [P, 2, P])
        AM = sb("AM", [P, 2, GB])
        QS = sb("QS", [P, 2, GB])
        DQ = sb("DQ", [P, 4, GB])
        WSC = sb("WSC", [P, 3, 3])
        SG = sb("SG", [P, 8, GB * 16])
        BIG = sb("BIG", [P, 16384])
        KD = BIG[:, 0:8192].rearrange("p (u j t) -> p u j t", u=16, j=4)
        POS = BIG[:, 8192:16384].rearrange("p (u j s) -> p u j s", u=16, j=4)
        Q1 = QK[:]
        K1 = BIG[:, 0:8192].rearrange("p (c b r t) -> p c b r t", c=8, b=GB, r=2)
        V1 = BIG[:, 8192:12352].rearrange("p (b h d) -> p b h d", b=GB, h=H)
        ON1 = BIG[:, 12352:13376]
        OT1 = BIG[:, 13376:14400].rearrange("p (c t) -> p c t", c=8)
        MROWS1 = BIG[:, 14400:15424].rearrange("p (r t) -> p r t", r=2)
        MASK1 = BIG[:, 8192:8704].bitcast(U8).rearrange("p (b k) -> p b k", b=B)
        WQ = BIG[:, 8192:8960].bitcast(BF16).rearrange("p (m n) -> p m n", m=3)
        XQT = BIG[:, 9216:9472].bitcast(BF16)
        HQT = BIG[:, 9728:10240].bitcast(BF16).rearrange("p (r n) -> p r n", r=2)
        HID = BIG[:, 10240:11264].rearrange("p (r n) -> p r n", r=2)
        HQ = BIG[:, 11264:12288].rearrange("p (r n) -> p r n", r=2)
        PRE = BIG[:, 12288:13312].rearrange("p (r n) -> p r n", r=2)
        WTMP = BIG[:, 13312:14848].rearrange("p (m n) -> p m n", m=3)
        HIDT = BIG[:, 0:2048].rearrange("p (c t) -> p c t", c=4)
        ACC = BIG[:, 2048:2560].rearrange("p (b d) -> p b d", b=GB)
        EXPH = BIG[:, 2560:4608].rearrange("p (c t) -> p c t", c=4)
        XP = BIG[:, 0:3 * GB * 131].rearrange("p (m b t) -> p m b t", m=3, b=GB)
        CV = BIG[:, 2048:3584].rearrange("p (m t) -> p m t", m=3)
        GT = QT.rearrange("p g t -> p (g t)")
        SQ = BIG[:, 0:2048].rearrange("p (f t) -> p f t", f=16)
        SK = BIG[:, 2048:4096].rearrange("p (f t) -> p f t", f=16)
        SV = BIG[:, 4096:6144].rearrange("p (f t) -> p f t", f=16)
        SO = BIG[:, 6144:8192].rearrange("p (f t) -> p f t", f=16)
        SA = BIG[:, 8192:8448].rearrange("p (h t) -> p h t", h=2)
        SBT = BIG[:, 8448:8704].rearrange("p (h t) -> p h t", h=2)
        SAB = BIG[:, 8704:8960].rearrange("p (h t) -> p h t", h=2)
        HIST = BIG[:, 8960:11136].rearrange("p (t f e) -> p t f e", t=CHUNK + 1, f=16)
        PROD = BIG[:, 11136:13184]
        ST2 = BIG[:, 13312:13440].rearrange("p (f e) -> p f e", f=16)
        SU = BIG[:, 13440:13456]
        SKK = BIG[:, 14336:16384].rearrange("p (f t) -> p f t", f=16)
        SP9 = W[:, 0:CHUNK * 144].rearrange("p (t f e) -> p t f e", t=CHUNK, f=16)
        CK = W[:, 2304:2816].rearrange("p (m t f) -> p m t f", m=2, t=CHUNK)
        CA = W[:, 2816:2848].rearrange("p (t h) -> p t h", t=CHUNK)

        VE16 = tile(BIG[:, 8192:8704])
        YT = BIG[:, 0:512]
        PSA = stack.enter_context(nc.psum_tensor("PSA", [P, 8, T], F32))
        PS = [PSA[:, n, :] for n in range(8)]

        scratch = {n: nc.dram_tensor(f"scratch_{n}", (B, P, P), F32, kind="Internal").ap() for n in "qkvo"}
        scratch.update({n: nc.dram_tensor(f"scratch_{n}", (B, H, P), F32, kind="Internal").ap() for n in "ab"})

        def w(name, lo=0, width=None):
            at, full = W_AT[name]
            return W[:, at + lo:at + lo + (full if width is None else width)]

        def col(name, k=0, parts=P):
            return COLS[0:parts, C_AT[name][0] + k:C_AT[name][0] + k + 1]

        def row(name):
            at, n = R_AT[name]
            return ROWS[:, at:at + n]

        def const(name):
            at, n = K_AT[name]
            return K[:, at:at + n]

        ident = const("ident")

        def seqs(it):
            return X[:, bass.ds(it * GB, GB), :]

        def seq(it, i):
            return X[:, bass.ds(it * GB + i, 1), :].rearrange("p a d -> p (a d)")

        def mid(ap, n=GB):
            return ap.unsqueeze(1).to_broadcast([ap.shape[0], n] + list(ap.shape[1:]))

        def last(ap, n):
            return ap.unsqueeze(len(ap.shape)).to_broadcast(list(ap.shape) + [n])

        def tok(i, n=P):
            return slice(i * n, (i + 1) * n)

        each = lambda names, n=1: {p: n for p in names}
        attention = (*SMALL, "L1a")
        loaded = [sem(f"weights_loaded_{p}") for p in W_PHASE]
        inputs_loaded = sem("inputs_loaded")
        masks_loaded = sem("masks_loaded")
        setup_dve = sem("setup_dve")
        setup_pool = sem("setup_pool")
        kd_zero = sem("kd_zero")
        ctx_loaded = signal("ctx_loaded", each(CROSS, 16))
        before_loop = {p: 1 for p in ("L3x", phases[0]) if p in phases}
        before_loop_t = {p: 1 for p in ("L1a", "L2a", *before_loop) if p in phases and p not in BIT}
        ln_stats = signal("ln_stats", each(LN_PHASES), before_loop)
        ln_rstd = signal("ln_rstd", each(LN_PHASES), before_loop)
        xn_ready = signal("xn_ready", each(LN_PHASES), before_loop)
        xnt_psum = signal("xnt_psum", each([p for p in LN_PHASES if p not in BIT]), before_loop_t)
        xnt_ready = signal("xnt_ready", each([p for p in LN_PHASES if p not in BIT]), before_loop_t)
        xq_ready = signal("xq_ready", each(BIT))
        xqt_psum = signal("xqt_psum", each(BIT))
        xqt_ready = signal("xqt_ready", each(BIT))
        other_stats = {"L1a": 1, "L3f": 1, "L1f": 1 + GB}
        stats_ready = signal("stats_ready", other_stats)
        rstd_ready = signal("rstd_ready", other_stats)
        k_psum = signal("k_psum", {**each(SMALL, HG), "L1a": 8})
        q_psum = signal("q_psum", {**each(SMALL, HG), "L1a": 8})
        v_psum = signal("v_psum", {**each(SMALL), "L1a": 8})
        k_ready = signal("k_ready", {**each(SMALL, 4 * HG), "L0a": HG, "L1a": 16, "L2a": 4})
        q_ready = signal("q_ready", {**each(SMALL, HG), "L1a": 8})
        v_ready = signal("v_ready", {**each(SMALL), "L1a": 8})
        units = each(attention, GB * HG)
        units2 = {**units, "L2a": GB * 2}
        s1_psum = signal("s1_psum", units)
        max_taken = signal("max_taken", units)
        mexp_ready = signal("mexp_ready", each(attention, GB))
        mt_psum = signal("mt_psum", each(attention, GB))
        qaug_ready = signal("qaug_ready", each(attention, GB))
        s2_psum = signal("s2_psum", units2)
        p_ready = signal("p_ready", units2)
        pv_done = signal("pv_done", units2)
        on_ready = signal("on_ready", {**each(SMALL, GB), "L1a": GB * HG, "L2a": GB})
        ot_psum = signal("ot_psum", {**each(("L0a", "L1x", "L2x", "L2a")), "L1a": 2 * GB})
        ot_ready = signal("ot_ready", {**each(("L0a", "L1x", "L2x", "L2a")), "L1a": 2 * GB})
        y_psum = signal("y_psum", {**each([p for p in PHASES if p not in ("scan", "L3a", "L0x")]), "L1a": GB})
        y_taken = signal("y_taken", {"L1a": GB}, {"L1a": 1})
        x_updated = signal("x_updated", each([p for p in PHASES if p not in ("scan", "L3a")]), {phases[0]: 1})
        pos_psum = signal("pos_psum", {"L0a": 16})
        pos_even = signal("pos_even_ready", {"L0a": 8})
        pos_odd = signal("pos_odd_ready", {"L0a": 8})
        qd_ready = signal("qd_ready", {"L0a": 2})
        mask_ready = signal("mask_ready", {"L1x": 1})
        wsum_ready = sem("wsum_ready")
        wsum_psum = sem("wsum_psum")
        wq_ready = sem("wq_ready")
        h_psum = signal("h_psum", {"L0f": GB, "L1f": GB, "L2f": 9, "L3f": 4})
        dq_ready = signal("dq_ready", each(("L0f",)))
        pre_ready = signal("pre_ready", {"L1f": GB})
        act_ready = signal("act_ready", {"L0f": GB, "L1f": GB, "L2f": 11, "L3f": 4})
        hq_ready = signal("hq_ready", each(("L0f", "L1f"), GB))
        hqt_psum = signal("hqt_psum", each(("L0f", "L1f"), GB))
        hqt_ready = signal("hqt_ready", each(("L0f", "L1f"), GB))
        shared_ready = signal("shared_ready", {"L2f": 1})
        shared_psum = signal("shared_psum", {"L2f": 1})
        shared_taken = signal("shared_taken", {"L2f": 1})
        expert_used = signal("expert_used", {"L2f": 8})
        expert_psum = signal("expert_psum", {"L2f": 8})
        proj_psum = signal("proj_psum", each(("L2a", "L3a", "L3x")))
        proj_ready = signal("proj_ready", each(("L2a", "L3x")))
        kq_ready = signal("kq_ready", {"L3x": 1})
        gates_psum = signal("gates_psum", {"L2a": 1})
        gates_biased = signal("gates_biased", {"L2a": 1})
        gates_exp = signal("gates_exp", {"L2a": 1})
        beta_ready = signal("beta_ready", {"L2a": 1})
        lnbeta_ready = signal("lnbeta_ready", {"L2a": 1})
        decay_psum = signal("decay_psum", {"L2a": 1})
        decay_ready = signal("decay_ready", {"L2a": 1})
        vp_ready = signal("vp_ready", {"L2a": 1})
        conv_ready = signal("conv_ready", {"L3a": 1})
        silu_ready = signal("silu_ready", {"L3a": 1})
        square_ready = signal("square_ready", {"L3a": 1})
        norm2_psum = signal("norm2_psum", {"L3a": 1})
        norm_ready = signal("norm_ready", {"L3a": 1})
        store_ready = signal("store_ready", {"L3a": 1})
        stored = signal("stored", {"L3a": 80}, {"L3a": 1})
        scan_loaded = sem("scan_loaded")
        scan_step = signal("scan_step", {"scan": 5 * CHUNK})
        scan_done = sem("scan_done")
        scan_stored = sem("scan_stored")
        gn_var = sem("gn_var")
        gn_rstd = sem("gn_rstd")
        y_loaded = signal("y_loaded", {"L3o": 16})
        gated = signal("gated", {"L3o": 1})
        s3_psum = signal("s3_psum", {"L3x": 1})
        s3_shifted = signal("s3_shifted", {"L3x": 1})
        p3_ready = signal("p3_ready", {"L3x": 1})
        pt_psum = signal("pt_psum", {"L3x": 1})
        pt_ready = signal("pt_ready", {"L3x": 1})
        a3_psum = signal("a3_psum", {"L3x": 1})
        a3_ready = signal("a3_ready", {"L3x": 1})
        out_stored = sem("out_stored")

        block = stack.enter_context(nc.Block())
        run = [p for p in PHASES if p in phases]
        final = run[-1]
        quantised = [p for p in run if p in ("L0f", "L1f")]

        def mrows(p, i):
            return MROWS1[:, i % 2, :] if p == "L1a" else (TMP, TMP2)[i % 2][:]

        def kd_zeroed(p):
            return sum(q in run[1:run.index(p) + 1] for q in ("L0f", "L1x"))

        def strip_of(j):
            return slice(STRIP * j, STRIP * (j + 1))

        @block.sync
        def _(sp):
            sp.dma_start(X[:], x.rearrange("b t d -> t b d")).then_inc(inputs_loaded, 16)
            sp.dma_start(K[:], consts).then_inc(inputs_loaded, 16)
            sp.dma_start(COLS[:], cols).then_inc(inputs_loaded, 16)
            for n, (p, parts) in enumerate(W_PARTS):
                lo = W_AT[f"{p}.{parts[0][0]}"][0]
                hi = lo + sum(width for _, width in parts)
                sp.dma_start(W[:, lo:hi], w_all[:, lo:hi]).then_inc(loaded[n], 16)
                if n == 0:
                    sp.dma_start(ROWS[:], rows.to_broadcast([P, R_ALL])).then_inc(inputs_loaded, 16)
                    sp.dma_start(MASK3[:], mask3).then_inc(masks_loaded, 16)
            for p in run:
                if p == "L1x":
                    if run[0] != p:
                        sp.wait_ge(x_updated.sem, x_updated.before[p])
                    sp.dma_start(MASK1, mask1.rearrange("b o q k -> q (b o) k")).then_inc(masks_loaded, 16)
                if p in CROSS:
                    with sp.Fori(0, GROUPS) as it:
                        used = proj_psum if p == "L3x" else v_psum
                        sp.wait_ge(used.sem, used.at(p, it, -1))
                        sp.dma_start(CTX[:], ctx_t[:, bass.ds(it * T, T)]).then_inc(ctx_loaded.sem, 16)
                if p == "L3a":
                    with sp.Fori(0, GROUPS) as it:
                        sp.wait_ge(store_ready.sem, store_ready.at(p, it))
                        for m, n in enumerate("qkv"):
                            sp.dma_start(scratch[n][bass.ds(it * GB, GB)].rearrange("b f t -> f b t"),
                                         tile(CV[:, m, :])).then_inc(stored.sem, 16)
                        for m, n in enumerate("ab"):
                            sp.dma_start(scratch[n][bass.ds(it * GB, GB)].rearrange("b h t -> h b t"),
                                         tile(PR[0:H, m, :])).then_inc(stored.sem, 16)
                if p == "scan":
                    sp.wait_ge(stored.sem, stored.before["L3a"] + 80 * GROUPS)
                    for dst, n in ((SQ, "q"), (SK, "k"), (SV, "v"), (SA, "a"), (SBT, "b")):
                        sp.dma_start(dst.rearrange("p f t -> p (f t)"),
                                     scratch[n].rearrange("b (g f) t -> (b g) (f t)", g=8)).then_inc(scan_loaded, 16)
                    sp.wait_ge(scan_done, 1)
                    sp.dma_start(scratch["o"].rearrange("b (g f) t -> (b g) (f t)", g=8),
                                 SO.rearrange("p f t -> p (f t)")).then_inc(scan_stored, 16)
                    sp.wait_ge(scan_stored, 16)
                if p == "L3o":
                    with sp.Fori(0, GROUPS) as it:
                        sp.wait_ge(x_updated.sem, x_updated.at(p, it, -1))
                        sp.dma_start(tile(YT), scratch["o"][bass.ds(it * GB, GB)].rearrange("b f t -> f b t")
                                     ).then_inc(y_loaded.sem, 16)
            if final not in ("L3a", "scan"):
                sp.wait_ge(x_updated.sem, x_updated.before[final] + GROUPS)
            sp.dma_start(out.rearrange("b t d -> t b d"), X[:]).then_inc(out_stored, 16)
            sp.wait_ge(out_stored, 16)

        @block.gpsimd
        def _(pool):
            pool.memset(HALF[:], -0.5)
            pool.memset(MEXP[:], 0.0)
            pool.memset(VE[:], 1.0)
            pool.memset(ONES[:], 1.0)
            pool.memset(BIG[:, 0:8192], 0.0).then_inc(setup_pool, 1)

            def ln_root(p, it):
                pool.wait_ge(ln_stats.sem, ln_stats.at(p, it))
                pool.tensor_tensor(RSTD[:, 0, :], VEPS[:, 0, :], HALF[:], ALU.pow).then_inc(ln_rstd.sem, 1)

            def root(p, it, k):
                pool.wait_ge(stats_ready.sem, stats_ready.at(p, it, k))
                n = 1 if p == "L1f" and k else GB
                pool.tensor_tensor(RSTD[:, 1, 0:n], VEPS[:, 1, 0:n], HALF[:, 0:n], ALU.pow).then_inc(rstd_ready.sem, 1)

            for p in run:
                if p == "scan":
                    pool.wait_ge(gn_var, 1)
                    pool.tensor_tensor(RD[:, 8:10], RD[:, 6:8], HALF[:, 0:2], ALU.pow).then_inc(gn_rstd, 1)
                if p not in LN_PHASES:
                    continue
                if p in ("L0f", "L1x") and p != run[0]:
                    pool.wait_ge(x_updated.sem, x_updated.before[p])
                    pool.memset(BIG[:, 0:8192], 0.0).then_inc(kd_zero, 1)
                if p == "L1x":
                    pool.wait_ge(masks_loaded, 32)
                if p == "L1a":
                    if p != run[0]:
                        pool.wait_ge(x_updated.sem, x_updated.before["L1a"])
                    pool.memset(V1[:, :, :, 64:65], 1.0).then_inc(setup_pool, 1)
                if p in before_loop:
                    ln_root(p, BEFORE_LOOP)
                with pool.Fori(0, GROUPS) as it:
                    if p == "L1x":
                        pool.wait_ge(x_updated.sem, x_updated.at(p, it, -1))
                        pool.tensor_copy(MKB[:], MASK1[:, bass.ds(it * GB, GB), :]).then_inc(mask_ready.sem, 1)
                    if p == "L1f":
                        root(p, it, 0)
                    ln_root(p, it)
                    for k in range(p == "L1f", stats_ready.per.get(p, 0)):
                        root(p, it, k)

        @block.tensor
        def _(pe):
            pe.wait_ge(inputs_loaded, 64)
            pe.wait_ge(setup_pool, 1)
            pe.wait_ge(setup_dve, 1)

            def transpose_next(p, it):
                pe.wait_ge(xn_ready.sem, xn_ready.at(p, it))
                for i in range(GB):
                    mm = pe.transpose(PS[XNT_BANK.get(p, 5)][:, tok(i)], XN[:, i, :], ident)
                mm.then_inc(xnt_psum.sem, 1)

            def scores1(p, it, i, g):
                u = i * 4 + g
                bank = PS[1 + u % 2]
                if u >= 2:
                    pe.wait_ge(max_taken.sem, max_taken.at(p, it, u - 2))
                if p == "L0a":
                    for j in range(4):
                        pe.matmul(bank[:, tok(j)], KD[:, u, j, :], KT[:, g, tok(i)], start=True, stop=False, skip_group_check=True)
                        mm = pe.matmul(bank[:, tok(j)], POS[:, u, j, :], I2[:], start=False, stop=True, skip_group_check=True)
                elif p == "L1a":
                    for n in range(2):
                        c = 2 * g + n
                        mm = pe.matmul(bank[:, tok(n, 256)], Q1[:, c, tok(i)], K1[:, c, i].rearrange("p r t -> p (r t)"),
                                       start=True, stop=True)
                else:
                    if p == "L1x":
                        pe.matmul(tile(bank), NEGI[:], mid(MKB[:, i, :]), start=True, stop=False, skip_group_check=True)
                    mm = pe.matmul(bank, QT[:, g, tok(i)], KD[:, u].rearrange("p j t -> p (j t)"), start=p != "L1x", stop=True,
                                   skip_group_check=True)
                mm.then_inc(s1_psum.sem, 1)

            def maxima(p, it, i):
                pe.wait_ge(mexp_ready.sem, mexp_ready.at(p, it, i))
                for g in range(HG):
                    mm = pe.transpose(PS[5][:, tok(g)], MEXP[:, g].rearrange("p j r -> p (j r)"), ident)
                mm.then_inc(mt_psum.sem, 1)

            def scores2(p, it, i, g):
                u = i * 4 + g
                bank = PS[3 + u % 2]
                if g == 0:
                    pe.wait_ge(qaug_ready.sem, qaug_ready.at(p, it, i))
                if u >= 2:
                    pe.wait_ge(p_ready.sem, p_ready.at(p, it, u - 2))
                if p == "L0a":
                    pe.matmul(bank, KT[:, g, tok(i)], KD[:, u].rearrange("p j t -> p (j t)"), start=True, stop=False,
                              skip_group_check=True)
                    pe.matmul(bank, I2[:], POS[:, u].rearrange("p j s -> p (j s)"), start=False, stop=False, skip_group_check=True)
                if p == "L1x":
                    pe.matmul(tile(bank), MKB[:, i, :], mid(NEGI[:]), start=True, stop=False, skip_group_check=True)
                for j in range(4):
                    if p == "L1a":
                        c, r = 2 * g + j // 2, j % 2
                        pe.matmul(bank[:, tok(j)], K1[:, c, i, r, :], Q1[:, c, tok(i)], start=True, stop=False, skip_group_check=True)
                    if p in ("L0a", "L1a"):
                        mm = pe.matmul(bank[:, tok(j)], const("sel")[:, tok(j)], mrows(p, i)[:, tok(g)], start=False, stop=True,
                                       skip_group_check=True)
                    else:
                        mm = pe.matmul(bank[:, tok(j)], KD[:, u, j, :], QT[:, g, tok(i)], start=p != "L1x", stop=True,
                                       skip_group_check=True)
                mm.then_inc(s2_psum.sem, 1)

            def product_v(p, it, i, g):
                u = i * 4 + g
                pe.wait_ge(p_ready.sem, p_ready.at(p, it, u))
                if p == "L1a":
                    if u >= 2:
                        pe.wait_ge(on_ready.sem, on_ready.at(p, it, u - 2))
                elif g == 0 and i >= 2:
                    pe.wait_ge(on_ready.sem, on_ready.at(p, it, i - 2))
                for j in range(4):
                    h = 4 * g + j
                    if p == "L1a":
                        dst, val = PS[6 + u % 2][:, j * 65:(j + 1) * 65], V1[:, i, h, :]
                    else:
                        dst, val = PS[6 + i % 2][:, h * 9:(h + 1) * 9], VE[:, i, h, :]
                    mm = pe.matmul(dst, PR[:, u % 2, tok(j)], val, start=True, stop=True)
                if p == "L1x" and g == 3:
                    mm = pe.matmul(PS[6 + i % 2][:, 144:288], ONES[:], VE[:, i].rearrange("p h d -> p (h d)"),
                                   start=True, stop=True)
                mm.then_inc(pv_done.sem, 1)

            def attend(p, it, tail=None):
                for g in range(HG):
                    scores1(p, it, 0, g)
                scores1(p, it, 1, 0)
                scores1(p, it, 1, 1)
                maxima(p, it, 0)
                scores1(p, it, 1, 2)
                scores1(p, it, 1, 3)
                for i in range(GB):
                    scores2(p, it, i, 0)
                    if i + 1 < GB:
                        maxima(p, it, i + 1)
                    else:
                        transpose_next(p, it)
                    if i + 2 < GB:
                        scores1(p, it, i + 2, 0)
                    if tail and i:
                        tail(p, it, i - 1)
                    for g in range(1, HG):
                        scores2(p, it, i, g)
                        product_v(p, it, i, g - 1)
                        if i + 2 < GB:
                            scores1(p, it, i + 2, g)
                    product_v(p, it, i, HG - 1)
                if tail:
                    tail(p, it, GB - 1)

            def project_out(p, it):
                pe.wait_ge(on_ready.sem, on_ready.at(p, it, GB - 1))
                for i in range(GB):
                    mm = pe.transpose(PS[7][:, tok(i)], ON[:, i, :], ident)
                mm.then_inc(ot_psum.sem, 1)
                pe.wait_ge(ot_ready.sem, ot_ready.at(p, it))
                for i in range(GB):
                    mm = pe.matmul(PS[0][:, tok(i)], OT[:, tok(i)], w(f"{p}.o"), start=True, stop=True)
                mm.then_inc(y_psum.sem, 1)

            def small(p, it):
                cross = p in CROSS
                src = CTX if cross else XNT

                def keys_values():
                    for g in range(HG):
                        mm = pe.matmul(PS[g], w(f"{p}.k", g * P, P), src[:], start=True, stop=True)
                        mm.then_inc(k_psum.sem, 1)

                def values():
                    pe.wait_ge(k_ready.sem, k_ready.at(p, it, 0 if p == "L0a" else 3))
                    for i in range(GB):
                        mm = pe.matmul(PS[0][:, tok(i)], src[:, tok(i)], w(f"{p}.v"), start=True, stop=True)
                    mm.then_inc(v_psum.sem, 1)

                if cross:
                    pe.wait_ge(ctx_loaded.sem, ctx_loaded.at(p, it, 15))
                    pe.wait_ge(x_updated.sem, x_updated.at(p, it, -1))
                    keys_values()
                    values()
                else:
                    pe.wait_ge(x_updated.sem, x_updated.at(p, it, -1))
                    pe.wait_ge(xnt_ready.sem, xnt_ready.at(p, it - 1))
                    keys_values()
                pe.wait_ge(xnt_ready.sem, xnt_ready.at(p, it - 1))
                for g in range(HG):
                    pe.matmul(PS[4 + g], w(f"{p}.q", g * P, P), XNT[:], start=True, stop=True).then_inc(q_psum.sem, 1)
                if not cross:
                    values()
                pe.wait_ge(v_ready.sem, v_ready.at(p, it))
                pe.wait_ge(k_ready.sem, k_ready.at(p, it, k_ready.per[p] - 1))
                pe.wait_ge(q_ready.sem, q_ready.at(p, it, HG - 1))
                if p == "L0a":
                    pe.wait_ge(qd_ready.sem, qd_ready.at(p, it, 1))
                    pe_table = w("L0a.pe")
                    for c in range(16):
                        if c >= 2:
                            copied = (pos_even, pos_odd)[c % 2]
                            pe.wait_ge(copied.sem, copied.at(p, it, c // 2 - 1))
                        for n in range(8):
                            s = 8 * c + n
                            mm = pe.matmul(PS[1 + c % 2][:, n * 64:(n + 1) * 64], pe_table[:, P - 1 - s:2 * P - 1 - s],
                                           KD[:, :, :, s].rearrange("p u j -> p (u j)"), start=True, stop=True)
                        mm.then_inc(pos_psum.sem, 1)
                    pe.wait_ge(pos_even.sem, pos_even.at(p, it, 7))
                    pe.wait_ge(pos_odd.sem, pos_odd.at(p, it, 7))
                if p == "L1x":
                    pe.wait_ge(mask_ready.sem, mask_ready.at(p, it))
                attend(p, it)
                if p != "L0x":
                    project_out(p, it)

            def l1_attention(p, it):
                pe.wait_ge(y_taken.sem, y_taken.at(p, it, -1))
                pe.wait_ge(xnt_ready.sem, xnt_ready.at(p, it - 1))
                for c in range(8):
                    if c >= 4:
                        pe.wait_ge(q_ready.sem, q_ready.at(p, it, c - 4))
                    pe.matmul(PS[c % 4], w("L1a.q", c * P, P), XNT[:], start=True, stop=True).then_inc(q_psum.sem, 1)
                    if c >= 4:
                        pe.wait_ge(k_ready.sem, k_ready.at(p, it, 2 * (c - 4) + 1))
                    pe.matmul(PS[4 + c % 4], w("L1a.k", c * P, P), XNT[:], start=True, stop=True).then_inc(k_psum.sem, 1)
                for c in range(8):
                    if c < 4:
                        pe.wait_ge(q_ready.sem, q_ready.at(p, it, 4 + c))
                    else:
                        pe.wait_ge(v_ready.sem, v_ready.at(p, it, c - 4))
                    pe.matmul(PS[c % 4], XNT[:, tok(c // 2)], w("L1a.v", (c % 2) * T, T), start=True, stop=True).then_inc(v_psum.sem, 1)
                pe.wait_ge(k_ready.sem, k_ready.at(p, it, 15))
                pe.wait_ge(v_ready.sem, v_ready.at(p, it, 7))

                def tail(p, it, i):
                    pe.wait_ge(on_ready.sem, on_ready.at(p, it, i * HG + 3))
                    for half in range(2):
                        if half:
                            pe.wait_ge(ot_ready.sem, ot_ready.at(p, it, 2 * i))
                        elif i:
                            pe.wait_ge(y_taken.sem, y_taken.at(p, it, i - 1))
                        for c in range(4):
                            mm = pe.transpose(PS[0][:, tok(c)], ON1[:, tok(4 * half + c)], ident)
                        mm.then_inc(ot_psum.sem, 1)
                    pe.wait_ge(ot_ready.sem, ot_ready.at(p, it, 2 * i + 1))
                    for c in range(8):
                        mm = pe.matmul(PS[0][:, 0:P], OT1[:, c, :], w("L1a.o", c * P, P), start=c == 0, stop=c == 7)
                    mm.then_inc(y_psum.sem, 1)

                attend(p, it, tail)

            def bit_ffn(p, it):
                pe.wait_ge(xq_ready.sem, xq_ready.at(p, it))
                for i in range(GB):
                    mm = pe.transpose(PS[7][:, tok(i)], XN[:, i, :], ident)
                mm.then_inc(xqt_psum.sem, 1)
                pe.wait_ge(xqt_ready.sem, xqt_ready.at(p, it))
                gated_ = p == "L0f"

                def up(i):
                    if i >= 2:
                        pe.wait_ge(hq_ready.sem, hq_ready.at(p, it, i - 2))
                    mm = pe.matmul(PS[2 * (i % 2)], XQT[:, tok(i)], WQ[:, 0, :], start=True, stop=True)
                    if gated_:
                        mm = pe.matmul(PS[2 * (i % 2) + 1], XQT[:, tok(i)], WQ[:, 1, :], start=True, stop=True)
                    mm.then_inc(h_psum.sem, 1)

                up(0)
                for i in range(GB):
                    if i + 1 < GB:
                        up(i + 1)
                    pe.wait_ge(hq_ready.sem, hq_ready.at(p, it, i))
                    for c in range(4):
                        mm = pe.transpose(PS[4 + i % 2][:, tok(c)], HQ[:, i % 2, tok(c)], ident)
                    mm.then_inc(hqt_psum.sem, 1)
                    pe.wait_ge(hqt_ready.sem, hqt_ready.at(p, it, i))
                    for c in range(4):
                        mm = pe.matmul(PS[6][:, tok(i)], HQT[:, i % 2, tok(c)], WQ[:, 2, tok(c)], start=c == 0, stop=c == 3)
                mm.then_inc(y_psum.sem, 1)

            def weight_means(value):
                pe.wait_ge(wsum_ready, value)
                pe.matmul(PS[0][:, 0:3], ONES[:], WSC[:, 0, :], start=True, stop=True).then_inc(wsum_psum, 1)

            def linear_attention(p, it):
                pe.wait_ge(x_updated.sem, x_updated.at(p, it, -1))
                pe.wait_ge(xnt_ready.sem, xnt_ready.at(p, it - 1))
                for n, name in enumerate(("q", "qs", "k", "ks")):
                    for g in range(2):
                        mm = pe.matmul(PS[2 * n + g], w(f"{p}.{name}", g * P, P), XNT[:], start=True, stop=True)
                mm.then_inc(proj_psum.sem, 1)
                pe.wait_ge(proj_ready.sem, proj_ready.at(p, it))
                for i in range(GB):
                    pe.matmul(PS[0][:, tok(i)], XNT[:, tok(i)], w(f"{p}.v"), start=True, stop=True)
                    mm = pe.matmul(PS[1][:, tok(i, 16)], XNT[:, tok(i)], w(f"{p}.gates"), start=True, stop=True)
                mm.then_inc(gates_psum.sem, 1)
                pe.wait_ge(lnbeta_ready.sem, lnbeta_ready.at(p, it))
                pe.matmul(PS[2][:, 0:32], const("tri"), SG[:, 3, 0:32], start=True, stop=True).then_inc(decay_psum.sem, 1)

                def scores(u):
                    i, g = u // 2, u % 2
                    if u >= 2:
                        pe.wait_ge(p_ready.sem, p_ready.at(p, it, u - 2))
                    for j in range(4):
                        mm = pe.matmul(PS[3 + u % 2][:, tok(j)], KD[:, 4 * i + g, j, :], QT[:, g, tok(i)], start=True, stop=True)
                    mm.then_inc(s2_psum.sem, 1)

                pe.wait_ge(k_ready.sem, k_ready.at(p, it, 3))
                scores(0)
                for u in range(8):
                    if u < 7:
                        scores(u + 1)
                    if u == 0:
                        pe.wait_ge(vp_ready.sem, vp_ready.at(p, it))
                    pe.wait_ge(p_ready.sem, p_ready.at(p, it, u))
                    i, g = u // 2, u % 2
                    if g == 0 and i >= 2:
                        pe.wait_ge(on_ready.sem, on_ready.at(p, it, i - 2))
                    for j in range(4):
                        h = 4 * g + j
                        mm = pe.matmul(PS[5 + i % 2][:, h * 16:h * 16 + 16], PR[:, u % 2, tok(j)],
                                       VE16[:, i, h * 16:h * 16 + 16], start=True, stop=True)
                    mm.then_inc(pv_done.sem, 1)
                    if u == 5:
                        transpose_next(p, it)
                project_out(p, it)

            def experts(p, it):
                pe.wait_ge(x_updated.sem, x_updated.at(p, it, -1))
                pe.wait_ge(xnt_ready.sem, xnt_ready.at(p, it - 1))
                for c in range(2):
                    pe.matmul(PS[c], w("L2f.sw1", c * P, P), XNT[:], start=True, stop=True)
                    pe.matmul(PS[2 + c], w("L2f.sw3", c * P, P), XNT[:], start=True, stop=True)
                for i in range(GB):
                    mm = pe.matmul(PS[6][:, tok(i, 8)], XNT[:, tok(i)], w("L2f.router"), start=True, stop=True)
                mm.then_inc(h_psum.sem, 1)
                pe.wait_ge(shared_ready.sem, shared_ready.at(p, it))
                for i in range(GB):
                    for c in range(2):
                        mm = pe.matmul(PS[7][:, tok(i)], HIDT[:, c, tok(i)], w("L2f.sw2", c * P, P), start=c == 0, stop=c == 1)
                mm.then_inc(shared_psum.sem, 1)

                def up(e):
                    if e >= 2:
                        pe.wait_ge(act_ready.sem, act_ready.at(p, it, 3 + e - 2))
                    pe.matmul(PS[e % 2], w("L2f.ew1", e * P, P), XNT[:], start=True, stop=True).then_inc(h_psum.sem, 1)

                up(0)
                for e in range(8):
                    if e < 7:
                        up(e + 1)
                    pe.wait_ge(act_ready.sem, act_ready.at(p, it, 3 + e))
                    if e >= 2:
                        pe.wait_ge(expert_used.sem, expert_used.at(p, it, e - 2))
                    for i in range(GB):
                        mm = pe.matmul(PS[2 + e % 2][:, tok(i)], EXPH[:, e % 4, tok(i)], w("L2f.ew2", e * P, P),
                                       start=True, stop=True)
                    mm.then_inc(expert_psum.sem, 1)
                    if e == 6:
                        transpose_next(p, it)
                pe.nop().then_inc(y_psum.sem, 1)

            def delta_project(p, it):
                pe.wait_ge(xnt_ready.sem, xnt_ready.at(p, it - 1))
                for n, name in enumerate("qkvg"):
                    pe.matmul(PS[n], w(f"L3a.{name}"), XNT[:], start=True, stop=True)
                for n, name in enumerate("ab"):
                    mm = pe.matmul(PS[4 + n][0:H, :], w(f"L3a.{name}"), XNT[:], start=True, stop=True)
                mm.then_inc(proj_psum.sem, 1)
                pe.wait_ge(square_ready.sem, square_ready.at(p, it))
                pe.matmul(PS[6], const("heads"), TMP[:], start=True, stop=True)
                pe.matmul(PS[7], const("heads"), TMP2[:], start=True, stop=True).then_inc(norm2_psum.sem, 1)
                transpose_next(p, it)

            def delta_out(p, it):
                pe.wait_ge(gated.sem, gated.at(p, it))
                for i in range(GB):
                    mm = pe.matmul(PS[1][:, tok(i)], TMP2[:, tok(i)], w("L3a.o"), start=True, stop=True)
                mm.then_inc(y_psum.sem, 1)

            def one_head(p, it):
                pe.wait_ge(xnt_ready.sem, xnt_ready.at(p, it - 1))
                pe.wait_ge(ctx_loaded.sem, ctx_loaded.at(p, it, 15))
                pe.wait_ge(x_updated.sem, x_updated.at(p, it, -1))
                pe.matmul(PS[0], w("L3x.k"), CTX[:], start=True, stop=True)
                for i in range(GB):
                    pe.matmul(PS[2][:, tok(i)], CTX[:, tok(i)], w("L3x.v"), start=True, stop=True)
                pe.matmul(PS[1], w("L3x.q"), XNT[:], start=True, stop=True).then_inc(proj_psum.sem, 1)
                pe.wait_ge(kq_ready.sem, kq_ready.at(p, it))
                for i in range(GB):
                    mm = pe.matmul(PS[3][:, tok(i)], QT[:, 0, tok(i)], KT[:, 0, tok(i)], start=True, stop=True)
                mm.then_inc(s3_psum.sem, 1)
                transpose_next(p, it)
                pe.wait_ge(p3_ready.sem, p3_ready.at(p, it))
                for i in range(GB):
                    mm = pe.transpose(PS[4][:, tok(i)], PR[:, 0, tok(i)], ident)
                mm.then_inc(pt_psum.sem, 1)
                pe.wait_ge(pt_ready.sem, pt_ready.at(p, it))
                pe.wait_ge(proj_ready.sem, proj_ready.at(p, it))
                for i in range(GB):
                    mm = pe.matmul(PS[5][:, tok(i)], ON[:, i, :], PR[:, 1, tok(i)], start=True, stop=True)
                mm.then_inc(a3_psum.sem, 1)
                pe.wait_ge(a3_ready.sem, a3_ready.at(p, it))
                for i in range(GB):
                    mm = pe.matmul(PS[0][:, tok(i)], OT[:, tok(i)], w("L3x.o"), start=True, stop=True)
                mm.then_inc(y_psum.sem, 1)

            def relu_ffn(p, it):
                pe.wait_ge(x_updated.sem, x_updated.at(p, it, -1))
                pe.wait_ge(xnt_ready.sem, xnt_ready.at(p, it - 1))
                for c in range(4):
                    pe.matmul(PS[c], w("L3f.w1", c * P, P), XNT[:], start=True, stop=True).then_inc(h_psum.sem, 1)
                transpose_next(p, it)
                pe.wait_ge(act_ready.sem, act_ready.at(p, it, 3))
                for i in range(GB):
                    for c in range(4):
                        mm = pe.matmul(PS[4][:, tok(i)], HIDT[:, c, tok(i)], w("L3f.w2", c * P, P), start=c == 0, stop=c == 3)
                mm.then_inc(y_psum.sem, 1)

            bodies = {**each(SMALL, small), "L1a": l1_attention, "L0f": bit_ffn, "L1f": bit_ffn, "L2a": linear_attention,
                      "L2f": experts, "L3a": delta_project, "L3o": delta_out, "L3x": one_head, "L3f": relu_ffn}
            for p in run:
                if p in W_PHASE:
                    pe.wait_ge(loaded[W_PHASE.index(p)], 16)
                if p == "scan":
                    continue
                if p in ("L0f", "L1f"):
                    weight_means(quantised.index(p) + 1)
                    pe.wait_ge(wq_ready, quantised.index(p) + 1)
                if p == "L1a":
                    pe.wait_ge(setup_pool, 2)
                pe.wait_ge(x_updated.sem, x_updated.before[p])
                if p in before_loop_t:
                    transpose_next(p, BEFORE_LOOP)
                with pe.Fori(0, GROUPS) as it:
                    bodies[p](p, it)

        @block.scalar
        def _(act):
            act.wait_ge(inputs_loaded, 64)

            def xnt_next(p, it):
                act.wait_ge(xnt_psum.sem, xnt_psum.at(p, it))
                act.activation(XNT[:], PS[XNT_BANK.get(p, 5)], ACT.Copy).then_inc(xnt_ready.sem, 1)

            def exponentials(p, it, scale):
                for u in range(GB * HG):
                    act.wait_ge(s2_psum.sem, s2_psum.at(p, it, u))
                    if u >= 2:
                        act.wait_ge(pv_done.sem, pv_done.at(p, it, u - 2))
                    act.activation(PR[:, u % 2, :], PS[3 + u % 2], ACT.Exp, scale=scale).then_inc(p_ready.sem, 1)
                    if p == "L1a" and u % HG == 0 and u:
                        outputs_t(p, it, u // HG - 1)
                    if u == 13:
                        xnt_next(p, it)
                if p == "L1a":
                    outputs_t(p, it, GB - 1)

            def outputs_t(p, it, i):
                for half in range(2):
                    act.wait_ge(ot_psum.sem, ot_psum.at(p, it, 2 * i + half))
                    act.activation(OT1[:, 4 * half:4 * half + 4, :], tile(PS[0]), ACT.Copy).then_inc(ot_ready.sem, 1)

            def small(p, it):
                for g in range(HG):
                    act.wait_ge(k_psum.sem, k_psum.at(p, it, g))
                    func = ACT.Relu if p == "L0x" else ACT.Identity
                    if p == "L0a":
                        act.activation(KT[:, g, :], PS[g], func, bias=col(f"{p}.bk", g)).then_inc(k_ready.sem, 1)
                        continue
                    for j in range(4):
                        r = strip_of(j)
                        act.activation(KD.rearrange("p (i g) j t -> p i g j t", g=HG)[r, :, g, j, :], tile(PS[g][r]), func,
                                       bias=col(f"{p}.bk", g)[r]).then_inc(k_ready.sem, 1)
                if p == "L0a":
                    for j in range(3):
                        if j == 0:
                            act.wait_ge(q_ready.sem, q_ready.at(p, it, HG - 1))
                        r = strip_of(j)
                        ins = act.copy(KD.rearrange("p (i g) j t -> p i g j t", g=HG)[r, :, :, j, :],
                                       QT[r].rearrange("p g (i t) -> p i g t", i=GB))
                    ins.then_inc(qd_ready.sem, 1)
                    for c in range(0, 16, 2):
                        act.wait_ge(pos_psum.sem, pos_psum.at(p, it, c))
                        act.activation(POS.rearrange("p u j s -> p (u j) s")[:, :, 8 * c:8 * c + 8],
                                       PS[1].rearrange("p (s u) -> p u s", u=64), ACT.Copy).then_inc(pos_even.sem, 1)
                exponentials(p, it, float(HD) ** -0.5)
                if p != "L0x":
                    act.wait_ge(ot_psum.sem, ot_psum.at(p, it))
                    act.activation(OT[:], PS[7], ACT.Copy).then_inc(ot_ready.sem, 1)

            def l1_attention(p, it):
                for c in range(8):
                    act.wait_ge(k_psum.sem, k_psum.at(p, it, c))
                    for r in range(2):
                        half = slice(64 * r, 64 * r + 64)
                        act.activation(K1[half, c, :, r, :], tile(PS[4 + c % 4][half]), ACT.Identity,
                                       bias=col("L1a.bk", c)[half]).then_inc(k_ready.sem, 1)
                exponentials(p, it, 64.0 ** -0.5)

            def bit_ffn(p, it):
                act.wait_ge(xqt_psum.sem, xqt_psum.at(p, it))
                act.activation(XQT, PS[7], ACT.Copy).then_inc(xqt_ready.sem, 1)
                if p == "L0f":
                    act.wait_ge(dq_ready.sem, dq_ready.at(p, it))
                for i in range(GB):
                    if p == "L0f":
                        act.wait_ge(h_psum.sem, h_psum.at(p, it, i))
                        if i >= 2:
                            act.wait_ge(hq_ready.sem, hq_ready.at(p, it, i - 2))
                        act.activation(HID[:, i % 2, :], PS[2 * (i % 2)], ACT.Silu, scale=DQ[:, 0, i:i + 1]).then_inc(act_ready.sem, 1)
                    else:
                        act.wait_ge(pre_ready.sem, pre_ready.at(p, it, i))
                        act.activation(HID[:, i % 2, :], PRE[:, i % 2, :], ACT.Gelu).then_inc(act_ready.sem, 1)
                    act.wait_ge(hqt_psum.sem, hqt_psum.at(p, it, i))
                    act.activation(HQT[:, i % 2, :], PS[4 + i % 2], ACT.Copy).then_inc(hqt_ready.sem, 1)

            def linear_attention(p, it):
                act.wait_ge(proj_ready.sem, proj_ready.at(p, it))
                for j in range(4):
                    r = strip_of(j)
                    act.copy(KD.rearrange("p (i g) j t -> p i g j t", g=HG)[r, :, 0:2, j, :],
                             KT[r, 0:2].rearrange("p g (i t) -> p i g t", i=GB)).then_inc(k_ready.sem, 1)
                act.wait_ge(gates_biased.sem, gates_biased.at(p, it))
                act.activation(SG[:, 1, :], SG[:, 0, :], ACT.Exp, scale=-1.0).then_inc(gates_exp.sem, 1)
                act.wait_ge(beta_ready.sem, beta_ready.at(p, it))
                act.activation(SG[:, 3, 0:32], SG[:, 2, 0:32], ACT.Ln).then_inc(lnbeta_ready.sem, 1)
                act.wait_ge(decay_psum.sem, decay_psum.at(p, it))
                act.activation(SG[:, 4, 0:32], PS[2][:, 0:32], ACT.Exp)
                act.activation(SG[:, 5, 0:32], PS[2][:, 0:32], ACT.Exp, scale=-1.0).then_inc(decay_ready.sem, 1)
                xnt_next(p, it)
                act.wait_ge(ot_psum.sem, ot_psum.at(p, it))
                act.activation(OT[:], PS[7], ACT.Copy).then_inc(ot_ready.sem, 1)

            def experts(p, it):
                act.wait_ge(h_psum.sem, h_psum.at(p, it, 0))
                for c in range(2):
                    act.activation(HIDT[:, c, :], PS[c], ACT.Silu).then_inc(act_ready.sem, 1)
                act.activation(SG[:, 0, 0:32], PS[6][:, 0:32], ACT.Sigmoid).then_inc(act_ready.sem, 1)
                for e in range(8):
                    act.wait_ge(h_psum.sem, h_psum.at(p, it, 1 + e))
                    if e >= 4:
                        act.wait_ge(expert_psum.sem, expert_psum.at(p, it, e - 4))
                    act.activation(EXPH[:, e % 4, :], PS[e % 2], ACT.Gelu).then_inc(act_ready.sem, 1)
                xnt_next(p, it)

            def delta_project(p, it):
                act.wait_ge(proj_psum.sem, proj_psum.at(p, it))
                act.activation(GT[:, bass.ds(it * T, T)], PS[3], ACT.Silu, bias=col("L3a.bg"))
                act.wait_ge(conv_ready.sem, conv_ready.at(p, it))
                act.activation(CV, CV, ACT.Silu).then_inc(silu_ready.sem, 1)
                for m, n in enumerate("ab"):
                    act.activation(PR[0:H, m, :], PS[4 + m][0:H, :], ACT.Sigmoid, bias=col(f"L3a.b{n}", 0, H))
                act.wait_ge(norm2_psum.sem, norm2_psum.at(p, it))
                act.activation(TMP[:], PS[6], ACT.Sqrt)
                act.activation(TMP2[:], PS[7], ACT.Sqrt).then_inc(norm_ready.sem, 1)
                xnt_next(p, it)

            def one_head(p, it):
                act.wait_ge(proj_psum.sem, proj_psum.at(p, it))
                act.activation(KT[:, 0, :], PS[0], ACT.Identity, bias=col("L3x.bk"))
                act.activation(QT[:, 0, :], PS[1], ACT.Identity, bias=col("L3x.bq")).then_inc(kq_ready.sem, 1)
                xnt_next(p, it)
                act.wait_ge(s3_shifted.sem, s3_shifted.at(p, it))
                act.activation(PR[:, 0, :], TMP[:], ACT.Exp).then_inc(p3_ready.sem, 1)
                act.wait_ge(pt_psum.sem, pt_psum.at(p, it))
                act.activation(PR[:, 1, :], PS[4], ACT.Copy).then_inc(pt_ready.sem, 1)
                act.wait_ge(a3_psum.sem, a3_psum.at(p, it))
                act.activation(OT[:], PS[5], ACT.Copy).then_inc(a3_ready.sem, 1)

            def relu_ffn(p, it):
                for c in range(4):
                    act.wait_ge(h_psum.sem, h_psum.at(p, it, c))
                    act.activation(HIDT[:, c, :], PS[c], ACT.Relu, bias=col("L3f.b1", c)).then_inc(act_ready.sem, 1)
                xnt_next(p, it)

            bodies = {**each(SMALL, small), "L1a": l1_attention, "L0f": bit_ffn, "L1f": bit_ffn, "L2a": linear_attention,
                      "L2f": experts, "L3a": delta_project, "L3x": one_head, "L3f": relu_ffn}
            for p in run:
                if p in ("L1a", "L1x") and kd_zeroed(p):
                    act.wait_ge(kd_zero, kd_zeroed(p))
                if p == "L0x" or p in ("L0a", "L2a", "L2x"):
                    act.wait_ge(setup_pool, 1)
                if p in before_loop_t:
                    act.drain()
                    xnt_next(p, BEFORE_LOOP)
                if p in bodies:
                    with act.Fori(0, GROUPS) as it:
                        bodies[p](p, it)

        @block.vector
        def _(dve):
            dve.wait_ge(inputs_loaded, 64)
            dve.tensor_scalar(I2[:], ident, 2.0, None, ALU.mult)
            dve.tensor_scalar(NEGI[:], ident, MASKED, None, ALU.mult).then_inc(setup_dve, 1)
            dve.wait_ge(setup_pool, 1)
            dve.nop().then_inc(x_updated.sem, 1)

            def moments(src, mv):
                for i in range(GB):
                    dve.bn_stats(ST[:, i, :], src(i))
                dve.drain()
                for i in range(GB):
                    dve.bn_aggr(mv[:, i, :], ST[:, i, :])
                dve.drain()

            def next_group(it):
                return (it + 1) % GROUPS

            def next_moments(p, it):
                moments(lambda i: seq(next_group(it), i), MV)
                dve.tensor_scalar(VEPS[:, 0, :], MV[:, :, 1], 1e-5, None, ALU.add).then_inc(ln_stats.sem, 1)

            def next_normed(p, it):
                dve.wait_ge(ln_rstd.sem, ln_rstd.at(p, it))
                if it is not BEFORE_LOOP:
                    if p in BIT:
                        dve.wait_ge(xqt_psum.sem, xqt_psum.at(p, it))
                    else:
                        dve.wait_ge(xnt_psum.sem, xnt_psum.at(p, it - 1))
                for i in range(GB):
                    ins = dve.tensor_scalar(XN[:, i, :], seq(next_group(it), i), MV[:, i, 0:1], RSTD[:, 0, i:i + 1],
                                            ALU.subtract, ALU.mult)
                ins.then_inc(xn_ready.sem, 1)

            def add_to_x(p, it, y, bias=None):
                if bias is not None:
                    dve.tensor_tensor(tile(TMP[:]), y, mid(bias), ALU.add)
                    dve.drain()
                    y = tile(TMP[:])
                dve.tensor_tensor(seqs(it), seqs(it), y, ALU.add).then_inc(x_updated.sem, 1)
                dve.drain()

            def take_max(p, it, i, between=None):
                for g in range(HG):
                    u = i * 4 + g
                    dve.wait_ge(s1_psum.sem, s1_psum.at(p, it, u))
                    dve.tensor_reduce(MX[:, 4 * g:4 * g + 4], tile(PS[1 + u % 2]), AX_X, ALU.max).then_inc(max_taken.sem, 1)
                    if between:
                        between(g)
                dve.drain()
                scale = FULL[:, 1, i:i + 1] if p == "L1x" else 1.0
                dve.tensor_scalar(MEXP[:, :, :, PAD_ROW], tile(MX[:], HG), scale, -1.0, ALU.mult, ALU.mult
                                  ).then_inc(mexp_ready.sem, 1)

            def augment_q(p, it, i):
                dve.wait_ge(mt_psum.sem, mt_psum.at(p, it, i))
                if p in ("L0a", "L1a"):
                    ins = dve.tensor_copy(mrows(p, i), PS[5])
                else:
                    q = QT[:, :, tok(i)]
                    ins = dve.tensor_tensor(q, q, tile(PS[5], HG), ALU.add)
                ins.then_inc(qaug_ready.sem, 1)

            def normalise(p, it, i):
                dve.wait_ge(pv_done.sem, pv_done.at(p, it, i * HG + HG - 1))
                o = PS[6 + i % 2][:, 0:144].rearrange("p (h d) -> p h d", h=H)
                if p == "L1x":
                    vs = PS[6 + i % 2][:, 144:288].rearrange("p (h d) -> p h d", h=H)
                    os = OS[:, i % 2]
                    dve.tensor_copy(os, o)
                    dve.drain()
                    dve.scalar_tensor_tensor(os, vs, FULL[:, 0, i:i + 1], os, ALU.mult, ALU.add)
                    dve.drain()
                    o = os
                rd = RD[:, H * (i % 2):H * (i % 2) + H]
                dve.reciprocal(rd, o[:, :, HD])
                dve.drain()
                dve.tensor_tensor(ON[:, i, :].rearrange("p (h d) -> p h d", h=H), o[:, :, 0:HD], last(rd, HD),
                                  ALU.mult).then_inc(on_ready.sem, 1)

            def prepare_next(p, it, i):
                if i == 0:
                    next_moments(p, it)
                if i == 1:
                    next_normed(p, it)

            def attend_by_unit(p, it, norm_unit):
                take_max(p, it, 0)
                augment_q(p, it, 0)
                take_max(p, it, 1)
                for i in range(GB):
                    if i + 1 < GB:
                        augment_q(p, it, i + 1)
                    if i + 2 < GB:
                        take_max(p, it, i + 2, lambda g: norm_unit(i, g))
                    else:
                        for g in range(HG):
                            norm_unit(i, g)
                    prepare_next(p, it, i)

            def attend(p, it, norm):
                take_max(p, it, 0)
                augment_q(p, it, 0)
                take_max(p, it, 1)
                for i in range(GB):
                    if i + 1 < GB:
                        augment_q(p, it, i + 1)
                    if i + 2 < GB:
                        take_max(p, it, i + 2)
                    norm(p, it, i)
                    prepare_next(p, it, i)

            def small(p, it):
                if p == "L1x":
                    dve.wait_ge(mask_ready.sem, mask_ready.at(p, it))
                    dve.tensor_reduce(FULL[:, 0, :], MKB[:], AX_X, ALU.min)
                    dve.drain()
                    dve.tensor_scalar(FULL[:, 1, :], FULL[:, 0, :], -1.0, 1.0, ALU.mult, ALU.add)

                def values():
                    dve.wait_ge(v_psum.sem, v_psum.at(p, it))
                    dst = VE[:, :, :, 0:HD]
                    src = PS[0].rearrange("p (b h d) -> p b h d", b=GB, h=H)
                    if p == "L0a":
                        ins = dve.tensor_copy(dst, src)
                    elif p == "L0x":
                        ins = dve.tensor_scalar(dst, src, 0.0, None, ALU.max)
                    else:
                        for i in range(GB):
                            ins = dve.tensor_tensor(dst[:, i], src[:, i], row(f"{p}.bv").rearrange("p (h d) -> p h d", h=H), ALU.add)
                    ins.then_inc(v_ready.sem, 1)

                if p in CROSS:
                    values()
                for g in range(HG):
                    dve.wait_ge(q_psum.sem, q_psum.at(p, it, g))
                    dve.tensor_scalar(QT[:, g, :], PS[4 + g], col(f"{p}.bq", g), 0.0 if p == "L0x" else None, ALU.add,
                                      ALU.max if p == "L0x" else ALU.bypass).then_inc(q_ready.sem, 1)
                if p not in CROSS:
                    values()
                if p == "L0a":
                    dve.drain()
                    r = strip_of(3)
                    dve.tensor_copy(KD.rearrange("p (i g) j t -> p i g j t", g=HG)[r, :, :, 3, :],
                                    QT[r].rearrange("p g (i t) -> p i g t", i=GB)).then_inc(qd_ready.sem, 1)
                    for c in range(1, 16, 2):
                        dve.wait_ge(pos_psum.sem, pos_psum.at(p, it, c))
                        dve.tensor_copy(POS.rearrange("p u j s -> p (u j) s")[:, :, 8 * c:8 * c + 8], PS[2].rearrange("p (s u) -> p u s", u=64)
                                        ).then_inc(pos_odd.sem, 1)
                attend(p, it, normalise)
                if p == "L0x":
                    dve.drain()
                    add_to_x(p, it, ON[:])
                else:
                    dve.wait_ge(y_psum.sem, y_psum.at(p, it))
                    add_to_x(p, it, tile(PS[0]), None if p == "L0a" else row(f"{p}.bo"))

            def residual(p, it, bias):
                dve.drain()
                dve.tensor_tensor(tile(RES[:]), XN[:], mid(bias), ALU.add)

            def l1_attention(p, it):
                residual(p, it, row("L1a.bo"))
                for c in range(8):
                    dve.wait_ge(q_psum.sem, q_psum.at(p, it, c))
                    dve.tensor_scalar(Q1[:, c, :], PS[c % 4], col("L1a.bq", c), None, ALU.add).then_inc(q_ready.sem, 1)
                for c in range(8):
                    dve.wait_ge(v_psum.sem, v_psum.at(p, it, c))
                    i, h8 = c // 2, 8 * (c % 2)
                    dve.tensor_tensor(V1[:, i, h8:h8 + 8, 0:64], PS[c % 4].rearrange("p (h d) -> p h d", h=8),
                                      row("L1a.bv")[:, h8 * 64:h8 * 64 + 512].rearrange("p (h d) -> p h d", h=8),
                                      ALU.add).then_inc(v_ready.sem, 1)

                def norm(i, g):
                    u = i * HG + g
                    dve.wait_ge(pv_done.sem, pv_done.at(p, it, u))
                    o = PS[6 + u % 2][:, 0:260].rearrange("p (h d) -> p h d", h=4)
                    dve.reciprocal(RD[:, 4 * g:4 * g + 4], o[:, :, 64])
                    dve.drain()
                    if g == 0 and i:
                        dve.wait_ge(ot_psum.sem, ot_psum.at(p, it, 2 * i - 1))
                    dve.tensor_tensor(ON1[:, g * 256:(g + 1) * 256].rearrange("p (h d) -> p h d", h=4), o[:, :, 0:64],
                                      last(RD[:, 4 * g:4 * g + 4], 64), ALU.mult).then_inc(on_ready.sem, 1)
                    if g == 1 and i:
                        take_y(i - 1)

                def take_y(i):
                    dve.wait_ge(y_psum.sem, y_psum.at(p, it, i))
                    dve.tensor_tensor(TMP[:, tok(i)], PS[0][:, 0:P], RES[:, tok(i)], ALU.add).then_inc(y_taken.sem, 1)

                attend_by_unit(p, it, norm)
                take_y(GB - 1)
                post_norm(p, it, 1e-3)

            def post_norm(p, it, eps):
                dve.drain()
                moments(lambda i: TMP[:, tok(i)], MV2)
                dve.tensor_scalar(VEPS[:, 1, :], MV2[:, :, 1], eps, None, ALU.add).then_inc(stats_ready.sem, 1)
                dve.wait_ge(rstd_ready.sem, rstd_ready.at(p, it))
                for i in range(GB):
                    dve.tensor_scalar(TMP2[:, tok(i)], TMP[:, tok(i)], MV2[:, i, 0:1], RSTD[:, 1, i:i + 1], ALU.subtract, ALU.mult)
                dve.drain()
                dve.tensor_tensor(tile(TMP2[:]), tile(TMP2[:]), mid(row(f"{p}.gamma")), ALU.mult)
                dve.drain()
                add_to_x(p, it, tile(TMP2[:]), row(f"{p}.beta"))

            def quantise(src, dst, magnitudes, scale, n):
                dve.tensor_reduce(magnitudes, src, AX_X, ALU.max)
                dve.tensor_reduce(scale, src, AX_X, ALU.min)
                dve.drain()
                dve.scalar_tensor_tensor(magnitudes, scale, -1.0, magnitudes, ALU.mult, ALU.max)
                dve.drain()
                dve.tensor_scalar(magnitudes, magnitudes, 1e-5, None, ALU.max)
                dve.drain()
                dve.reciprocal(scale, magnitudes)
                dve.drain()
                dve.tensor_scalar(scale, scale, 127.0, None, ALU.mult)
                dve.drain()
                for i in range(n):
                    dve.tensor_scalar(dst[:, i, :], src[:, i, :], scale[:, i:i + 1], ROUND, ALU.mult, ALU.add)
                dve.drain()
                return dve.tensor_scalar(dst, dst, ROUND, 127.0, ALU.subtract, ALU.min)

            def quantise_weights(p, value):
                dve.wait_ge(loaded[W_PHASE.index(p)], 16)
                names = ("gate", "up", "down") if p == "L0f" else ("w1", "w1", "w2")
                for m, n in enumerate(names):
                    dve.scalar_tensor_tensor(WTMP[:, m, :], w(f"{p}.{n}"), -1.0, w(f"{p}.{n}"), ALU.mult, ALU.max)
                dve.drain()
                dve.tensor_reduce(WSC[:, 0, :], WTMP, AX_X, ALU.add).then_inc(wsum_ready, 1)
                dve.wait_ge(wsum_psum, value)
                dve.tensor_scalar(WSC[:, 1, :], PS[0][:, 0:3], 1.0 / (P * INNER), 1e-5, ALU.mult, ALU.max)
                dve.drain()
                dve.reciprocal(WSC[:, 2, :], WSC[:, 1, :])
                dve.drain()
                for m, n in enumerate(names):
                    dve.tensor_scalar(WTMP[:, m, :], w(f"{p}.{n}"), WSC[:, 2, m:m + 1], ROUND, ALU.mult, ALU.add)
                dve.drain()
                dve.tensor_scalar(WTMP, WTMP, ROUND, 1.0, ALU.subtract, ALU.min)
                dve.drain()
                dve.tensor_scalar(WQ, WTMP, -1.0, None, ALU.max).then_inc(wq_ready, 1)
                dve.drain()

            def bit_ffn(p, it):
                if p == "L1f":
                    dve.drain()
                    mean_square(p, it, 0, XN[:], TMP, GB, P)
                    for i in range(GB):
                        dve.tensor_scalar(XN[:, i, :], XN[:, i, :], RSTD[:, 1, i:i + 1], None, ALU.mult)
                dve.drain()
                quantise(XN[:], XN[:], AM[:, 0, :], QS[:, 0, :], GB).then_inc(xq_ready.sem, 1)
                for m in range(2):
                    ins = dve.tensor_scalar(DQ[:, m, :], AM[:, 0, :], WSC[:, 1, m:m + 1], 1.0 / 127.0, ALU.mult, ALU.mult)
                if p == "L0f":
                    ins.then_inc(dq_ready.sem, 1)
                dve.drain()
                next_moments(p, it)

                for i in range(GB):
                    if i == 1:
                        next_normed(p, it)
                    hid = HID[:, i % 2, :]
                    if p == "L0f":
                        dve.wait_ge(act_ready.sem, act_ready.at(p, it, i))
                        dve.scalar_tensor_tensor(hid, PS[2 * (i % 2) + 1], DQ[:, 1, i:i + 1], hid, ALU.mult, ALU.mult)
                    else:
                        dve.wait_ge(h_psum.sem, h_psum.at(p, it, i))
                        dve.scalar_tensor_tensor(PRE[:, i % 2, :], PS[2 * (i % 2)], DQ[:, 0, i:i + 1], row("L1f.b1"),
                                                 ALU.mult, ALU.add).then_inc(pre_ready.sem, 1)
                        dve.wait_ge(act_ready.sem, act_ready.at(p, it, i))
                        mean_square(p, it, 1 + i, HID[:, i % 2:i % 2 + 1, :], PRE[:, i % 2, :], 1, INNER)
                        dve.tensor_scalar(hid, hid, RSTD[:, 1, 0:1], None, ALU.mult)
                    dve.drain()
                    if i >= 2:
                        dve.wait_ge(hqt_psum.sem, hqt_psum.at(p, it, i - 2))
                    quantise(HID[:, i % 2:i % 2 + 1, :], HQ[:, i % 2:i % 2 + 1, :], AM[:, 1, i:i + 1], QS[:, 1, i:i + 1], 1
                             ).then_inc(hq_ready.sem, 1)
                dve.drain()
                dve.tensor_scalar(DQ[:, 2, :], AM[:, 1, :], WSC[:, 1, 2:3], 1.0 / 127.0, ALU.mult, ALU.mult)
                dve.drain()
                dve.wait_ge(y_psum.sem, y_psum.at(p, it))
                for i in range(GB):
                    if p == "L0f":
                        ins = dve.scalar_tensor_tensor(seq(it, i), PS[6][:, tok(i)], DQ[:, 2, i:i + 1], seq(it, i), ALU.mult, ALU.add)
                    else:
                        dve.scalar_tensor_tensor(TMP[:, tok(i)], PS[6][:, tok(i)], DQ[:, 2, i:i + 1], row("L1f.b2"), ALU.mult, ALU.add)
                if p == "L0f":
                    ins.then_inc(x_updated.sem, 1)
                    dve.drain()
                else:
                    dve.drain()
                    add_to_x(p, it, tile(TMP[:]))

            def mean_square(p, it, k, src, work, n, width):
                sq = tile(work[:], n) if n > 1 else work.unsqueeze(1)
                dve.tensor_tensor(sq, src, src, ALU.mult)
                dve.drain()
                dve.tensor_reduce(VEPS[:, 1, 0:n], sq, AX_X, ALU.add)
                dve.drain()
                dve.tensor_scalar(VEPS[:, 1, 0:n], VEPS[:, 1, 0:n], 1.0 / width, 1e-6, ALU.mult, ALU.add).then_inc(stats_ready.sem, 1)
                dve.wait_ge(rstd_ready.sem, rstd_ready.at(p, it, k))

            def linear_attention(p, it):
                next_moments(p, it)
                dve.wait_ge(proj_psum.sem, proj_psum.at(p, it))
                cos = mid(const("cos"), 2 * GB)
                sin = mid(const("sin"), 2 * GB)
                for n, dst in ((0, QT), (4, KT)):
                    pair = lambda lo: PSA[:, lo:lo + 2, :].rearrange("p g (b t) -> p (g b) t", b=GB)
                    d = dst[:, 0:2, :].rearrange("p g (b t) -> p (g b) t", b=GB)
                    e = dst[:, 2:4, :].rearrange("p g (b t) -> p (g b) t", b=GB)
                    dve.tensor_tensor(d, pair(n), cos, ALU.mult)
                    dve.tensor_tensor(e, pair(n + 2), sin, ALU.mult)
                    dve.drain()
                    ins = dve.tensor_tensor(d, d, e, ALU.add)
                ins.then_inc(proj_ready.sem, 1)
                next_normed(p, it)
                dve.wait_ge(gates_psum.sem, gates_psum.at(p, it))
                dve.tensor_tensor(tile(SG[:, 0, :]), tile(PS[1][:, 0:64]), mid(row("L2a.gates")), ALU.add).then_inc(gates_biased.sem, 1)
                dve.wait_ge(gates_exp.sem, gates_exp.at(p, it))
                dve.tensor_scalar(SG[:, 1, :], SG[:, 1, :], 1.0, None, ALU.add)
                dve.drain()
                dve.reciprocal(SG[:, 6, :], SG[:, 1, :])
                dve.drain()
                sig = tile(SG[:, 6, :])
                dve.tensor_scalar(tile(SG[:, 2, 0:32]), sig[:, :, 0:8], 0.999 - 0.85, 0.85, ALU.mult, ALU.add).then_inc(beta_ready.sem, 1)
                dve.wait_ge(decay_ready.sem, decay_ready.at(p, it))
                dve.tensor_tensor(tile(SG[:, 7, 0:32]), tile(SG[:, 5, 0:32]), sig[:, :, 8:16], ALU.mult)
                dve.drain()
                heads = lambda ap: ap.rearrange("p (u d) -> p u d", u=32)
                dve.tensor_tensor(heads(VE16.rearrange("p b d -> p (b d)")), heads(PS[0]), last(SG[:, 7, 0:32], 16),
                                  ALU.mult).then_inc(vp_ready.sem, 1)
                def norm(i):
                    dve.wait_ge(pv_done.sem, pv_done.at(p, it, 2 * i + 1))
                    dve.tensor_tensor(ON[:, i, :].rearrange("p (h d) -> p h d", h=8),
                                      PS[5 + i % 2][:, 0:P].rearrange("p (h d) -> p h d", h=8),
                                      last(SG[:, 4, 8 * i:8 * i + 8], 16), ALU.mult).then_inc(on_ready.sem, 1)

                for u in range(8):
                    dve.wait_ge(s2_psum.sem, s2_psum.at(p, it, u))
                    if u >= 2:
                        dve.wait_ge(pv_done.sem, pv_done.at(p, it, u - 2))
                    dve.tensor_tensor(tile(PR[:, u % 2, :]), tile(PS[3 + u % 2]), mid(const("tri")), ALU.mult).then_inc(p_ready.sem, 1)
                    if u >= 3 and u % 2:
                        norm(u // 2 - 1)
                norm(GB - 1)
                dve.wait_ge(y_psum.sem, y_psum.at(p, it))
                add_to_x(p, it, tile(PS[0]), row("L2a.bo"))

            def experts(p, it):
                next_moments(p, it)
                dve.wait_ge(act_ready.sem, act_ready.at(p, it, 1))
                dve.tensor_tensor(HIDT[:, 0:2, :], HIDT[:, 0:2, :], PSA[:, 2:4, :], ALU.mult).then_inc(shared_ready.sem, 1)
                dve.wait_ge(act_ready.sem, act_ready.at(p, it, 2))
                v = lambda k: tile(SG[:, k, 0:32])
                s, sel, pick, a, b, rank = v(0), v(1), v(2), v(3), v(4), mid(row("rank"))
                small_ = lambda k: SG[:, 5, k * GB:(k + 1) * GB]
                dve.tensor_tensor(sel, s, mid(row("L2f.bias")), ALU.add)
                dve.drain()
                for n in range(2):
                    dve.tensor_reduce(small_(0), sel, AX_X, ALU.max)
                    dve.drain()
                    dve.tensor_tensor(a, sel, last(small_(0), 8), ALU.is_equal)
                    dve.drain()
                    dve.tensor_tensor(a, a, rank, ALU.mult)
                    dve.drain()
                    dve.tensor_reduce(small_(1), a, AX_X, ALU.max)
                    dve.drain()
                    dve.tensor_tensor(a, a, last(small_(1), 8), ALU.is_equal)
                    dve.drain()
                    if n == 0:
                        dve.tensor_copy(pick, a)
                        dve.scalar_tensor_tensor(sel, a, -1e30, sel, ALU.mult, ALU.add)
                    else:
                        dve.tensor_tensor(pick, pick, a, ALU.add)
                    dve.drain()
                dve.tensor_tensor(a, pick, s, ALU.mult)
                dve.drain()
                dve.tensor_reduce(small_(0), a, AX_X, ALU.add)
                dve.drain()
                dve.tensor_scalar(small_(1), small_(0), 1e-9, None, ALU.add)
                dve.tensor_scalar(small_(2), small_(0), 1e-9, None, ALU.is_gt)
                dve.drain()
                dve.reciprocal(small_(1), small_(1))
                dve.tensor_scalar(small_(3), small_(2), -0.5, 0.5, ALU.mult, ALU.add)
                dve.drain()
                dve.tensor_tensor(small_(1), small_(1), small_(2), ALU.mult)
                dve.tensor_tensor(b, pick, last(small_(3), 8), ALU.mult)
                dve.drain()
                dve.tensor_tensor(a, a, last(small_(1), 8), ALU.mult)
                dve.drain()
                dve.tensor_tensor(a, a, b, ALU.add)
                next_normed(p, it)
                dve.wait_ge(shared_psum.sem, shared_psum.at(p, it))
                dve.tensor_copy(ACC, tile(PS[7]))
                dve.drain()
                for e in range(8):
                    dve.wait_ge(expert_psum.sem, expert_psum.at(p, it, e))
                    for i in range(GB):
                        ins = dve.scalar_tensor_tensor(ACC[:, i, :], PS[2 + e % 2][:, tok(i)], SG[:, 3, 8 * i + e:8 * i + e + 1],
                                                       ACC[:, i, :], ALU.mult, ALU.add)
                    ins.then_inc(expert_used.sem, 1)
                    dve.drain()
                dve.wait_ge(y_psum.sem, y_psum.at(p, it))
                add_to_x(p, it, ACC)

            def delta_project(p, it):
                next_moments(p, it)
                dve.wait_ge(proj_psum.sem, proj_psum.at(p, it))
                for m, n in enumerate("qkv"):
                    dve.tensor_scalar(XP[:, m, :, 3:3 + P], tile(PS[m]), col(f"L3a.b{n}"), None, ALU.add)
                dve.drain()
                dve.wait_ge(stored.sem, stored.at(p, it - 1, 79))
                for tap in range(4):
                    for m, n in enumerate("qkv"):
                        c = tile(CV[:, m, :])
                        src = XP[:, m, :, tap:tap + P]
                        if tap == 0:
                            ins = dve.tensor_scalar(c, src, col(f"L3a.conv{n}", tap), None, ALU.mult)
                        else:
                            ins = dve.scalar_tensor_tensor(c, src, col(f"L3a.conv{n}", tap), c, ALU.mult, ALU.add)
                    if tap < 3:
                        dve.drain()
                ins.then_inc(conv_ready.sem, 1)
                next_normed(p, it)
                dve.wait_ge(silu_ready.sem, silu_ready.at(p, it))
                dve.tensor_tensor(TMP[:], CV[:, 0, :], CV[:, 0, :], ALU.mult)
                dve.tensor_tensor(TMP2[:], CV[:, 1, :], CV[:, 1, :], ALU.mult).then_inc(square_ready.sem, 1)
                dve.wait_ge(norm_ready.sem, norm_ready.at(p, it))
                for t in (TMP, TMP2):
                    dve.tensor_scalar(t[:], t[:], 1e-6, None, ALU.add)
                dve.drain()
                for t in (TMP, TMP2):
                    dve.reciprocal(t[:], t[:])
                dve.drain()
                dve.tensor_tensor(CV[:, 0, :], CV[:, 0, :], TMP[:], ALU.mult)
                dve.tensor_tensor(CV[:, 1, :], CV[:, 1, :], TMP2[:], ALU.mult).then_inc(store_ready.sem, 1)

            def scan():
                dve.wait_ge(scan_loaded, 80)
                dve.tensor_tensor(SAB, SA, SBT, ALU.mult)
                for h in range(2):
                    dve.tensor_tensor(SV[:, 8 * h:8 * h + 8, :], SV[:, 8 * h:8 * h + 8, :], mid(SBT[:, h, :], 8), ALU.mult)
                dve.memset(HIST[:, 0], 0.0)
                dve.drain()
                for h in range(2):
                    dve.scalar_tensor_tensor(SKK[:, 8 * h:8 * h + 8, :], SK[:, 8 * h:8 * h + 8, :], -1.0, mid(SAB[:, h, :], 8),
                                             ALU.mult, ALU.mult)
                dve.drain()
                with dve.Fori(0, P // CHUNK) as it:
                    chunk = lambda ap: ap[:, :, bass.ds(it * CHUNK, CHUNK)].rearrange("p f t -> p t f")
                    dve.tensor_copy(SP9[:, :, :, HD], chunk(SV))
                    dve.tensor_copy(CK[:, 0], chunk(SK))
                    dve.tensor_copy(CK[:, 1], chunk(SKK))
                    dve.tensor_copy(CA, chunk(SA))
                    dve.drain()
                    for n in range(CHUNK):
                        heads = lambda ap: ap.rearrange("p (h d) e -> p h d e", h=2)
                        key = lambda m: CK[:, m, n].rearrange("p (h e) -> p h e", h=2).unsqueeze(2).to_broadcast([P, 2, 8, 8])
                        now, new = HIST[:, n], HIST[:, n + 1]
                        if n:
                            dve.wait_ge(scan_step.sem, scan_step.at("scan", it, 5 * n - 1))
                        dve.tensor_tensor(heads(SP9[:, n, :, 0:HD]), heads(now), key(1), ALU.mult).then_inc(scan_step.sem, 1)
                        dve.tensor_tensor(new.rearrange("p (h d) e -> p h (d e)", h=2), now.rearrange("p (h d) e -> p h (d e)", h=2),
                                          last(CA[:, n], 64), ALU.mult).then_inc(scan_step.sem, 1)
                        dve.wait_ge(scan_step.sem, scan_step.at("scan", it, 5 * n))
                        dve.tensor_reduce(SU, SP9[:, n], AX_X, ALU.add).then_inc(scan_step.sem, 1)
                        dve.wait_ge(scan_step.sem, scan_step.at("scan", it, 5 * n + 2))
                        dve.tensor_tensor(heads(ST2), last(SU.rearrange("p (h d) -> p h d", h=2), HD), key(0), ALU.mult
                                          ).then_inc(scan_step.sem, 1)
                        dve.wait_ge(scan_step.sem, scan_step.at("scan", it, 5 * n + 3))
                        dve.tensor_tensor(new, new, ST2, ALU.add).then_inc(scan_step.sem, 1)
                    dve.drain()
                    span = bass.ds(it * CHUNK, CHUNK)
                    for h in range(2):
                        f = slice(8 * h, 8 * h + 8)
                        prod = PROD[:, h * 1024:(h + 1) * 1024].rearrange("p (t d e) -> p t d e", t=CHUNK, d=8)
                        q = SQ[:, f, span].rearrange("p e t -> p t e").unsqueeze(2).to_broadcast([P, CHUNK, 8, 8])
                        dve.tensor_tensor(prod, HIST[:, 1:CHUNK + 1, f, :], q, ALU.mult)
                    dve.tensor_copy(HIST[:, 0], HIST[:, CHUNK])
                    dve.drain()
                    for h in range(2):
                        f = slice(8 * h, 8 * h + 8)
                        prod = PROD[:, h * 1024:(h + 1) * 1024].rearrange("p (t d e) -> p t d e", t=CHUNK, d=8)
                        dve.tensor_reduce(SO[:, f, span].rearrange("p d t -> p t d"), prod, AX_X, ALU.add)
                    dve.drain()
                both = SO.rearrange("p (h d) t -> p h (d t)", h=2)
                dve.tensor_reduce(RD[:, 0:2], both, AX_X, ALU.add)
                dve.tensor_tensor(PROD, SO.rearrange("p f t -> p (f t)"), SO.rearrange("p f t -> p (f t)"), ALU.mult)
                dve.drain()
                dve.tensor_reduce(RD[:, 2:4], tile(PROD, 2), AX_X, ALU.add)
                dve.tensor_scalar(RD[:, 0:2], RD[:, 0:2], 1.0 / (P * HD), None, ALU.mult)
                dve.drain()
                dve.tensor_tensor(RD[:, 4:6], RD[:, 0:2], RD[:, 0:2], ALU.mult)
                dve.tensor_scalar(RD[:, 2:4], RD[:, 2:4], 1.0 / (P * HD), 1e-5, ALU.mult, ALU.add)
                dve.drain()
                dve.tensor_tensor(RD[:, 6:8], RD[:, 2:4], RD[:, 4:6], ALU.subtract).then_inc(gn_var, 1)
                dve.wait_ge(gn_rstd, 1)
                for h in range(2):
                    ins = dve.tensor_scalar(both[:, h], both[:, h], RD[:, h:h + 1], RD[:, 8 + h:9 + h], ALU.subtract, ALU.mult)
                ins.then_inc(scan_done, 1)

            def delta_out(p, it):
                dve.wait_ge(y_loaded.sem, y_loaded.at(p, it, 15))
                dve.tensor_scalar(TMP[:], YT, col("L3a.scale"), col("L3a.bias"), ALU.mult, ALU.add)
                dve.drain()
                dve.tensor_tensor(TMP2[:], TMP[:], GT[:, bass.ds(it * T, T)], ALU.mult).then_inc(gated.sem, 1)
                dve.wait_ge(y_psum.sem, y_psum.at(p, it))
                add_to_x(p, it, tile(PS[1]), row("L3a.bo"))

            def one_head(p, it):
                next_moments(p, it)
                dve.wait_ge(proj_psum.sem, proj_psum.at(p, it))
                dve.tensor_tensor(ON[:], tile(PS[2]), mid(row("L3x.bv")), ALU.add).then_inc(proj_ready.sem, 1)
                next_normed(p, it)
                dve.wait_ge(s3_psum.sem, s3_psum.at(p, it))
                s = tile(TMP[:])
                dve.scalar_tensor_tensor(s, tile(PS[3]), float(P // 16) ** -0.5, mid(KEEP[:, 0, :]), ALU.mult, ALU.mult)
                dve.drain()
                dve.tensor_tensor(s, s, mid(KEEP[:, 1, :]), ALU.add)
                dve.drain()
                dve.tensor_reduce(MX[:, 0:GB], s, AX_X, ALU.max)
                dve.drain()
                dve.tensor_tensor(s, s, last(MX[:, 0:GB], P), ALU.subtract).then_inc(s3_shifted.sem, 1)
                dve.wait_ge(p3_ready.sem, p3_ready.at(p, it))
                dve.tensor_reduce(RD[:, 0:GB], tile(PR[:, 0, :]), AX_X, ALU.add)
                dve.drain()
                dve.reciprocal(RD[:, GB:2 * GB], RD[:, 0:GB])
                dve.drain()
                dve.wait_ge(y_psum.sem, y_psum.at(p, it))
                for i in range(GB):
                    dve.scalar_tensor_tensor(TMP[:, tok(i)], PS[0][:, tok(i)], RD[:, GB + i:GB + i + 1], row("L3x.bo"),
                                             ALU.mult, ALU.add)
                dve.drain()
                add_to_x(p, it, tile(TMP[:]))

            def relu_ffn(p, it):
                residual(p, it, row("L3f.b2"))
                next_moments(p, it)
                next_normed(p, it)
                dve.wait_ge(y_psum.sem, y_psum.at(p, it))
                dve.tensor_tensor(TMP[:], PS[4], RES[:], ALU.add)
                post_norm(p, it, 1e-5)

            bodies = {**each(SMALL, small), "L1a": l1_attention, "L0f": bit_ffn, "L1f": bit_ffn, "L2a": linear_attention,
                      "L2f": experts, "L3a": delta_project, "L3o": delta_out, "L3x": one_head, "L3f": relu_ffn}
            for n, p in enumerate(run):
                if p == "scan":
                    scan()
                    continue
                if p in ("L0f", "L1f"):
                    quantise_weights(p, quantised.index(p) + 1)
                if p == "L1a":
                    dve.nop().then_inc(y_taken.sem, 1)
                if p == "L3a":
                    dve.memset(XP[:, :, :, 0:3], 0.0).then_inc(stored.sem, 1)
                if p == "L3x":
                    dve.wait_ge(masks_loaded, 16 * (1 + ("L1x" in run)))
                    dve.tensor_copy(KEEP[:, 1, :], MASK3[:])
                    dve.drain()
                    dve.tensor_scalar(KEEP[:, 0, :], KEEP[:, 1, :], 0.0, None, ALU.not_equal)
                    dve.drain()
                    dve.tensor_scalar(KEEP[:, 1, :], KEEP[:, 0, :], -NEG, NEG, ALU.mult, ALU.add)
                    dve.drain()
                if p in before_loop:
                    next_moments(p, BEFORE_LOOP)
                    next_normed(p, BEFORE_LOOP)
                with dve.Fori(0, GROUPS) as it:
                    bodies[p](p, it)


def strips(a, heads=16, width=HD):
    a = a.reshape(*a.shape[:-1], heads, width)
    out = np.zeros((*a.shape[:-1], STRIP), a.dtype)
    out[..., :width] = a
    return out.reshape(*a.shape[:-2], heads * STRIP)


def chunks(a):
    n = a.shape[0] // P
    return a.reshape(n, P, a.shape[1]).transpose(1, 0, 2).reshape(P, -1)


def neighbours(a):
    return a.reshape(a.shape[0], -1, 2)[:, :, ::-1].reshape(a.shape)


def tables():
    k = np.zeros((P, K_ALL), np.float32)

    def put(name, a):
        k[:, K_AT[name][0]:K_AT[name][0] + P] = a

    put("ident", np.eye(P))
    put("tri", np.triu(np.ones((P, P))))
    half = 8
    inv = (1.0 / 10000.0 ** (np.arange(half, dtype=np.float32) / np.float32(half))).astype(np.float32)
    freqs = (np.arange(P, dtype=np.float32)[:, None] * inv[None, :]).astype(np.float32)
    cos, sin = np.zeros((P, P), np.float32), np.zeros((P, P), np.float32)
    for r in range(P):
        d = r % STRIP
        if d < 16:
            cos[r] = np.cos(freqs[:, d // 2])
            sin[r] = np.sin(freqs[:, d // 2]) * (-1.0 if d % 2 == 0 else 1.0)
    put("cos", cos)
    put("sin", sin)
    for j in range(4):
        k[STRIP * j + PAD_ROW, K_AT["sel"][0] + j * P:K_AT["sel"][0] + (j + 1) * P] = 1.0
    put("heads", np.kron(np.eye(H), np.ones((HD, HD))))
    return k


def lay_out(inp):
    a = {k: np.asarray(v) for k, v in inp.items()}
    parts = {}
    for p, t in (("L0a", "L0_attn"), ("L0x", "L0_xattn"), ("L1x", "L1_xattn")):
        parts[f"{p}.q"] = strips(a[f"{t}_Wq"].T)
        parts[f"{p}.k"] = strips(a[f"{t}_Wk"].T)
        parts[f"{p}.v"] = a[f"{t}_Wv"].T
    parts["L0a.o"] = a["L0_attn_Wp"].T
    table = np.zeros((4, STRIP, 2 * P), np.float32)
    table[:, :HD, :] = a["L0_attn_pos_emb_k"][(np.arange(2 * P) - (P - 1)) % (2 * P)].T
    parts["L0a.pe"] = table.reshape(P, 2 * P)
    parts["L0f.gate"], parts["L0f.up"] = a["L0_ffn_w_gate"].T, a["L0_ffn_w_up"].T
    parts["L0f.down"] = chunks(a["L0_ffn_w_down"].T)
    for n in "qkv":
        parts[f"L1a.{n}"] = a[f"L1_attn_W{n}"].reshape(P, 1024)
    parts["L1a.o"] = chunks(a["L1_attn_Wo"].reshape(1024, P))
    parts["L1x.o"] = a["L1_xattn_Wo"].T
    parts["L1f.w1"], parts["L1f.w2"] = a["L1_ffn_w1"].T, chunks(a["L1_ffn_w2"].T)
    for n in "qk":
        t = a[f"L2_attn_W{n}"].T
        parts[f"L2a.{n}"], parts[f"L2a.{n}s"] = strips(t, 8, 16), strips(neighbours(t), 8, 16)
        parts[f"L2x.{n}"] = strips(a[f"L2_xattn_W{n}"])
    parts["L2a.v"], parts["L2a.o"] = a["L2_attn_Wv"].T, a["L2_attn_Wo"].T
    parts["L2a.gates"] = np.concatenate([a["L2_attn_Wbeta"].T, a["L2_attn_Walpha"].T], 1)
    parts["L2x.v"], parts["L2x.o"] = a["L2_xattn_Wv"], a["L2_xattn_Wo"]
    parts["L2f.sw1"], parts["L2f.sw3"], parts["L2f.sw2"] = a["L2_ffn_sw1"], a["L2_ffn_sw3"], chunks(a["L2_ffn_sw2"])
    parts["L2f.router"] = a["L2_ffn_router_w"].T
    for n in ("ew1", "ew2"):
        parts[f"L2f.{n}"] = a[f"L2_ffn_{n}"].transpose(1, 0, 2).reshape(P, -1)
    for n in "qkvgabo":
        parts[f"L3a.{n}"] = a[f"L3_attn_W{n}"]
    for n in "qkvo":
        parts[f"L3x.{n}"] = a[f"L3_xattn_W{n}"]
    parts["L3f.w1"], parts["L3f.w2"] = a["L3_ffn_w1"][0], chunks(a["L3_ffn_w2"][0])
    w = np.concatenate([parts[n] for n in W_AT], 1)

    c = {}
    spare = np.tile((np.arange(STRIP) == PAD_ROW).astype(np.float32), H)
    for p in SMALL:
        for n in "qk":
            b = strips(a[f"{p[:2]}_xattn_b{n}"]) if p in ("L1x", "L2x") else np.zeros(H * STRIP, np.float32)
            if n == "k":
                b = np.where(spare > 0, spare, b)
            c[f"{p}.b{n}"] = b.reshape(HG, P).T
    for n in "qk":
        c[f"L1a.b{n}"] = a[f"L1_attn_b{n}"].reshape(8, P).T
        c[f"L3x.b{n}"] = a[f"L3_xattn_b{n}"][:, None]
    for n in "qkvg":
        c[f"L3a.b{n}"] = a[f"L3_attn_b{n}"][:, None]
    c["L3a.scale"], c["L3a.bias"] = a["L3_attn_gn_scale"][:, None], a["L3_attn_gn_bias"][:, None]
    for n in "ab":
        c[f"L3a.b{n}"] = np.concatenate([a[f"L3_attn_b{n}"], np.zeros(P - H, np.float32)])[:, None]
    for n in "qkv":
        c[f"L3a.conv{n}"] = a[f"L3_attn_{n}_conv"]
    c["L3f.b1"] = a["L3_ffn_b1"][0].reshape(4, P).T
    cols = np.concatenate([c[n] for n in C_AT], 1)

    r = {"L1a.bv": a["L1_attn_bv"], "L2a.gates": np.concatenate([a["L2_attn_bbeta"], a["L2_attn_balpha"]]),
         "L2f.bias": a["L2_ffn_router_bias"], "L1f.b1": a["L1_ffn_b1"], "L1f.b2": a["L1_ffn_b2"],
         "L3f.b2": a["L3_ffn_b2"][0], "rank": np.arange(8, 0, -1, dtype=np.float32)}
    for p, t in (("L1a", "L1_attn"), ("L1x", "L1_xattn"), ("L2a", "L2_attn"), ("L2x", "L2_xattn"), ("L3a", "L3_attn"),
                 ("L3x", "L3_xattn"), ("L3f", "L3_ffn")):
        for n in ("bv", "bo", "gamma", "beta"):
            if f"{p}.{n}" in R_AT and f"{p}.{n}" not in r:
                r[f"{p}.{n}"] = a[f"{t}_{n}"]
    rows = np.concatenate([r[n].reshape(-1) for n in R_AT])[None, :]

    return {"x": a["x"], "ctx_t": a["ctx_1024"].transpose(2, 0, 1).reshape(P, B * P),
            "mask1": a["mask_Bx1xSxS2_bk1"], "mask3": a["mask_SxS2_ik0"],
            "w": w, "cols": cols, "rows": rows, "consts": tables()}


def build(nc, arrays, phases=PHASES):
    args = [nc.dram_tensor(f"in_{n}", a.shape, mybir.dt.from_np(a.dtype), kind="ExternalInput").ap() for n, a in arrays.items()]
    out = nc.dram_tensor("out", (B, P, P), F32, kind="ExternalOutput").ap()
    decoder(nc, *args, out, phases=phases)


def kernel(**inputs):
    import concourse.bacc as bacc
    from concourse.bass_utils import run_bass_kernel_spmd

    arrays = {n: np.ascontiguousarray(a) for n, a in lay_out(inputs).items()}
    nc = bacc.Bacc("TRN2", target_bir_lowering=False, num_devices=1)
    build(nc, arrays)
    r = run_bass_kernel_spmd(nc, [{f"in_{n}": a for n, a in arrays.items()}], core_ids=[0])
    return r.results[0]["out"]
```

```python
from contextlib import ExitStack

import numpy as np
import concourse.bass as bass
from concourse import mybir

F32 = mybir.dt.float32
BF16 = mybir.dt.bfloat16
I32 = mybir.dt.int32
U8 = mybir.dt.uint8
ALU = mybir.AluOpType
ACT = mybir.ActivationFunctionType
AX_X = mybir.AxisListType.X

P = 128
B = 16
GB = 4
GROUPS = B // GB
T = GB * P
H = 16
HD = 8
STRIP = 32
HG = 4
INNER = 512
ROUND = float(1.5 * 2 ** 23)
MASKED = float(-2 ** 30)
NEG = -1e9

SMALL = ("L0a", "L0x", "L1x", "L2x")
CROSS = ("L0x", "L1x", "L2x", "L3x")
PHASES = ("L0a", "L0x", "L0f", "L1a", "L1x", "L1f", "L2a", "L2x", "L2f", "L3a", "scan", "L3o", "L3x", "L3f")
BIT = ("L0f", "L1f")
BEFORE_LOOP = -1
XNT_BANK = {"L2f": 4, "L3a": 7, "L3x": 6, "L3f": 5}
K_BANK = (0, 3, 1, 2)
V_BANK = 4
Q_BANK = (7, 0, 3, 1)
UNITS = GB * 4
LN_PHASES = tuple(p for p in PHASES if p not in ("scan", "L3o"))
CHUNK = 16


def sections(parts):
    at, out = 0, {}
    for name, width in parts:
        out[name] = (at, width)
        at += width
    return out, at


W_PARTS = [
    ("L0a", [("q", 512), ("k", 512), ("v", 128), ("o", 128), ("pe", 256)]),
    ("L0x", [("q", 512), ("k", 512), ("v", 128)]),
    ("L0f", [("gate", 512), ("up", 512), ("down", 512)]),
    ("L1a", [("q", 1024), ("k", 1024), ("v", 1024), ("o", 1024)]),
    ("L1x", [("q", 512), ("k", 512), ("v", 128), ("o", 128)]),
    ("L1f", [("w1", 512), ("w2", 512)]),
    ("L2a", [("q", 256), ("qs", 256), ("k", 256), ("ks", 256), ("v", 128), ("gates", 16), ("o", 128)]),
    ("L2x", [("q", 512), ("k", 512), ("v", 128), ("o", 128)]),
    ("L2f", [("sw1", 256), ("sw3", 256), ("sw2", 256), ("router", 8), ("ew1", 1024), ("ew2", 1024)]),
    ("L3a", [("q", 128), ("k", 128), ("v", 128), ("g", 128), ("a", 16), ("b", 16), ("o", 128)]),
    ("L3x", [("q", 128), ("k", 128), ("v", 128), ("o", 128)]),
    ("L3f", [("w1", 512), ("w2", 512)]),
]
W_AT, W_ALL = sections([(f"{p}.{n}", w) for p, parts in W_PARTS for n, w in parts])
W_PHASE = [p for p, _ in W_PARTS]

C_AT, C_ALL = sections(
    [(f"{p}.{n}", HG) for p in SMALL for n in ("bq", "bk")]
    + [("L1a.bq", 8), ("L1a.bk", 8)]
    + [(f"L3a.{n}", 1) for n in ("bq", "bk", "bv", "bg", "scale", "bias", "ba", "bb")]
    + [(f"L3a.conv{n}", 4) for n in "qkv"]
    + [("L3x.bq", 1), ("L3x.bk", 1), ("L3f.b1", 4)])
R_AT, R_ALL = sections([
    ("L1a.bv", 1024), ("L1a.bo", 128), ("L1a.gamma", 128), ("L1a.beta", 128),
    ("L1x.bv", 128), ("L1x.bo", 128), ("L1f.b1", 512), ("L1f.b2", 128),
    ("L2a.gates", 16), ("L2a.bo", 128), ("L2x.bv", 128), ("L2x.bo", 128), ("L2f.bias", 8),
    ("L3a.bo", 128), ("L3x.bv", 128), ("L3x.bo", 128),
    ("L3f.b2", 128), ("L3f.gamma", 128), ("L3f.beta", 128), ("rank", 8)])
K_AT, K_ALL = sections([("ident", P), ("tri", P), ("cos", P), ("sin", P), ("heads", P)])


class Signal:

    def __init__(self, sem, per, phases, pre):
        self.sem, self.per, self.before = sem, per, {}
        total = 0
        for phase in phases:
            total += pre.get(phase, 0)
            self.before[phase] = total
            total += per.get(phase, 0) * passes(phase)

    def at(self, phase, it, k=0):
        return it * self.per[phase] + (self.before[phase] + k + 1)


def passes(phase):
    return P // CHUNK if phase == "scan" else GROUPS


def decoder(nc, x, ctx_t, mask1, mask3, w_all, cols, rows, consts, out, phases=PHASES):
    with ExitStack() as stack:
        def sb(name, shape, dt=F32):
            return stack.enter_context(nc.sbuf_tensor(name, shape, dt))

        def sem(name):
            return stack.enter_context(nc.semaphore(name))

        def signal(name, per, pre={}):
            return Signal(sem(name), per, phases, pre)

        def tile(ap, n=GB):
            return ap.rearrange("p (b d) -> p b d", b=n)

        X = sb("X", [P, B, P])
        W = sb("W", [P, W_ALL])
        COLS = sb("COLS", [P, C_ALL])
        ROWS = sb("ROWS", [P, R_ALL])
        K = sb("K", [P, K_ALL])
        XN = sb("XN", [P, GB, P])
        XNT = sb("XNT", [P, T])
        CTX = sb("CTX", [P, T])
        QK = sb("QK", [P, 2 * HG, T])
        QT = QK[:, 0:HG, :]
        KT = QK[:, HG:2 * HG, :]
        VE = sb("VE", [P, GB, H, HD + 1])
        PR = sb("PR", [P, 2, T])
        ON = sb("ON", [P, GB, P])
        OT = sb("OT", [P, T])
        TMP = sb("TMP", [P, T])
        TMP2 = sb("TMP2", [P, T])
        PQ = [TMP2[:], sb("PQ", [P, T])[:]]
        MX = sb("MX", [P, H])
        RD = sb("RD", [P, 64])
        OS = sb("OS", [P, 2, H, HD + 1])
        ST = sb("ST", [P, GB, 6])
        MV = sb("MV", [P, GB, 2])
        VEPS = sb("VEPS", [P, 2, GB])
        RSTD = sb("RSTD", [P, 2, GB])
        MV2 = sb("MV2", [P, GB, 2])
        RES = OT
        HALF = sb("HALF", [P, GB])
        ONES = sb("ONES", [P, P])
        I2 = sb("I2", [P, P])
        NEGI = sb("NEGI", [P, P], BF16)
        MKB = sb("MKB", [P, GB, P], BF16)
        FULL = sb("FULL", [P, 2, GB])
        MASK3 = sb("MASK3", [P, P], I32)
        KEEP = sb("KEEP", [P, 2, P])
        SS = sb("SS", [P, 2, GB])
        AM = sb("AM", [P, 2, GB])
        QS = sb("QS", [P, 2, GB])
        DQ = sb("DQ", [P, 4, GB])
        WSC = sb("WSC", [P, 3, 3])
        SG = sb("SG", [P, 8, GB * 16])
        BIG = sb("BIG", [P, 16384])
        KD = BIG[:, 0:8192].rearrange("p (u j t) -> p u j t", u=16, j=4)
        POS = BIG[:, 8192:16384].rearrange("p (u j s) -> p u j s", u=16, j=4)
        QB = W[:, W_AT["L1a.q"][0]:W_AT["L1a.q"][0] + 8192].rearrange("p (m r h) -> p m r h", m=32, r=4)
        Q1 = QK[:]
        K1 = BIG[:, 0:8192].rearrange("p (c b r t) -> p c b r t", c=8, b=GB, r=2)
        V1 = BIG[:, 8192:12352].rearrange("p (b h d) -> p b h d", b=GB, h=H)
        ON1 = BIG[:, 12352:13376]
        OT1 = BIG[:, 13376:14400].rearrange("p (c t) -> p c t", c=8)
        MASK1 = BIG[:, 8192:8704].bitcast(U8).rearrange("p (b k) -> p b k", b=B)
        WQ = BIG[:, 8192:8960].bitcast(BF16).rearrange("p (m n) -> p m n", m=3)
        XQT = BIG[:, 9216:9472].bitcast(BF16)
        HID = BIG[:, 10240:12288].rearrange("p (b n) -> p b n", b=GB)
        HQT = BIG[:, 12288:13312].bitcast(BF16).rearrange("p (b n) -> p b n", b=GB)
        WTMP = BIG[:, 13312:14848].rearrange("p (m n) -> p m n", m=3)
        HIDT = BIG[:, 0:2048].rearrange("p (c t) -> p c t", c=4)
        ACC = BIG[:, 2048:2560].rearrange("p (b d) -> p b d", b=GB)
        EXPH = BIG[:, 2560:4608].rearrange("p (c t) -> p c t", c=4)
        XP = BIG[:, 0:3 * GB * 131].rearrange("p (m b t) -> p m b t", m=3, b=GB)
        CV = BIG[:, 2048:3584].rearrange("p (m t) -> p m t", m=3)
        TAPS = BIG[:, 5120:6656].rearrange("p (m n t) -> p m n t", m=3, n=4)
        GT = QT.rearrange("p g t -> p (g t)")
        SQ = BIG[:, 0:2048].rearrange("p (f t) -> p f t", f=16)
        SK = BIG[:, 2048:4096].rearrange("p (f t) -> p f t", f=16)
        SV = BIG[:, 4096:6144].rearrange("p (f t) -> p f t", f=16)
        SO = BIG[:, 6144:8192].rearrange("p (f t) -> p f t", f=16)
        SA = BIG[:, 8192:8448].rearrange("p (h t) -> p h t", h=2)
        SBT = BIG[:, 8448:8704].rearrange("p (h t) -> p h t", h=2)
        SAB = BIG[:, 8704:8960].rearrange("p (h t) -> p h t", h=2)
        STATE = BIG[:, 8960:9216].rearrange("p (n f e) -> p n f e", n=2, f=16)
        SPQ = BIG[:, 9216:9344].rearrange("p (f e) -> p f e", f=16)
        OUTC = BIG[:, 9344:9600].rearrange("p (t f) -> p t f", t=CHUNK)
        PROD = BIG[:, 11136:13184]
        ST2 = BIG[:, 13312:13440].rearrange("p (f e) -> p f e", f=16)
        SU = BIG[:, 13440:13456]
        SKK = BIG[:, 14336:16384].rearrange("p (f t) -> p f t", f=16)
        SP9 = W[:, 0:CHUNK * 144].rearrange("p (t f e) -> p t f e", t=CHUNK, f=16)
        CK = W[:, 2304:3072].rearrange("p (m t f) -> p m t f", m=3, t=CHUNK)
        CA = W[:, 3072:3104].rearrange("p (t h) -> p t h", t=CHUNK)

        VE16 = tile(BIG[:, 8192:8704])
        NORM = SG[:, 0:2, :].rearrange("p a b -> p (a b)")
        YT = BIG[:, 0:2048]
        PSA = stack.enter_context(nc.psum_tensor("PSA", [P, 8, T], F32))
        PS = [PSA[:, n, :] for n in range(8)]

        scratch = {n: nc.dram_tensor(f"scratch_{n}", (B, P, P), F32, kind="Internal").ap() for n in "qkvo"}
        scratch.update({n: nc.dram_tensor(f"scratch_{n}", (B, H, P), F32, kind="Internal").ap() for n in "ab"})

        def w(name, lo=0, width=None):
            at, full = W_AT[name]
            return W[:, at + lo:at + lo + (full if width is None else width)]

        def col(name, k=0, parts=P):
            return COLS[0:parts, C_AT[name][0] + k:C_AT[name][0] + k + 1]

        def row(name):
            at, n = R_AT[name]
            return ROWS[:, at:at + n]

        def const(name):
            at, n = K_AT[name]
            return K[:, at:at + n]

        ident = const("ident")

        def seqs(it):
            return X[:, bass.ds(it * GB, GB), :]

        def seq(it, i):
            return X[:, bass.ds(it * GB + i, 1), :].rearrange("p a d -> p (a d)")

        def mid(ap, n=GB):
            return ap.unsqueeze(1).to_broadcast([ap.shape[0], n] + list(ap.shape[1:]))

        def last(ap, n):
            return ap.unsqueeze(len(ap.shape)).to_broadcast(list(ap.shape) + [n])

        def tok(i, n=P):
            return slice(i * n, (i + 1) * n)

        each = lambda names, n=1: {p: n for p in names}
        attention = (*SMALL, "L1a")
        loaded = [sem(f"weights_loaded_{p}") for p in W_PHASE]
        inputs_loaded = sem("inputs_loaded")
        rest_loaded = sem("rest_loaded")
        masks_loaded = sem("masks_loaded")
        setup_dve = sem("setup_dve")
        setup_pool = sem("setup_pool")
        kd_zero = sem("kd_zero")
        ctx_loaded = signal("ctx_loaded", each(CROSS, 16))
        before_loop = {p: 1 for p in ("L3x", phases[0]) if p in phases}
        before_loop_t = {p: 1 for p in ("L1a", "L2a", *before_loop) if p in phases and p not in BIT}
        ln_stats = signal("ln_stats", each(LN_PHASES), before_loop)
        ln_rstd = signal("ln_rstd", each(LN_PHASES), before_loop)
        xn_ready = signal("xn_ready", each(LN_PHASES), before_loop)
        xnt_psum = signal("xnt_psum", each([p for p in LN_PHASES if p not in BIT]), before_loop_t)
        xnt_ready = signal("xnt_ready", each([p for p in LN_PHASES if p not in BIT]), before_loop_t)
        xq_ready = signal("xq_ready", each(BIT))
        xqt_psum = signal("xqt_psum", each(BIT))
        xqt_ready = signal("xqt_ready", each(BIT))
        other_stats = {"L1a": 1, "L3f": 1, "L1f": 2}
        stats_ready = signal("stats_ready", other_stats)
        rstd_ready = signal("rstd_ready", other_stats)
        k_psum = signal("k_psum", {**each(SMALL, HG), "L1a": 8})
        q_psum = signal("q_psum", {**each(SMALL, HG), "L1a": 8})
        v_psum = signal("v_psum", {**each(SMALL), "L1a": 8})
        k_ready_dve = signal("k_ready_dve", each(("L0x", "L1x", "L2x"), HG))
        k_ready = signal("k_ready", {**each(SMALL, 3 * HG), "L0a": HG, "L1a": 16, "L2a": 4})
        q_ready = signal("q_ready", {**each(SMALL, HG), "L1a": 8})
        v_ready = signal("v_ready", {**each(SMALL), "L1a": 8})
        units = each(attention, GB * HG)
        units2 = {**units, "L2a": GB * 2}
        s1_psum = signal("s1_psum", units)
        max_taken = signal("max_taken", units)
        shifted = signal("shifted", units)
        exp_ready = signal("exp_ready", units)
        t_psum = signal("t_psum", units)
        s2_psum = signal("s2_psum", {"L2a": GB * 2})
        p_ready = signal("p_ready", units2)
        pv_done = signal("pv_done", units2)
        on_ready = signal("on_ready", {**each(SMALL, GB), "L1a": GB * HG, "L2a": GB})
        ot_psum = signal("ot_psum", {**each(("L0a", "L1x", "L2x", "L2a")), "L1a": 2 * GB})
        ot_ready = signal("ot_ready", {**each(("L0a", "L1x", "L2x", "L2a")), "L1a": 2 * GB})
        y_psum = signal("y_psum", {**each([p for p in PHASES if p not in ("scan", "L3a", "L0x")]), "L1a": GB})
        y_taken = signal("y_taken", {"L1a": GB}, {"L1a": 1})
        x_updated = signal("x_updated", each([p for p in PHASES if p not in ("scan", "L3a")]), {phases[0]: 1})
        pos_psum = signal("pos_psum", {"L0a": 16})
        pos_even = signal("pos_even_ready", {"L0a": 8})
        pos_odd = signal("pos_odd_ready", {"L0a": 8})
        kd_ready = signal("kd_ready", {"L0a": 4})
        qd_ready = signal("qd_ready", {"L0a": 4})
        mask_ready = signal("mask_ready", {"L1x": 1})
        wsum_ready = sem("wsum_ready")
        wsum_psum = sem("wsum_psum")
        wq_ready = sem("wq_ready")
        h_psum = signal("h_psum", {"L0f": GB, "L1f": GB, "L2f": 9, "L3f": 4})
        dq_ready = signal("dq_ready", each(("L0f",)))
        pre_ready = signal("pre_ready", {"L1f": GB})
        squares_ready = signal("squares_ready", {"L1f": 2})
        act_ready = signal("act_ready", {"L0f": GB, "L1f": GB, "L2f": 11, "L3f": 4})
        hq_ready = signal("hq_ready", each(("L0f", "L1f"), GB))
        hqt_psum = signal("hqt_psum", each(("L0f", "L1f"), GB))
        hqt_ready = signal("hqt_ready", each(("L0f", "L1f"), GB))
        shared_ready = signal("shared_ready", {"L2f": 1})
        shared_psum = signal("shared_psum", {"L2f": 1})
        shared_taken = signal("shared_taken", {"L2f": 1})
        expert_used = signal("expert_used", {"L2f": 8})
        expert_psum = signal("expert_psum", {"L2f": 8})
        proj_psum = signal("proj_psum", {"L2a": 2, "L3a": 2, "L3x": 1})
        proj_ready = signal("proj_ready", {"L2a": 2, "L3x": 1})
        kq_ready = signal("kq_ready", {"L3x": 1})
        gates_psum = signal("gates_psum", {"L2a": 1})
        gates_biased = signal("gates_biased", {"L2a": 1})
        gates_exp = signal("gates_exp", {"L2a": 1})
        beta_ready = signal("beta_ready", {"L2a": 1})
        lnbeta_ready = signal("lnbeta_ready", {"L2a": 1})
        decay_psum = signal("decay_psum", {"L2a": 1})
        decay_ready = signal("decay_ready", {"L2a": 1})
        vp_ready = signal("vp_ready", {"L2a": 1})
        taps_ready = sem("taps_ready")
        xp_ready = signal("xp_ready", {"L3a": 3})
        conv_psum = signal("conv_psum", {"L3a": 3})
        norm_inverse = signal("norm_inverse", {"L3a": 1})
        inverse_psum = signal("inverse_psum", {"L3a": 1})
        silu_ready = signal("silu_ready", {"L3a": 3})
        square_ready = signal("square_ready", {"L3a": 1})
        norm2_psum = signal("norm2_psum", {"L3a": 1})
        ab_ready = signal("ab_ready", {"L3a": 2})
        norm_ready = signal("norm_ready", {"L3a": 1})
        store_ready = signal("store_ready", {"L3a": 1})
        stored = signal("stored", {"L3a": 80}, {"L3a": 1})
        scan_loaded = sem("scan_loaded")
        scan_step = signal("scan_step", {"scan": 7 * CHUNK})
        scan_done = sem("scan_done")
        scan_stored = sem("scan_stored")
        gn_var = sem("gn_var")
        gn_rstd = sem("gn_rstd")
        y_loaded = sem("y_loaded")
        gated = signal("gated", {"L3o": 1})
        s3_psum = signal("s3_psum", {"L3x": 1})
        s3_shifted = signal("s3_shifted", {"L3x": 1})
        p3_ready = signal("p3_ready", {"L3x": 1})
        pt_psum = signal("pt_psum", {"L3x": 1})
        pt_ready = signal("pt_ready", {"L3x": 1})
        a3_psum = signal("a3_psum", {"L3x": 1})
        a3_ready = signal("a3_ready", {"L3x": 1})
        out_stored = sem("out_stored")

        block = stack.enter_context(nc.Block())
        run = [p for p in PHASES if p in phases]
        final = run[-1]
        quantised = [p for p in run if p in ("L0f", "L1f")]

        def kd_zeroed(p):
            return sum(q in run[1:run.index(p) + 1] for q in ("L0f", "L1x"))

        def strip_of(j):
            return slice(STRIP * j, STRIP * (j + 1))

        def spread_q(copy, j):
            for r in range(4):
                yield copy(QB[strip_of(r), :, r].rearrange("p m (i g j) -> p m i g j", i=GB, g=HG)[:, :, :, :, j]
                           .rearrange("p m i g -> p i g m"),
                           QT[strip_of(j)].rearrange("p g (i m r) -> p i g m r", i=GB, r=4)[:, :, :, :, r])

        @block.sync
        def _(sp):
            sp.dma_start(X[:, 0:GB], x.rearrange("b t d -> t b d")[:, 0:GB]).then_inc(inputs_loaded, 16)
            sp.dma_start(K[:], consts).then_inc(inputs_loaded, 16)
            sp.dma_start(COLS[:], cols).then_inc(inputs_loaded, 16)
            for n, (p, parts) in enumerate(W_PARTS):
                if p == "L1a" and run[0] == "L0a" and len(run) > 1:
                    sp.wait_ge(x_updated.sem, x_updated.before["L0x"])
                if p == "L1a" and final == "L0a":
                    break
                lo = W_AT[f"{p}.{parts[0][0]}"][0]
                hi = lo + sum(width for _, width in parts)
                sp.dma_start(W[:, lo:hi], w_all[:, lo:hi]).then_inc(loaded[n], 16)
                if n == 0:
                    sp.dma_start(X[:, GB:B], x.rearrange("b t d -> t b d")[:, GB:B]).then_inc(rest_loaded, 16)
                    sp.dma_start(ROWS[:], rows.to_broadcast([P, R_ALL])).then_inc(rest_loaded, 16)
                    sp.dma_start(MASK3[:], mask3).then_inc(masks_loaded, 16)
            for p in run:
                if p == "L1x":
                    if run[0] != p:
                        sp.wait_ge(x_updated.sem, x_updated.before[p])
                    sp.dma_start(MASK1, mask1.rearrange("b o q k -> q (b o) k")).then_inc(masks_loaded, 16)
                if p in CROSS:
                    with sp.Fori(0, GROUPS) as it:
                        used = proj_psum if p == "L3x" else v_psum
                        sp.wait_ge(used.sem, used.at(p, it, -1))
                        sp.dma_start(CTX[:], ctx_t[:, bass.ds(it * T, T)]).then_inc(ctx_loaded.sem, 16)
                if p == "L3a":
                    with sp.Fori(0, GROUPS) as it:
                        sp.wait_ge(store_ready.sem, store_ready.at(p, it))
                        for m, n in enumerate("qkv"):
                            sp.dma_start(scratch[n][bass.ds(it * GB, GB)].rearrange("b f t -> f b t"),
                                         tile(CV[:, m, :])).then_inc(stored.sem, 16)
                        sp.wait_ge(ab_ready.sem, ab_ready.at(p, it, 1))
                        for m, n in enumerate("ab"):
                            sp.dma_start(scratch[n][bass.ds(it * GB, GB)].rearrange("b h t -> h b t"),
                                         tile(PR[0:H, m, :])).then_inc(stored.sem, 16)
                if p == "scan":
                    sp.wait_ge(stored.sem, stored.before["L3a"] + 80 * GROUPS)
                    for dst, n in ((SQ, "q"), (SK, "k"), (SV, "v"), (SA, "a"), (SBT, "b")):
                        sp.dma_start(dst.rearrange("p f t -> p (f t)"),
                                     scratch[n].rearrange("b (g f) t -> (b g) (f t)", g=8)).then_inc(scan_loaded, 16)
                    sp.wait_ge(scan_done, 1)
                    sp.dma_start(scratch["o"].rearrange("b (g f) t -> (b g) (f t)", g=8),
                                 SO.rearrange("p f t -> p (f t)")).then_inc(scan_stored, 16)
                    sp.wait_ge(scan_stored, 16)
                    sp.dma_start(tile(YT, B), scratch["o"].rearrange("b f t -> f b t")).then_inc(y_loaded, 16)
            if final not in ("L3a", "scan"):
                sp.wait_ge(x_updated.sem, x_updated.before[final] + GROUPS)
            sp.dma_start(out.rearrange("b t d -> t b d"), X[:]).then_inc(out_stored, 16)
            sp.wait_ge(out_stored, 16)

        @block.gpsimd
        def _(pool):
            pool.memset(HALF[:], -0.5)
            pool.memset(VE[:], 1.0)
            pool.memset(ONES[:], 1.0)
            pool.memset(BIG[:, 0:8192], 0.0).then_inc(setup_pool, 1)

            def ln_root(p, it):
                pool.wait_ge(ln_stats.sem, ln_stats.at(p, it))
                pool.tensor_tensor(RSTD[:, 0, :], VEPS[:, 0, :], HALF[:], ALU.pow).then_inc(ln_rstd.sem, 1)

            def root(p, it, k):
                pool.wait_ge(stats_ready.sem, stats_ready.at(p, it, k))
                pool.tensor_tensor(RSTD[:, 1, :], VEPS[:, 1, :], HALF[:], ALU.pow).then_inc(rstd_ready.sem, 1)

            for p in run:
                if p == "scan":
                    pool.wait_ge(gn_var, 1)
                    pool.tensor_tensor(RD[:, 8:10], RD[:, 6:8], HALF[:, 0:2], ALU.pow).then_inc(gn_rstd, 1)
                if p not in LN_PHASES:
                    continue
                if p in ("L0f", "L1x") and p != run[0]:
                    pool.wait_ge(x_updated.sem, x_updated.before[p])
                    pool.memset(BIG[:, 0:8192], 0.0).then_inc(kd_zero, 1)
                if p == "L1x":
                    pool.wait_ge(masks_loaded, 32)
                if p == "L1a":
                    if p != run[0]:
                        pool.wait_ge(x_updated.sem, x_updated.before["L1a"])
                    pool.memset(V1[:, :, :, 64:65], 1.0).then_inc(setup_pool, 1)
                if p in before_loop:
                    ln_root(p, BEFORE_LOOP)
                with pool.Fori(0, GROUPS) as it:
                    if p == "L1x":
                        pool.wait_ge(s1_psum.sem, s1_psum.at(p, it, -1))
                        pool.tensor_copy(MKB[:], MASK1[:, bass.ds(it * GB, GB), :]).then_inc(mask_ready.sem, 1)
                    if p == "L1f":
                        root(p, it, 0)
                    ln_root(p, it)
                    for k in range(p == "L1f", stats_ready.per.get(p, 0)):
                        root(p, it, k)

        @block.tensor
        def _(pe):
            pe.wait_ge(inputs_loaded, 48)
            pe.wait_ge(setup_pool, 1)
            pe.wait_ge(setup_dve, 1 + ("L0a" in run))

            def transpose_next(p, it):
                pe.wait_ge(xn_ready.sem, xn_ready.at(p, it))
                for i in range(GB):
                    mm = pe.transpose(PS[XNT_BANK.get(p, 2)][:, tok(i)], XN[:, i, :], ident)
                mm.then_inc(xnt_psum.sem, 1)

            def scores1(p, it, u):
                i, g = u // HG, u % HG
                bank = PS[1 + u % 3]
                if u >= 3:
                    pe.wait_ge(shifted.sem, shifted.at(p, it, u - 3))
                if p == "L0a":
                    for j in range(4):
                        pe.matmul(bank[:, tok(j)], KD[:, u, j, :], KT[:, g, tok(i)], start=True, stop=False, skip_group_check=True)
                        mm = pe.matmul(bank[:, tok(j)], POS[:, u, j, :], I2[:], start=False, stop=True, skip_group_check=True)
                elif p == "L1a":
                    for n in range(2):
                        c = 2 * g + n
                        mm = pe.matmul(bank[:, tok(n, 256)], Q1[:, c, tok(i)], K1[:, c, i].rearrange("p r t -> p (r t)"),
                                       start=True, stop=True)
                else:
                    if p == "L1x":
                        pe.matmul(tile(bank), NEGI[:], mid(MKB[:, i, :]), start=True, stop=False, skip_group_check=True)
                    mm = pe.matmul(bank, QT[:, g, tok(i)], KD[:, u].rearrange("p j t -> p (j t)"), start=p != "L1x", stop=True,
                                   skip_group_check=True)
                mm.then_inc(s1_psum.sem, 1)

            def transpose_p(p, it, u):
                pe.wait_ge(exp_ready.sem, exp_ready.at(p, it, u))
                if u >= 2:
                    pe.wait_ge(p_ready.sem, p_ready.at(p, it, u - 2))
                for j in range(4):
                    mm = pe.transpose(PS[4 + u % 2][:, tok(j)], PQ[u % 2][:, tok(j)], ident)
                mm.then_inc(t_psum.sem, 1)

            def product_v(p, it, u):
                i, g = u // HG, u % HG
                pe.wait_ge(p_ready.sem, p_ready.at(p, it, u))
                if p == "L1a":
                    if u >= 2:
                        pe.wait_ge(on_ready.sem, on_ready.at(p, it, u - 2))
                elif g == 0 and i >= 2:
                    pe.wait_ge(on_ready.sem, on_ready.at(p, it, i - 2))
                elif g == 0 and i == 0:
                    pe.wait_ge(x_updated.sem, x_updated.at(p, it, -1))
                for j in range(4):
                    h = 4 * g + j
                    if p == "L1a":
                        dst, val = PS[6 + u % 2][:, j * 65:(j + 1) * 65], V1[:, i, h, :]
                    else:
                        dst, val = PS[6 + i % 2][:, h * 9:(h + 1) * 9], VE[:, i, h, :]
                    mm = pe.matmul(dst, PR[:, u % 2, tok(j)], val, start=True, stop=True)
                if p == "L1x" and g == 3:
                    mm = pe.matmul(PS[6 + i % 2][:, 144:288], ONES[:], VE[:, i].rearrange("p h d -> p (h d)"),
                                   start=True, stop=True)
                mm.then_inc(pv_done.sem, 1)

            def attend(p, it, tail=None, fill=None):
                for u in range(3):
                    scores1(p, it, u)
                transpose_p(p, it, 0)
                for u in range(UNITS):
                    if tail and u >= 6 and u % HG == 2:
                        tail(p, it, (u - 6) // HG)
                    if u + 3 < UNITS:
                        scores1(p, it, u + 3)
                    if u == UNITS - 3:
                        pe.wait_ge(shifted.sem, shifted.at(p, it, u))
                        transpose_next(p, it)
                    if u + 1 < UNITS:
                        transpose_p(p, it, u + 1)
                    if fill:
                        fill(u)
                    product_v(p, it, u)
                if tail:
                    tail(p, it, GB - 1)

            def outputs_t(p, it, bank):
                pe.wait_ge(on_ready.sem, on_ready.at(p, it, GB - 1))
                for i in range(GB):
                    mm = pe.transpose(PS[bank][:, tok(i)], ON[:, i, :], ident)
                mm.then_inc(ot_psum.sem, 1)

            def project_out(p, it, bank):
                pe.wait_ge(ot_ready.sem, ot_ready.at(p, it))
                for i in range(GB):
                    mm = pe.matmul(PS[bank][:, tok(i)], OT[:, tok(i)], w(f"{p}.o"), start=True, stop=True)
                mm.then_inc(y_psum.sem, 1)

            def keys(p, g):
                pe.matmul(PS[K_BANK[g]], w(f"{p}.k", g * P, P), (CTX if p in CROSS else XNT)[:], start=True, stop=True
                          ).then_inc(k_psum.sem, 1)

            def values(p):
                for i in range(GB):
                    mm = pe.matmul(PS[V_BANK][:, tok(i)], (CTX if p in CROSS else XNT)[:, tok(i)], w(f"{p}.v"), start=True, stop=True)
                mm.then_inc(v_psum.sem, 1)

            def queries(p, new, g):
                if g:
                    pe.wait_ge(k_ready.sem, k_ready.at(p, new, g * k_ready.per[p] // HG - 1))
                    if p in CROSS:
                        pe.wait_ge(k_ready_dve.sem, k_ready_dve.at(p, new, g - 1))
                pe.matmul(PS[Q_BANK[g]], w(f"{p}.q", g * P, P), XNT[:], start=True, stop=True).then_inc(q_psum.sem, 1)

            def small_first(p):
                if p in CROSS:
                    pe.wait_ge(ctx_loaded.sem, ctx_loaded.at(p, 0, 15))
                pe.wait_ge(xnt_ready.sem, xnt_ready.at(p, -1))
                for g in range(HG):
                    keys(p, g)
                values(p)
                for g in range(HG):
                    queries(p, 0, g)

            def small(p, it, more):
                def fill(u):
                    if u == UNITS - 3 and p in CROSS:
                        pe.wait_ge(ctx_loaded.sem, ctx_loaded.at(p, it + 1, 15))
                        keys(p, 0)
                    if u == UNITS - 2:
                        if p not in CROSS:
                            pe.wait_ge(xnt_ready.sem, xnt_ready.at(p, it))
                            keys(p, 0)
                        keys(p, 1)
                    if u == UNITS - 1:
                        keys(p, 2)

                pe.wait_ge(v_ready.sem, v_ready.at(p, it))
                pe.wait_ge(k_ready.sem, k_ready.at(p, it, k_ready.per[p] - 1))
                pe.wait_ge(q_ready.sem, q_ready.at(p, it, HG - 1))
                if p in CROSS:
                    pe.wait_ge(k_ready_dve.sem, k_ready_dve.at(p, it, HG - 1))
                if p == "L0a":
                    pe.wait_ge(qd_ready.sem, qd_ready.at(p, it, 3))
                    pe_table = w("L0a.pe")
                    for c in range(16):
                        if c >= 4:
                            copied = (pos_even, pos_odd)[c % 2]
                            pe.wait_ge(copied.sem, copied.at(p, it, c // 2 - 2))
                        for n in range(2):
                            m = 2 * c + n
                            mm = pe.matmul(PS[1 + c % 4][:, tok(n, 256)], pe_table[:, P - 1 - 4 * m:2 * P - 1 - 4 * m],
                                           QB[:, m].rearrange("p r h -> p (r h)"), start=True, stop=True)
                        mm.then_inc(pos_psum.sem, 1)
                    pe.wait_ge(kd_ready.sem, kd_ready.at(p, it, 3))
                    pe.wait_ge(pos_even.sem, pos_even.at(p, it, 7))
                    pe.wait_ge(pos_odd.sem, pos_odd.at(p, it, 7))
                if p == "L1x":
                    pe.wait_ge(mask_ready.sem, mask_ready.at(p, it))
                attend(p, it, fill=fill if more else None)
                if more:
                    pe.wait_ge(xnt_ready.sem, xnt_ready.at(p, it))
                    keys(p, 3)
                    values(p)
                pe.wait_ge(on_ready.sem, on_ready.at(p, it, GB - 1))
                if p != "L0x":
                    outputs_t(p, it, 5)
                if more:
                    queries(p, it + 1, 0)
                    queries(p, it + 1, 1)
                if p != "L0x":
                    project_out(p, it, 6)
                if more:
                    queries(p, it + 1, 2)
                    queries(p, it + 1, 3)

            def l1_attention(p, it):
                pe.wait_ge(y_taken.sem, y_taken.at(p, it, -1))
                pe.wait_ge(xnt_ready.sem, xnt_ready.at(p, it - 1))
                for c in range(8):
                    if c >= 4:
                        pe.wait_ge(q_ready.sem, q_ready.at(p, it, c - 4))
                    pe.matmul(PS[c % 4], w("L1a.q", c * P, P), XNT[:], start=True, stop=True).then_inc(q_psum.sem, 1)
                    if c >= 4:
                        pe.wait_ge(k_ready.sem, k_ready.at(p, it, 2 * (c - 4) + 1))
                    pe.matmul(PS[4 + c % 4], w("L1a.k", c * P, P), XNT[:], start=True, stop=True).then_inc(k_psum.sem, 1)
                for c in range(8):
                    if c < 4:
                        pe.wait_ge(q_ready.sem, q_ready.at(p, it, 4 + c))
                    else:
                        pe.wait_ge(v_ready.sem, v_ready.at(p, it, c - 4))
                    pe.matmul(PS[c % 4], XNT[:, tok(c // 2)], w("L1a.v", (c % 2) * T, T), start=True, stop=True).then_inc(v_psum.sem, 1)
                pe.wait_ge(k_ready.sem, k_ready.at(p, it, 15))
                pe.wait_ge(v_ready.sem, v_ready.at(p, it, 7))

                def tail(p, it, i):
                    pe.wait_ge(on_ready.sem, on_ready.at(p, it, i * HG + 3))
                    for half in range(2):
                        if half:
                            pe.wait_ge(ot_ready.sem, ot_ready.at(p, it, 2 * i))
                        elif i:
                            pe.wait_ge(y_taken.sem, y_taken.at(p, it, i - 1))
                        for c in range(4):
                            mm = pe.transpose(PS[0][:, tok(c)], ON1[:, tok(4 * half + c)], ident)
                        mm.then_inc(ot_psum.sem, 1)
                    pe.wait_ge(ot_ready.sem, ot_ready.at(p, it, 2 * i + 1))
                    for c in range(8):
                        mm = pe.matmul(PS[0][:, 0:P], OT1[:, c, :], w("L1a.o", c * P, P), start=c == 0, stop=c == 7)
                    mm.then_inc(y_psum.sem, 1)

                attend(p, it, tail)

            def bit_ffn(p, it):
                pe.wait_ge(xq_ready.sem, xq_ready.at(p, it))
                for i in range(GB):
                    mm = pe.transpose(PS[7][:, tok(i)], XN[:, i, :], ident)
                mm.then_inc(xqt_psum.sem, 1)
                pe.wait_ge(xqt_ready.sem, xqt_ready.at(p, it))
                if p == "L0f":
                    pe.wait_ge(x_updated.sem, x_updated.at(p, it, -1))
                for i in range(GB):
                    mm = pe.matmul(PS[i], XQT[:, tok(i)], WQ[:, 0, :], start=True, stop=True)
                    if p == "L0f":
                        mm = pe.matmul(PS[4 + i], XQT[:, tok(i)], WQ[:, 1, :], start=True, stop=True)
                    mm.then_inc(h_psum.sem, 1)

                def down(i):
                    pe.wait_ge(hqt_ready.sem, hqt_ready.at(p, it, i))
                    for c in range(4):
                        mm = pe.matmul(PS[4][:, tok(i)], HQT[:, i, tok(c)], WQ[:, 2, tok(c)], start=c == 0, stop=c == 3)
                    return mm

                for i in range(GB):
                    pe.wait_ge(hq_ready.sem, hq_ready.at(p, it, i))
                    for c in range(4):
                        mm = pe.transpose(PS[i][:, tok(c)], HID[:, i, tok(c)], ident)
                    mm.then_inc(hqt_psum.sem, 1)
                    if i:
                        down(i - 1)
                down(GB - 1).then_inc(y_psum.sem, 1)

            def weight_means(value):
                pe.wait_ge(wsum_ready, value)
                pe.matmul(PS[0][:, 0:3], ONES[:], WSC[:, 0, :], start=True, stop=True).then_inc(wsum_psum, 1)

            def linear_attention(p, it):
                def project(name, bank):
                    for g in range(2):
                        mm = pe.matmul(PS[bank + g], w(f"{p}.{name}", g * P, P), XNT[:], start=True, stop=True)
                    return mm

                pe.wait_ge(xnt_ready.sem, xnt_ready.at(p, it - 1))
                for i in range(GB):
                    pe.matmul(PS[0][:, tok(i)], XNT[:, tok(i)], w(f"{p}.v"), start=True, stop=True)
                    mm = pe.matmul(PS[1][:, tok(i, 16)], XNT[:, tok(i)], w(f"{p}.gates"), start=True, stop=True)
                mm.then_inc(gates_psum.sem, 1)
                project("k", 2)
                project("ks", 4).then_inc(proj_psum.sem, 1)
                pe.wait_ge(x_updated.sem, x_updated.at(p, it, -1))
                project("q", 6)
                pe.wait_ge(lnbeta_ready.sem, lnbeta_ready.at(p, it))
                pe.matmul(PS[1][:, 0:32], const("tri"), SG[:, 3, 0:32], start=True, stop=True).then_inc(decay_psum.sem, 1)
                pe.wait_ge(proj_ready.sem, proj_ready.at(p, it, 0))
                project("qs", 2).then_inc(proj_psum.sem, 1)

                def scores(u):
                    i, g = u // 2, u % 2
                    if u >= 2:
                        pe.wait_ge(p_ready.sem, p_ready.at(p, it, u - 2))
                    for j in range(4):
                        mm = pe.matmul(PS[4 + u % 2][:, tok(j)], KD[:, 4 * i + g, j, :], QT[:, g, tok(i)], start=True, stop=True)
                    mm.then_inc(s2_psum.sem, 1)

                pe.wait_ge(k_ready.sem, k_ready.at(p, it, 3))
                pe.wait_ge(proj_ready.sem, proj_ready.at(p, it, 1))
                scores(0)
                for u in range(8):
                    if u < 7:
                        scores(u + 1)
                    if u == 0:
                        pe.wait_ge(vp_ready.sem, vp_ready.at(p, it))
                    pe.wait_ge(p_ready.sem, p_ready.at(p, it, u))
                    i, g = u // 2, u % 2
                    if g == 0 and i >= 2:
                        pe.wait_ge(on_ready.sem, on_ready.at(p, it, i - 2))
                    for j in range(4):
                        h = 4 * g + j
                        mm = pe.matmul(PS[6 + i % 2][:, h * 16:h * 16 + 16], PR[:, u % 2, tok(j)],
                                       VE16[:, i, h * 16:h * 16 + 16], start=True, stop=True)
                    mm.then_inc(pv_done.sem, 1)
                    if u == 5:
                        transpose_next(p, it)
                outputs_t(p, it, 3)
                project_out(p, it, 6)

            def experts(p, it):
                pe.wait_ge(xnt_ready.sem, xnt_ready.at(p, it - 1))
                for c in range(2):
                    pe.matmul(PS[c], w("L2f.sw1", c * P, P), XNT[:], start=True, stop=True)
                for i in range(GB):
                    pe.matmul(PS[6][:, tok(i, 8)], XNT[:, tok(i)], w("L2f.router"), start=True, stop=True)
                pe.wait_ge(x_updated.sem, x_updated.at(p, it, -1))
                for c in range(2):
                    mm = pe.matmul(PS[2 + c], w("L2f.sw3", c * P, P), XNT[:], start=True, stop=True)
                mm.then_inc(h_psum.sem, 1)
                pe.wait_ge(shared_ready.sem, shared_ready.at(p, it))
                for i in range(GB):
                    for c in range(2):
                        mm = pe.matmul(PS[7][:, tok(i)], HIDT[:, c, tok(i)], w("L2f.sw2", c * P, P), start=c == 0, stop=c == 1)
                mm.then_inc(shared_psum.sem, 1)

                def up(e):
                    if e >= 2:
                        pe.wait_ge(act_ready.sem, act_ready.at(p, it, 3 + e - 2))
                    pe.matmul(PS[e % 2], w("L2f.ew1", e * P, P), XNT[:], start=True, stop=True).then_inc(h_psum.sem, 1)

                up(0)
                for e in range(8):
                    if e < 7:
                        up(e + 1)
                    pe.wait_ge(act_ready.sem, act_ready.at(p, it, 3 + e))
                    if e >= 2:
                        pe.wait_ge(expert_used.sem, expert_used.at(p, it, e - 2))
                    for i in range(GB):
                        mm = pe.matmul(PS[2 + e % 2][:, tok(i)], EXPH[:, e % 4, tok(i)], w("L2f.ew2", e * P, P),
                                       start=True, stop=True)
                    mm.then_inc(expert_psum.sem, 1)
                    if e == 6:
                        transpose_next(p, it)
                pe.nop().then_inc(y_psum.sem, 1)

            def delta_inputs(p, new):
                pe.wait_ge(xnt_ready.sem, xnt_ready.at(p, new - 1))
                for n, name in enumerate("qkv"):
                    mm = pe.matmul(PS[n], w(f"L3a.{name}"), XNT[:], start=True, stop=True)
                mm.then_inc(proj_psum.sem, 1)

            def delta_gates(p, new):
                pe.matmul(PS[3], w("L3a.g"), XNT[:], start=True, stop=True)
                for n, name in enumerate("ab"):
                    mm = pe.matmul(PS[4 + n][0:H, :], w(f"L3a.{name}"), XNT[:], start=True, stop=True)
                mm.then_inc(proj_psum.sem, 1)

            def delta_project(p, it, more):
                for m in range(3):
                    pe.wait_ge(xp_ready.sem, xp_ready.at(p, it, m))
                    for tap in range(4):
                        mm = pe.matmul(tile(PS[m]), TAPS[:, m, tap, :], XP[:, m, :, tap:tap + P], start=tap == 0, stop=tap == 3)
                    mm.then_inc(conv_psum.sem, 1)
                transpose_next(p, it)
                pe.wait_ge(square_ready.sem, square_ready.at(p, it))
                head_of = const("heads")[:, 0:P:HD]
                for i in range(GB):
                    for m, sq in enumerate((TMP, TMP2)):
                        mm = pe.matmul(PS[6][:, tok(2 * i + m, H)], sq[:, tok(i)], head_of, start=True, stop=True)
                mm.then_inc(norm2_psum.sem, 1)
                pe.wait_ge(xnt_ready.sem, xnt_ready.at(p, it))
                if more:
                    pe.wait_ge(silu_ready.sem, silu_ready.at(p, it, 2))
                    delta_inputs(p, it + 1)
                pe.wait_ge(norm_inverse.sem, norm_inverse.at(p, it))
                for m in range(2):
                    for i in range(GB):
                        mm = pe.matmul(PS[6 + m][:, tok(i)], (TMP, TMP2)[m][:, tok(i)], ident, start=True, stop=True)
                mm.then_inc(inverse_psum.sem, 1)
                if more:
                    pe.wait_ge(ab_ready.sem, ab_ready.at(p, it, 1))
                    delta_gates(p, it + 1)

            def delta_out(p, it):
                pe.wait_ge(gated.sem, gated.at(p, it))
                for i in range(GB):
                    mm = pe.matmul(PS[1][:, tok(i)], TMP2[:, tok(i)], w("L3a.o"), start=True, stop=True)
                mm.then_inc(y_psum.sem, 1)

            def one_head(p, it):
                pe.wait_ge(xnt_ready.sem, xnt_ready.at(p, it - 1))
                pe.wait_ge(ctx_loaded.sem, ctx_loaded.at(p, it, 15))
                pe.matmul(PS[0], w("L3x.k"), CTX[:], start=True, stop=True)
                for i in range(GB):
                    pe.matmul(PS[2][:, tok(i)], CTX[:, tok(i)], w("L3x.v"), start=True, stop=True)
                pe.matmul(PS[1], w("L3x.q"), XNT[:], start=True, stop=True).then_inc(proj_psum.sem, 1)
                pe.wait_ge(kq_ready.sem, kq_ready.at(p, it))
                for i in range(GB):
                    mm = pe.matmul(PS[3][:, tok(i)], QT[:, 0, tok(i)], KT[:, 0, tok(i)], start=True, stop=True)
                mm.then_inc(s3_psum.sem, 1)
                transpose_next(p, it)
                pe.wait_ge(p3_ready.sem, p3_ready.at(p, it))
                for i in range(GB):
                    mm = pe.transpose(PS[4][:, tok(i)], PR[:, 0, tok(i)], ident)
                mm.then_inc(pt_psum.sem, 1)
                pe.wait_ge(pt_ready.sem, pt_ready.at(p, it))
                pe.wait_ge(proj_ready.sem, proj_ready.at(p, it))
                for i in range(GB):
                    mm = pe.matmul(PS[5][:, tok(i)], ON[:, i, :], PR[:, 1, tok(i)], start=True, stop=True)
                mm.then_inc(a3_psum.sem, 1)
                pe.wait_ge(a3_ready.sem, a3_ready.at(p, it))
                pe.wait_ge(x_updated.sem, x_updated.at(p, it, -1))
                for i in range(GB):
                    mm = pe.matmul(PS[7][:, tok(i)], OT[:, tok(i)], w("L3x.o"), start=True, stop=True)
                mm.then_inc(y_psum.sem, 1)

            def relu_ffn(p, it):
                pe.wait_ge(x_updated.sem, x_updated.at(p, it, -1))
                pe.wait_ge(xnt_ready.sem, xnt_ready.at(p, it - 1))
                for c in range(4):
                    pe.matmul(PS[c], w("L3f.w1", c * P, P), XNT[:], start=True, stop=True).then_inc(h_psum.sem, 1)
                transpose_next(p, it)
                pe.wait_ge(act_ready.sem, act_ready.at(p, it, 3))
                for i in range(GB):
                    for c in range(4):
                        mm = pe.matmul(PS[4][:, tok(i)], HIDT[:, c, tok(i)], w("L3f.w2", c * P, P), start=c == 0, stop=c == 3)
                mm.then_inc(y_psum.sem, 1)

            bodies = {"L1a": l1_attention, "L0f": bit_ffn, "L1f": bit_ffn, "L2a": linear_attention,
                      "L2f": experts, "L3o": delta_out, "L3x": one_head, "L3f": relu_ffn}
            for p in run:
                if p in W_PHASE:
                    pe.wait_ge(loaded[W_PHASE.index(p)], 16)
                if p == "scan":
                    continue
                if p == "L3a":
                    pe.wait_ge(taps_ready, 1)
                if p in ("L0f", "L1f"):
                    weight_means(quantised.index(p) + 1)
                    pe.wait_ge(wq_ready, quantised.index(p) + 1)
                if p == "L1a":
                    pe.wait_ge(setup_pool, 2)
                pe.wait_ge(x_updated.sem, x_updated.before[p])
                if p in before_loop_t:
                    transpose_next(p, BEFORE_LOOP)
                if p == "L3a":
                    delta_inputs(p, 0)
                    delta_gates(p, 0)
                    with pe.Fori(0, GROUPS - 1) as it:
                        delta_project(p, it, True)
                    delta_project(p, GROUPS - 1, False)
                    continue
                if p in SMALL:
                    small_first(p)
                    with pe.Fori(0, GROUPS - 1) as it:
                        small(p, it, True)
                    small(p, GROUPS - 1, False)
                    continue
                with pe.Fori(0, GROUPS) as it:
                    bodies[p](p, it)

        @block.scalar
        def _(act):
            act.wait_ge(inputs_loaded, 48)

            def xnt_next(p, it):
                act.wait_ge(xnt_psum.sem, xnt_psum.at(p, it))
                act.activation(XNT[:], PS[XNT_BANK.get(p, 2)], ACT.Copy).then_inc(xnt_ready.sem, 1)

            def exponentials(p, it, scale, fill=None):
                def exp(u):
                    act.wait_ge(shifted.sem, shifted.at(p, it, u))
                    act.activation(PQ[u % 2], PQ[u % 2], ACT.Exp, scale=scale).then_inc(exp_ready.sem, 1)

                exp(0)
                for u in range(UNITS):
                    if u + 1 < UNITS:
                        exp(u + 1)
                    act.wait_ge(t_psum.sem, t_psum.at(p, it, u))
                    if u >= 2:
                        act.wait_ge(pv_done.sem, pv_done.at(p, it, u - 2))
                    act.activation(PR[:, u % 2, :], PS[4 + u % 2], ACT.Copy).then_inc(p_ready.sem, 1)
                    if p == "L1a" and u >= 5 and u % HG == 1:
                        outputs_t(p, it, (u - 5) // HG)
                    if u == UNITS - 3:
                        xnt_next(p, it)
                    if u == UNITS - 2 and fill:
                        fill()
                if p == "L1a":
                    outputs_t(p, it, GB - 1)

            def outputs_t(p, it, i):
                for half in range(2):
                    act.wait_ge(ot_psum.sem, ot_psum.at(p, it, 2 * i + half))
                    act.activation(OT1[:, 4 * half:4 * half + 4, :], tile(PS[0]), ACT.Copy).then_inc(ot_ready.sem, 1)

            def keys(p, new, g, strips):
                func = ACT.Relu if p == "L0x" else ACT.Identity
                if p == "L0a":
                    act.wait_ge(k_psum.sem, k_psum.at(p, new, g))
                    act.activation(KT[:, g, :], PS[K_BANK[g]], func, bias=col(f"{p}.bk", g)).then_inc(k_ready.sem, 1)
                    return
                act.wait_ge(k_psum.sem, k_psum.at(p, new, g))
                for j in strips:
                    r = strip_of(j)
                    act.activation(KD.rearrange("p (i g) j t -> p i g j t", g=HG)[r, :, g, j, :], tile(PS[K_BANK[g]][r]), func,
                                   bias=col(f"{p}.bk", g)[r]).then_inc(k_ready.sem, 1)

            def small(p, it, more):
                if p == "L0a":
                    act.wait_ge(q_ready.sem, q_ready.at(p, it, HG - 1))
                    for j in range(2):
                        for ins in spread_q(act.copy, j):
                            pass
                        ins.then_inc(qd_ready.sem, 1)
                    for c in range(0, 16, 2):
                        act.wait_ge(pos_psum.sem, pos_psum.at(p, it, c))
                        act.activation(POS.rearrange("p u j s -> p (u j) s")[:, :, 8 * c:8 * c + 8],
                                       PS[1 + c % 4].rearrange("p (s u) -> p u s", u=64), ACT.Copy).then_inc(pos_even.sem, 1)
                        if c < 8:
                            r = strip_of(c // 2)
                            act.copy(KD.rearrange("p (i g) j t -> p i g j t", g=HG)[r, :, :, c // 2, :],
                                     QT[r].rearrange("p g (i t) -> p i g t", i=GB)).then_inc(kd_ready.sem, 1)
                early = more and p in CROSS
                exponentials(p, it, float(HD) ** -0.5, (lambda: keys(p, it + 1, 0, (0, 1))) if early else None)
                if more:
                    keys(p, it + 1, 0, (2,))
                    keys(p, it + 1, 1, range(3))
                if p != "L0x":
                    act.wait_ge(ot_psum.sem, ot_psum.at(p, it))
                    act.activation(OT[:], PS[5], ACT.Copy).then_inc(ot_ready.sem, 1)
                if more:
                    keys(p, it + 1, 2, range(3))
                    keys(p, it + 1, 3, range(3))

            def l1_attention(p, it):
                for c in range(8):
                    act.wait_ge(k_psum.sem, k_psum.at(p, it, c))
                    for r in range(2):
                        half = slice(64 * r, 64 * r + 64)
                        act.activation(K1[half, c, :, r, :], tile(PS[4 + c % 4][half]), ACT.Identity,
                                       bias=col("L1a.bk", c)[half]).then_inc(k_ready.sem, 1)
                exponentials(p, it, 64.0 ** -0.5)

            def bit_ffn(p, it):
                if p == "L1f":
                    act.wait_ge(xn_ready.sem, xn_ready.at(p, it - 1))
                    for i in range(GB):
                        ins = act.activation(QK[:, 4 + i, 0:P], XN[:, i, :], ACT.Square, accum_out=SS[:, 0, i:i + 1])
                    ins.then_inc(squares_ready.sem, 1)
                act.wait_ge(xqt_psum.sem, xqt_psum.at(p, it))
                act.activation(XQT, PS[7], ACT.Copy).then_inc(xqt_ready.sem, 1)
                if p == "L0f":
                    act.wait_ge(dq_ready.sem, dq_ready.at(p, it))
                for i in range(GB):
                    if p == "L0f":
                        act.wait_ge(h_psum.sem, h_psum.at(p, it, i))
                        act.activation(HID[:, i, :], PS[i], ACT.Silu, scale=DQ[:, 0, i:i + 1]).then_inc(act_ready.sem, 1)
                    else:
                        act.wait_ge(pre_ready.sem, pre_ready.at(p, it, i))
                        act.activation(HID[:, i, :], HID[:, i, :], ACT.Gelu).then_inc(act_ready.sem, 1)
                if p == "L1f":
                    act.wait_ge(act_ready.sem, act_ready.at(p, it, GB - 1))
                    for i in range(GB):
                        ins = act.activation(QK[:, i, :], HID[:, i, :], ACT.Square, accum_out=SS[:, 1, i:i + 1])
                    ins.then_inc(squares_ready.sem, 1)
                for i in range(GB):
                    act.wait_ge(hqt_psum.sem, hqt_psum.at(p, it, i))
                    act.activation(HQT[:, i, :], PS[i], ACT.Copy).then_inc(hqt_ready.sem, 1)

            def linear_attention(p, it):
                act.wait_ge(gates_biased.sem, gates_biased.at(p, it))
                act.activation(SG[:, 1, :], SG[:, 0, :], ACT.Exp, scale=-1.0).then_inc(gates_exp.sem, 1)
                act.wait_ge(beta_ready.sem, beta_ready.at(p, it))
                act.activation(SG[:, 3, 0:32], SG[:, 2, 0:32], ACT.Ln).then_inc(lnbeta_ready.sem, 1)
                act.wait_ge(decay_psum.sem, decay_psum.at(p, it))
                act.activation(SG[:, 4, 0:32], PS[1][:, 0:32], ACT.Exp)
                act.activation(SG[:, 5, 0:32], PS[1][:, 0:32], ACT.Exp, scale=-1.0).then_inc(decay_ready.sem, 1)
                act.wait_ge(proj_ready.sem, proj_ready.at(p, it, 0))
                for j in range(4):
                    r = strip_of(j)
                    act.copy(KD.rearrange("p (i g) j t -> p i g j t", g=HG)[r, :, 0:2, j, :],
                             KT[r, 0:2].rearrange("p g (i t) -> p i g t", i=GB)).then_inc(k_ready.sem, 1)
                xnt_next(p, it)
                act.wait_ge(ot_psum.sem, ot_psum.at(p, it))
                act.activation(OT[:], PS[3], ACT.Copy).then_inc(ot_ready.sem, 1)

            def experts(p, it):
                act.wait_ge(h_psum.sem, h_psum.at(p, it, 0))
                for c in range(2):
                    act.activation(HIDT[:, c, :], PS[c], ACT.Silu).then_inc(act_ready.sem, 1)
                act.activation(SG[:, 0, 0:32], PS[6][:, 0:32], ACT.Sigmoid).then_inc(act_ready.sem, 1)
                for e in range(8):
                    act.wait_ge(h_psum.sem, h_psum.at(p, it, 1 + e))
                    if e >= 4:
                        act.wait_ge(expert_psum.sem, expert_psum.at(p, it, e - 4))
                    act.activation(EXPH[:, e % 4, :], PS[e % 2], ACT.Gelu).then_inc(act_ready.sem, 1)
                xnt_next(p, it)

            def delta_project(p, it):
                act.wait_ge(proj_psum.sem, proj_psum.at(p, it, 1))
                act.activation(GT[:, bass.ds(it * T, T)], PS[3], ACT.Silu, bias=col("L3a.bg"))
                act.wait_ge(stored.sem, stored.at(p, it - 1, 79))
                for m in range(3):
                    act.wait_ge(conv_psum.sem, conv_psum.at(p, it, m))
                    act.activation(CV[:, m, :], PS[m], ACT.Silu).then_inc(silu_ready.sem, 1)
                xnt_next(p, it)
                act.wait_ge(norm2_psum.sem, norm2_psum.at(p, it))
                act.activation(NORM, PS[6][:, 0:P], ACT.Sqrt).then_inc(norm_ready.sem, 1)
                for m, n in enumerate("ab"):
                    act.activation(PR[0:H, m, :], PS[4 + m][0:H, :], ACT.Sigmoid, bias=col(f"L3a.b{n}", 0, H)
                                   ).then_inc(ab_ready.sem, 1)

            def one_head(p, it):
                act.wait_ge(proj_psum.sem, proj_psum.at(p, it))
                act.activation(KT[:, 0, :], PS[0], ACT.Identity, bias=col("L3x.bk"))
                act.activation(QT[:, 0, :], PS[1], ACT.Identity, bias=col("L3x.bq")).then_inc(kq_ready.sem, 1)
                xnt_next(p, it)
                act.wait_ge(s3_shifted.sem, s3_shifted.at(p, it))
                act.activation(PR[:, 0, :], TMP[:], ACT.Exp).then_inc(p3_ready.sem, 1)
                act.wait_ge(pt_psum.sem, pt_psum.at(p, it))
                act.activation(PR[:, 1, :], PS[4], ACT.Copy).then_inc(pt_ready.sem, 1)
                act.wait_ge(a3_psum.sem, a3_psum.at(p, it))
                act.activation(OT[:], PS[5], ACT.Copy).then_inc(a3_ready.sem, 1)

            def relu_ffn(p, it):
                for c in range(4):
                    act.wait_ge(h_psum.sem, h_psum.at(p, it, c))
                    act.activation(HIDT[:, c, :], PS[c], ACT.Relu, bias=col("L3f.b1", c)).then_inc(act_ready.sem, 1)
                xnt_next(p, it)

            bodies = {"L1a": l1_attention, "L0f": bit_ffn, "L1f": bit_ffn, "L2a": linear_attention,
                      "L2f": experts, "L3a": delta_project, "L3x": one_head, "L3f": relu_ffn}
            for p in run:
                if p in ("L1a", "L1x") and kd_zeroed(p):
                    act.wait_ge(kd_zero, kd_zeroed(p))
                if p == "L0x" or p in ("L0a", "L2a", "L2x"):
                    act.wait_ge(setup_pool, 1)
                if p == "L0a":
                    act.wait_ge(setup_dve, 2)
                if p in before_loop_t:
                    act.drain()
                    xnt_next(p, BEFORE_LOOP)
                if p in SMALL:
                    for g in range(HG):
                        keys(p, 0, g, range(3))
                    with act.Fori(0, GROUPS - 1) as it:
                        small(p, it, True)
                    small(p, GROUPS - 1, False)
                if p in bodies:
                    with act.Fori(0, GROUPS) as it:
                        bodies[p](p, it)

        @block.vector
        def _(dve):
            if "L0a" in run:
                dve.memset(QB.rearrange("p m r h -> p (m r h)"), 0.0).then_inc(setup_dve, 1)
            dve.wait_ge(inputs_loaded, 48)
            dve.tensor_scalar(I2[:], ident, 2.0, None, ALU.mult)
            dve.tensor_scalar(NEGI[:], ident, MASKED, None, ALU.mult).then_inc(setup_dve, 1)
            dve.wait_ge(setup_pool, 1)
            dve.nop().then_inc(x_updated.sem, 1)

            def moments(src, mv):
                for i in range(GB):
                    dve.bn_stats(ST[:, i, :], src(i))
                dve.drain()
                for i in range(GB):
                    dve.bn_aggr(mv[:, i, :], ST[:, i, :])
                dve.drain()

            def next_group(it):
                return (it + 1) % GROUPS

            def next_moments(p, it):
                moments(lambda i: seq(next_group(it), i), MV)
                dve.tensor_scalar(VEPS[:, 0, :], MV[:, :, 1], 1e-5, None, ALU.add).then_inc(ln_stats.sem, 1)

            def next_normed(p, it):
                dve.wait_ge(ln_rstd.sem, ln_rstd.at(p, it))
                if it is not BEFORE_LOOP:
                    if p in BIT:
                        dve.wait_ge(xqt_psum.sem, xqt_psum.at(p, it))
                    else:
                        dve.wait_ge(xnt_psum.sem, xnt_psum.at(p, it - 1))
                for i in range(GB):
                    ins = dve.tensor_scalar(XN[:, i, :], seq(next_group(it), i), MV[:, i, 0:1], RSTD[:, 0, i:i + 1],
                                            ALU.subtract, ALU.mult)
                ins.then_inc(xn_ready.sem, 1)

            def add_to_x(p, it, y, bias=None):
                if bias is not None:
                    dve.tensor_tensor(tile(TMP[:]), y, mid(bias), ALU.add)
                    dve.drain()
                    y = tile(TMP[:])
                dve.tensor_tensor(seqs(it), seqs(it), y, ALU.add).then_inc(x_updated.sem, 1)
                dve.drain()

            def take_max(p, it, u):
                dve.wait_ge(s1_psum.sem, s1_psum.at(p, it, u))
                dve.tensor_reduce(MX[:, tok(u % 4, 4)], tile(PS[1 + u % 3]), AX_X, ALU.max).then_inc(max_taken.sem, 1)

            def shift(p, it, u):
                m = MX[:, tok(u % 4, 4)]
                dve.wait_ge(max_taken.sem, max_taken.at(p, it, u))
                if p == "L1x":
                    dve.tensor_scalar(m, m, FULL[:, 1, u // HG:u // HG + 1], None, ALU.mult)
                    dve.drain()
                if u >= 2:
                    dve.wait_ge(t_psum.sem, t_psum.at(p, it, u - 2))
                dve.tensor_tensor(tile(PQ[u % 2]), tile(PS[1 + u % 3]), last(m, P), ALU.subtract).then_inc(shifted.sem, 1)

            def normalise(p, it, i):
                dve.wait_ge(pv_done.sem, pv_done.at(p, it, i * HG + HG - 1))
                o = PS[6 + i % 2][:, 0:144].rearrange("p (h d) -> p h d", h=H)
                if p == "L1x":
                    vs = PS[6 + i % 2][:, 144:288].rearrange("p (h d) -> p h d", h=H)
                    os = OS[:, i % 2]
                    dve.tensor_copy(os, o)
                    dve.drain()
                    dve.scalar_tensor_tensor(os, vs, FULL[:, 0, i:i + 1], os, ALU.mult, ALU.add)
                    dve.drain()
                    o = os
                rd = RD[:, H * (i % 2):H * (i % 2) + H]
                dve.reciprocal(rd, o[:, :, HD])
                dve.drain()
                dve.tensor_tensor(ON[:, i, :].rearrange("p (h d) -> p h d", h=H), o[:, :, 0:HD], last(rd, HD),
                                  ALU.mult).then_inc(on_ready.sem, 1)

            def attend(p, it, norm, norm_unit=None, take_y=None, fill=None):
                take_max(p, it, 0)
                for u in range(UNITS):
                    if u + 1 < UNITS:
                        take_max(p, it, u + 1)
                    shift(p, it, u)
                    if norm_unit and u >= 3:
                        norm_unit(u - 3)
                    if norm and u >= 6 and u % HG == 2:
                        norm(p, it, (u - 6) // HG)
                    if take_y and u >= 8 and u % HG == 0:
                        take_y((u - 8) // HG)
                    if u == 5:
                        next_moments(p, it)
                    if u == 8:
                        next_normed(p, it)
                if fill:
                    fill()
                if norm:
                    norm(p, it, GB - 1)
                else:
                    for u in range(UNITS - 3, UNITS):
                        norm_unit(u)
                    take_y(GB - 2)
                    take_y(GB - 1)

            def values(p, new):
                dve.wait_ge(v_psum.sem, v_psum.at(p, new))
                dst = VE[:, :, :, 0:HD]
                src = PS[V_BANK].rearrange("p (b h d) -> p b h d", b=GB, h=H)
                if p == "L0a":
                    ins = dve.tensor_copy(dst, src)
                elif p == "L0x":
                    ins = dve.tensor_scalar(dst, src, 0.0, None, ALU.max)
                else:
                    for i in range(GB):
                        ins = dve.tensor_tensor(dst[:, i], src[:, i], row(f"{p}.bv").rearrange("p (h d) -> p h d", h=H), ALU.add)
                ins.then_inc(v_ready.sem, 1)

            def keys(p, new, g):
                if p == "L0a":
                    return
                dve.wait_ge(k_psum.sem, k_psum.at(p, new, g))
                r = strip_of(3)
                dve.tensor_scalar(KD.rearrange("p (i g) j t -> p i g j t", g=HG)[r, :, g, 3, :], tile(PS[K_BANK[g]][r]),
                                  col(f"{p}.bk", g)[r], 0.0 if p == "L0x" else None, ALU.add,
                                  ALU.max if p == "L0x" else ALU.bypass).then_inc(k_ready_dve.sem, 1)

            def queries(p, new, g):
                dve.wait_ge(q_psum.sem, q_psum.at(p, new, g))
                dve.tensor_scalar(QT[:, g, :], PS[Q_BANK[g]], col(f"{p}.bq", g), 0.0 if p == "L0x" else None, ALU.add,
                                  ALU.max if p == "L0x" else ALU.bypass).then_inc(q_ready.sem, 1)

            def small(p, it, more):
                if p == "L1x":
                    dve.wait_ge(mask_ready.sem, mask_ready.at(p, it))
                    dve.tensor_reduce(FULL[:, 0, :], MKB[:], AX_X, ALU.min)
                    dve.drain()
                    dve.tensor_scalar(FULL[:, 1, :], FULL[:, 0, :], -1.0, 1.0, ALU.mult, ALU.add)
                if p == "L0a":
                    dve.drain()
                    for j in range(2, 4):
                        for ins in spread_q(dve.tensor_copy, j):
                            pass
                        ins.then_inc(qd_ready.sem, 1)
                    for c in range(1, 16, 2):
                        dve.wait_ge(pos_psum.sem, pos_psum.at(p, it, c))
                        dve.tensor_copy(POS.rearrange("p u j s -> p (u j) s")[:, :, 8 * c:8 * c + 8],
                                        PS[1 + c % 4].rearrange("p (s u) -> p u s", u=64)
                                        ).then_inc(pos_odd.sem, 1)
                def first_keys():
                    keys(p, it + 1, 0)
                    keys(p, it + 1, 1)

                attend(p, it, normalise, fill=first_keys if more else None)
                if p == "L0x":
                    dve.drain()
                    add_to_x(p, it, ON[:])
                if more:
                    keys(p, it + 1, 2)
                    keys(p, it + 1, 3)
                    values(p, it + 1)
                    queries(p, it + 1, 0)
                    queries(p, it + 1, 1)
                if p != "L0x":
                    dve.wait_ge(y_psum.sem, y_psum.at(p, it))
                    add_to_x(p, it, tile(PS[6]), None if p == "L0a" else row(f"{p}.bo"))
                if more:
                    queries(p, it + 1, 2)
                    queries(p, it + 1, 3)

            def residual(p, it, bias):
                dve.drain()
                dve.tensor_tensor(tile(RES[:]), XN[:], mid(bias), ALU.add)

            def l1_attention(p, it):
                residual(p, it, row("L1a.bo"))
                for c in range(8):
                    dve.wait_ge(q_psum.sem, q_psum.at(p, it, c))
                    dve.tensor_scalar(Q1[:, c, :], PS[c % 4], col("L1a.bq", c), None, ALU.add).then_inc(q_ready.sem, 1)
                for c in range(8):
                    dve.wait_ge(v_psum.sem, v_psum.at(p, it, c))
                    i, h8 = c // 2, 8 * (c % 2)
                    dve.tensor_tensor(V1[:, i, h8:h8 + 8, 0:64], PS[c % 4].rearrange("p (h d) -> p h d", h=8),
                                      row("L1a.bv")[:, h8 * 64:h8 * 64 + 512].rearrange("p (h d) -> p h d", h=8),
                                      ALU.add).then_inc(v_ready.sem, 1)

                def norm(u):
                    i, g = u // HG, u % HG
                    dve.wait_ge(pv_done.sem, pv_done.at(p, it, u))
                    o = PS[6 + u % 2][:, 0:260].rearrange("p (h d) -> p h d", h=4)
                    dve.reciprocal(RD[:, 4 * g:4 * g + 4], o[:, :, 64])
                    dve.drain()
                    if g == 0 and i:
                        dve.wait_ge(ot_psum.sem, ot_psum.at(p, it, 2 * i - 1))
                    dve.tensor_tensor(ON1[:, g * 256:(g + 1) * 256].rearrange("p (h d) -> p h d", h=4), o[:, :, 0:64],
                                      last(RD[:, 4 * g:4 * g + 4], 64), ALU.mult).then_inc(on_ready.sem, 1)

                def take_y(i):
                    dve.wait_ge(y_psum.sem, y_psum.at(p, it, i))
                    dve.tensor_tensor(TMP[:, tok(i)], PS[0][:, 0:P], RES[:, tok(i)], ALU.add).then_inc(y_taken.sem, 1)

                attend(p, it, None, norm, take_y)
                post_norm(p, it, 1e-3)

            def post_norm(p, it, eps):
                dve.drain()
                moments(lambda i: TMP[:, tok(i)], MV2)
                dve.tensor_scalar(VEPS[:, 1, :], MV2[:, :, 1], eps, None, ALU.add).then_inc(stats_ready.sem, 1)
                dve.wait_ge(rstd_ready.sem, rstd_ready.at(p, it))
                for i in range(GB):
                    dve.tensor_scalar(TMP2[:, tok(i)], TMP[:, tok(i)], MV2[:, i, 0:1], RSTD[:, 1, i:i + 1], ALU.subtract, ALU.mult)
                dve.drain()
                dve.tensor_tensor(tile(TMP2[:]), tile(TMP2[:]), mid(row(f"{p}.gamma")), ALU.mult)
                dve.drain()
                add_to_x(p, it, tile(TMP2[:]), row(f"{p}.beta"))

            def magnitudes(src, k, n):
                dve.tensor_reduce(AM[:, k, n], src, AX_X, ALU.max)
                dve.tensor_reduce(QS[:, k, n], src, AX_X, ALU.min)

            def factors(p, it, k, width):
                dve.drain()
                dve.scalar_tensor_tensor(AM[:, k, :], QS[:, k, :], -1.0, AM[:, k, :], ALU.mult, ALU.max)
                rstd = rms(p, it, k, width)
                if rstd is None:
                    dve.drain()
                else:
                    dve.tensor_tensor(AM[:, k, :], AM[:, k, :], rstd, ALU.mult)
                    dve.drain()
                dve.tensor_scalar(AM[:, k, :], AM[:, k, :], 1e-5, None, ALU.max)
                dve.drain()
                dve.reciprocal(QS[:, k, :], AM[:, k, :])
                dve.drain()
                if rstd is not None:
                    dve.scalar_tensor_tensor(QS[:, k, :], QS[:, k, :], 127.0, rstd, ALU.mult, ALU.mult)
                else:
                    dve.tensor_scalar(QS[:, k, :], QS[:, k, :], 127.0, None, ALU.mult)
                dve.drain()

            def rounded(t, k):
                for i in range(GB):
                    dve.tensor_scalar(t[:, i, :], t[:, i, :], QS[:, k, i:i + 1], ROUND, ALU.mult, ALU.add)
                dve.drain()
                for i in range(GB):
                    yield dve.tensor_scalar(t[:, i, :], t[:, i, :], ROUND, 127.0, ALU.subtract, ALU.min)

            def quantise_weights(p, value):
                dve.wait_ge(loaded[W_PHASE.index(p)], 16)
                names = ("gate", "up", "down") if p == "L0f" else ("w1", "w1", "w2")
                for m, n in enumerate(names):
                    dve.scalar_tensor_tensor(WTMP[:, m, :], w(f"{p}.{n}"), -1.0, w(f"{p}.{n}"), ALU.mult, ALU.max)
                dve.drain()
                dve.tensor_reduce(WSC[:, 0, :], WTMP, AX_X, ALU.add).then_inc(wsum_ready, 1)
                dve.wait_ge(wsum_psum, value)
                dve.tensor_scalar(WSC[:, 1, :], PS[0][:, 0:3], 1.0 / (P * INNER), 1e-5, ALU.mult, ALU.max)
                dve.drain()
                dve.reciprocal(WSC[:, 2, :], WSC[:, 1, :])
                dve.drain()
                for m, n in enumerate(names):
                    dve.tensor_scalar(WTMP[:, m, :], w(f"{p}.{n}"), WSC[:, 2, m:m + 1], ROUND, ALU.mult, ALU.add)
                dve.drain()
                dve.tensor_scalar(WTMP, WTMP, ROUND, 1.0, ALU.subtract, ALU.min)
                dve.drain()
                dve.tensor_scalar(WQ, WTMP, -1.0, None, ALU.max).then_inc(wq_ready, 1)
                dve.drain()

            def bit_ffn(p, it):
                dve.drain()
                magnitudes(XN[:], 0, slice(0, GB))
                factors(p, it, 0, P)
                for ins in rounded(XN, 0):
                    pass
                ins.then_inc(xq_ready.sem, 1)
                for m in range(2):
                    ins = dve.tensor_scalar(DQ[:, m, :], AM[:, 0, :], WSC[:, 1, m:m + 1], 1.0 / 127.0, ALU.mult, ALU.mult)
                if p == "L0f":
                    ins.then_inc(dq_ready.sem, 1)
                dve.drain()
                next_moments(p, it)
                if p == "L1f":
                    for i in range(GB):
                        dve.wait_ge(h_psum.sem, h_psum.at(p, it, i))
                        dve.scalar_tensor_tensor(HID[:, i, :], PS[i], DQ[:, 0, i:i + 1], row("L1f.b1"),
                                                 ALU.mult, ALU.add).then_inc(pre_ready.sem, 1)
                next_normed(p, it)
                for i in range(GB):
                    dve.wait_ge(act_ready.sem, act_ready.at(p, it, i))
                    if p == "L0f":
                        dve.scalar_tensor_tensor(HID[:, i, :], PS[4 + i], DQ[:, 1, i:i + 1], HID[:, i, :], ALU.mult, ALU.mult)
                        dve.drain()
                    magnitudes(HID[:, i, :], 1, slice(i, i + 1))
                factors(p, it, 1, INNER)
                for ins in rounded(HID, 1):
                    ins.then_inc(hq_ready.sem, 1)
                dve.drain()
                dve.tensor_scalar(DQ[:, 2, :], AM[:, 1, :], WSC[:, 1, 2:3], 1.0 / 127.0, ALU.mult, ALU.mult)
                dve.drain()
                dve.wait_ge(y_psum.sem, y_psum.at(p, it))
                for i in range(GB):
                    if p == "L0f":
                        ins = dve.scalar_tensor_tensor(seq(it, i), PS[4][:, tok(i)], DQ[:, 2, i:i + 1], seq(it, i), ALU.mult, ALU.add)
                    else:
                        dve.scalar_tensor_tensor(TMP[:, tok(i)], PS[4][:, tok(i)], DQ[:, 2, i:i + 1], row("L1f.b2"), ALU.mult, ALU.add)
                if p == "L0f":
                    ins.then_inc(x_updated.sem, 1)
                    dve.drain()
                else:
                    dve.drain()
                    add_to_x(p, it, tile(TMP[:]))

            def rms(p, it, k, width):
                if p == "L0f":
                    return None
                dve.wait_ge(squares_ready.sem, squares_ready.at(p, it, k))
                dve.tensor_scalar(VEPS[:, 1, :], SS[:, k, :], 1.0 / width, 1e-6, ALU.mult, ALU.add).then_inc(stats_ready.sem, 1)
                dve.drain()
                dve.wait_ge(rstd_ready.sem, rstd_ready.at(p, it, k))
                return RSTD[:, 1, :]

            def linear_attention(p, it):
                next_moments(p, it)
                dve.wait_ge(gates_psum.sem, gates_psum.at(p, it))
                dve.tensor_tensor(tile(SG[:, 0, :]), tile(PS[1][:, 0:64]), mid(row("L2a.gates")), ALU.add).then_inc(gates_biased.sem, 1)
                dve.wait_ge(gates_exp.sem, gates_exp.at(p, it))
                dve.tensor_scalar(SG[:, 1, :], SG[:, 1, :], 1.0, None, ALU.add)
                dve.drain()
                dve.reciprocal(SG[:, 6, :], SG[:, 1, :])
                dve.drain()
                sig = tile(SG[:, 6, :])
                dve.tensor_scalar(tile(SG[:, 2, 0:32]), sig[:, :, 0:8], 0.999 - 0.85, 0.85, ALU.mult, ALU.add).then_inc(beta_ready.sem, 1)
                for n, (dst, bank, swapped) in enumerate(((KT, 2, 4), (QT, 6, 2))):
                    dve.wait_ge(proj_psum.sem, proj_psum.at(p, it, n))
                    pair = lambda lo: PSA[:, lo:lo + 2, :].rearrange("p g (b t) -> p (g b) t", b=GB)
                    d = dst[:, 0:2, :].rearrange("p g (b t) -> p (g b) t", b=GB)
                    e = dst[:, 2:4, :].rearrange("p g (b t) -> p (g b) t", b=GB)
                    dve.tensor_tensor(d, pair(bank), mid(const("cos"), 2 * GB), ALU.mult)
                    dve.tensor_tensor(e, pair(swapped), mid(const("sin"), 2 * GB), ALU.mult)
                    dve.drain()
                    dve.tensor_tensor(d, d, e, ALU.add).then_inc(proj_ready.sem, 1)
                dve.wait_ge(decay_ready.sem, decay_ready.at(p, it))
                dve.tensor_tensor(tile(SG[:, 7, 0:32]), tile(SG[:, 5, 0:32]), sig[:, :, 8:16], ALU.mult)
                dve.drain()
                heads = lambda ap: ap.rearrange("p (u d) -> p u d", u=32)
                dve.tensor_tensor(heads(VE16.rearrange("p b d -> p (b d)")), heads(PS[0]), last(SG[:, 7, 0:32], 16),
                                  ALU.mult).then_inc(vp_ready.sem, 1)
                next_normed(p, it)

                def norm(i):
                    dve.wait_ge(pv_done.sem, pv_done.at(p, it, 2 * i + 1))
                    dve.tensor_tensor(ON[:, i, :].rearrange("p (h d) -> p h d", h=8),
                                      PS[6 + i % 2][:, 0:P].rearrange("p (h d) -> p h d", h=8),
                                      last(SG[:, 4, 8 * i:8 * i + 8], 16), ALU.mult).then_inc(on_ready.sem, 1)

                for u in range(8):
                    dve.wait_ge(s2_psum.sem, s2_psum.at(p, it, u))
                    if u >= 2:
                        dve.wait_ge(pv_done.sem, pv_done.at(p, it, u - 2))
                    dve.tensor_tensor(tile(PR[:, u % 2, :]), tile(PS[4 + u % 2]), mid(const("tri")), ALU.mult).then_inc(p_ready.sem, 1)
                    if u >= 3 and u % 2:
                        norm(u // 2 - 1)
                norm(GB - 1)
                dve.wait_ge(y_psum.sem, y_psum.at(p, it))
                add_to_x(p, it, tile(PS[6]), row("L2a.bo"))

            def experts(p, it):
                next_moments(p, it)
                dve.wait_ge(act_ready.sem, act_ready.at(p, it, 1))
                dve.tensor_tensor(HIDT[:, 0:2, :], HIDT[:, 0:2, :], PSA[:, 2:4, :], ALU.mult).then_inc(shared_ready.sem, 1)
                dve.wait_ge(act_ready.sem, act_ready.at(p, it, 2))
                v = lambda k: tile(SG[:, k, 0:32])
                s, sel, pick, a, b, rank = v(0), v(1), v(2), v(3), v(4), mid(row("rank"))
                small_ = lambda k: SG[:, 5, k * GB:(k + 1) * GB]
                dve.tensor_tensor(sel, s, mid(row("L2f.bias")), ALU.add)
                dve.drain()
                for n in range(2):
                    dve.tensor_reduce(small_(0), sel, AX_X, ALU.max)
                    dve.drain()
                    dve.tensor_tensor(a, sel, last(small_(0), 8), ALU.is_equal)
                    dve.drain()
                    dve.tensor_tensor(a, a, rank, ALU.mult)
                    dve.drain()
                    dve.tensor_reduce(small_(1), a, AX_X, ALU.max)
                    dve.drain()
                    dve.tensor_tensor(a, a, last(small_(1), 8), ALU.is_equal)
                    dve.drain()
                    if n == 0:
                        dve.tensor_copy(pick, a)
                        dve.scalar_tensor_tensor(sel, a, -1e30, sel, ALU.mult, ALU.add)
                    else:
                        dve.tensor_tensor(pick, pick, a, ALU.add)
                    dve.drain()
                dve.tensor_tensor(a, pick, s, ALU.mult)
                dve.drain()
                dve.tensor_reduce(small_(0), a, AX_X, ALU.add)
                dve.drain()
                dve.tensor_scalar(small_(1), small_(0), 1e-9, None, ALU.add)
                dve.tensor_scalar(small_(2), small_(0), 1e-9, None, ALU.is_gt)
                dve.drain()
                dve.reciprocal(small_(1), small_(1))
                dve.tensor_scalar(small_(3), small_(2), -0.5, 0.5, ALU.mult, ALU.add)
                dve.drain()
                dve.tensor_tensor(small_(1), small_(1), small_(2), ALU.mult)
                dve.tensor_tensor(b, pick, last(small_(3), 8), ALU.mult)
                dve.drain()
                dve.tensor_tensor(a, a, last(small_(1), 8), ALU.mult)
                dve.drain()
                dve.tensor_tensor(a, a, b, ALU.add)
                next_normed(p, it)
                dve.wait_ge(shared_psum.sem, shared_psum.at(p, it))
                dve.tensor_copy(ACC, tile(PS[7]))
                dve.drain()
                for e in range(8):
                    dve.wait_ge(expert_psum.sem, expert_psum.at(p, it, e))
                    for i in range(GB):
                        ins = dve.scalar_tensor_tensor(ACC[:, i, :], PS[2 + e % 2][:, tok(i)], SG[:, 3, 8 * i + e:8 * i + e + 1],
                                                       ACC[:, i, :], ALU.mult, ALU.add)
                    ins.then_inc(expert_used.sem, 1)
                    dve.drain()
                dve.wait_ge(y_psum.sem, y_psum.at(p, it))
                add_to_x(p, it, ACC)

            def delta_project(p, it):
                next_moments(p, it)
                dve.wait_ge(proj_psum.sem, proj_psum.at(p, it))
                for m, n in enumerate("qkv"):
                    dve.tensor_scalar(XP[:, m, :, 3:3 + P], tile(PS[m]), col(f"L3a.b{n}"), None, ALU.add).then_inc(xp_ready.sem, 1)
                next_normed(p, it)
                dve.wait_ge(silu_ready.sem, silu_ready.at(p, it, 0))
                dve.tensor_tensor(TMP[:], CV[:, 0, :], CV[:, 0, :], ALU.mult)
                dve.wait_ge(silu_ready.sem, silu_ready.at(p, it, 1))
                dve.tensor_tensor(TMP2[:], CV[:, 1, :], CV[:, 1, :], ALU.mult).then_inc(square_ready.sem, 1)
                dve.wait_ge(norm_ready.sem, norm_ready.at(p, it))
                dve.tensor_scalar(NORM, NORM, 1e-6, None, ALU.add)
                dve.drain()
                dve.reciprocal(NORM, NORM)
                dve.drain()
                for m, t in enumerate((TMP, TMP2)):
                    ins = dve.tensor_copy(t[:].rearrange("p (b h d) -> p b h d", b=GB, h=H),
                                          last(NORM.rearrange("p (b m h) -> p b m h", b=GB, m=2)[:, :, m], HD))
                ins.then_inc(norm_inverse.sem, 1)
                dve.wait_ge(inverse_psum.sem, inverse_psum.at(p, it))
                dve.tensor_tensor(CV[:, 0:2, :], CV[:, 0:2, :], PSA[:, 6:8, :], ALU.mult).then_inc(store_ready.sem, 1)

            def scan():
                dve.wait_ge(scan_loaded, 80)
                dve.tensor_tensor(SAB, SA, SBT, ALU.mult)
                for h in range(2):
                    dve.tensor_tensor(SV[:, 8 * h:8 * h + 8, :], SV[:, 8 * h:8 * h + 8, :], mid(SBT[:, h, :], 8), ALU.mult)
                dve.memset(STATE[:, 0], 0.0)
                dve.drain()
                for h in range(2):
                    dve.scalar_tensor_tensor(SKK[:, 8 * h:8 * h + 8, :], SK[:, 8 * h:8 * h + 8, :], -1.0, mid(SAB[:, h, :], 8),
                                             ALU.mult, ALU.mult)
                dve.drain()
                with dve.Fori(0, P // CHUNK) as it:
                    chunk = lambda ap: ap[:, :, bass.ds(it * CHUNK, CHUNK)].rearrange("p f t -> p t f")
                    dve.tensor_copy(SP9[:, :, :, HD], chunk(SV))
                    dve.tensor_copy(CK[:, 0], chunk(SK))
                    dve.tensor_copy(CK[:, 1], chunk(SKK))
                    dve.tensor_copy(CK[:, 2], chunk(SQ))
                    dve.tensor_copy(CA, chunk(SA))
                    dve.drain()
                    by_head = lambda ap: ap.rearrange("p (h d) e -> p h d e", h=2)
                    key = lambda m, n: CK[:, m, n].rearrange("p (h e) -> p h e", h=2).unsqueeze(2).to_broadcast([P, 2, 8, 8])
                    k = -1
                    for n in range(CHUNK):
                        now, new = STATE[:, n % 2], STATE[:, (n + 1) % 2]
                        if n:
                            dve.wait_ge(scan_step.sem, scan_step.at("scan", it, k))
                        products, k = k + 1, k + 2
                        dve.tensor_tensor(by_head(SP9[:, n, :, 0:HD]), by_head(now), key(1, n), ALU.mult).then_inc(scan_step.sem, 1)
                        dve.tensor_tensor(new.rearrange("p (h d) e -> p h (d e)", h=2), now.rearrange("p (h d) e -> p h (d e)", h=2),
                                          last(CA[:, n], 64), ALU.mult).then_inc(scan_step.sem, 1)
                        dve.wait_ge(scan_step.sem, scan_step.at("scan", it, products))
                        u, k = k + 1, k + 1
                        dve.tensor_reduce(SU, SP9[:, n], AX_X, ALU.add).then_inc(scan_step.sem, 1)
                        if n:
                            q_products, k = k + 1, k + 1
                            dve.tensor_tensor(by_head(SPQ), by_head(now), key(2, n - 1), ALU.mult).then_inc(scan_step.sem, 1)
                        dve.wait_ge(scan_step.sem, scan_step.at("scan", it, u))
                        outer, k = k + 1, k + 1
                        dve.tensor_tensor(by_head(ST2), last(SU.rearrange("p (h d) -> p h d", h=2), HD), key(0, n), ALU.mult
                                          ).then_inc(scan_step.sem, 1)
                        if n:
                            dve.wait_ge(scan_step.sem, scan_step.at("scan", it, q_products))
                            k += 1
                            dve.tensor_reduce(OUTC[:, n - 1], SPQ, AX_X, ALU.add).then_inc(scan_step.sem, 1)
                        dve.wait_ge(scan_step.sem, scan_step.at("scan", it, outer))
                        k += 1
                        dve.tensor_tensor(new, new, ST2, ALU.add).then_inc(scan_step.sem, 1)
                    dve.wait_ge(scan_step.sem, scan_step.at("scan", it, k))
                    dve.tensor_tensor(by_head(SPQ), by_head(STATE[:, 0]), key(2, CHUNK - 1), ALU.mult).then_inc(scan_step.sem, 1)
                    dve.wait_ge(scan_step.sem, scan_step.at("scan", it, k + 1))
                    dve.tensor_reduce(OUTC[:, CHUNK - 1], SPQ, AX_X, ALU.add).then_inc(scan_step.sem, 1)
                    dve.wait_ge(scan_step.sem, scan_step.at("scan", it, k + 2))
                    dve.tensor_copy(SO[:, :, bass.ds(it * CHUNK, CHUNK)].rearrange("p f t -> p t f"), OUTC)
                    dve.drain()
                both = SO.rearrange("p (h d) t -> p h (d t)", h=2)
                dve.tensor_reduce(RD[:, 0:2], both, AX_X, ALU.add)
                dve.tensor_tensor(PROD, SO.rearrange("p f t -> p (f t)"), SO.rearrange("p f t -> p (f t)"), ALU.mult)
                dve.drain()
                dve.tensor_reduce(RD[:, 2:4], tile(PROD, 2), AX_X, ALU.add)
                dve.tensor_scalar(RD[:, 0:2], RD[:, 0:2], 1.0 / (P * HD), None, ALU.mult)
                dve.drain()
                dve.tensor_tensor(RD[:, 4:6], RD[:, 0:2], RD[:, 0:2], ALU.mult)
                dve.tensor_scalar(RD[:, 2:4], RD[:, 2:4], 1.0 / (P * HD), 1e-5, ALU.mult, ALU.add)
                dve.drain()
                dve.tensor_tensor(RD[:, 6:8], RD[:, 2:4], RD[:, 4:6], ALU.subtract).then_inc(gn_var, 1)
                dve.wait_ge(gn_rstd, 1)
                for h in range(2):
                    ins = dve.tensor_scalar(both[:, h], both[:, h], RD[:, h:h + 1], RD[:, 8 + h:9 + h], ALU.subtract, ALU.mult)
                ins.then_inc(scan_done, 1)

            def delta_out(p, it):
                dve.tensor_scalar(TMP[:], YT[:, bass.ds(it * T, T)], col("L3a.scale"), col("L3a.bias"), ALU.mult, ALU.add)
                dve.drain()
                dve.tensor_tensor(TMP2[:], TMP[:], GT[:, bass.ds(it * T, T)], ALU.mult).then_inc(gated.sem, 1)
                dve.wait_ge(y_psum.sem, y_psum.at(p, it))
                add_to_x(p, it, tile(PS[1]), row("L3a.bo"))

            def one_head(p, it):
                next_moments(p, it)
                dve.wait_ge(proj_psum.sem, proj_psum.at(p, it))
                dve.tensor_tensor(ON[:], tile(PS[2]), mid(row("L3x.bv")), ALU.add).then_inc(proj_ready.sem, 1)
                next_normed(p, it)
                dve.wait_ge(s3_psum.sem, s3_psum.at(p, it))
                s = tile(TMP[:])
                dve.scalar_tensor_tensor(s, tile(PS[3]), float(P // 16) ** -0.5, mid(KEEP[:, 0, :]), ALU.mult, ALU.mult)
                dve.drain()
                dve.tensor_tensor(s, s, mid(KEEP[:, 1, :]), ALU.add)
                dve.drain()
                dve.tensor_reduce(MX[:, 0:GB], s, AX_X, ALU.max)
                dve.drain()
                dve.tensor_tensor(s, s, last(MX[:, 0:GB], P), ALU.subtract).then_inc(s3_shifted.sem, 1)
                dve.wait_ge(p3_ready.sem, p3_ready.at(p, it))
                dve.tensor_reduce(RD[:, 0:GB], tile(PR[:, 0, :]), AX_X, ALU.add)
                dve.drain()
                dve.reciprocal(RD[:, GB:2 * GB], RD[:, 0:GB])
                dve.drain()
                dve.wait_ge(y_psum.sem, y_psum.at(p, it))
                for i in range(GB):
                    dve.scalar_tensor_tensor(TMP[:, tok(i)], PS[7][:, tok(i)], RD[:, GB + i:GB + i + 1], row("L3x.bo"),
                                             ALU.mult, ALU.add)
                dve.drain()
                add_to_x(p, it, tile(TMP[:]))

            def relu_ffn(p, it):
                residual(p, it, row("L3f.b2"))
                next_moments(p, it)
                next_normed(p, it)
                dve.wait_ge(y_psum.sem, y_psum.at(p, it))
                dve.tensor_tensor(TMP[:], PS[4], RES[:], ALU.add)
                post_norm(p, it, 1e-5)

            bodies = {"L1a": l1_attention, "L0f": bit_ffn, "L1f": bit_ffn, "L2a": linear_attention,
                      "L2f": experts, "L3a": delta_project, "L3o": delta_out, "L3x": one_head, "L3f": relu_ffn}
            for n, p in enumerate(run):
                if p == "scan":
                    scan()
                    continue
                if p in ("L0f", "L1f"):
                    quantise_weights(p, quantised.index(p) + 1)
                if p == "L1a":
                    dve.nop().then_inc(y_taken.sem, 1)
                if p == "L3o":
                    dve.wait_ge(y_loaded, 16)
                if p == "L3a":
                    for m, n in enumerate("qkv"):
                        for tap in range(4):
                            ins = dve.tensor_scalar(TAPS[:, m, tap, :], ident, col(f"L3a.conv{n}", tap), None, ALU.mult)
                    ins.then_inc(taps_ready, 1)
                    dve.memset(XP[:, :, :, 0:3], 0.0).then_inc(stored.sem, 1)
                if p == "L3x":
                    dve.wait_ge(masks_loaded, 16 * (1 + ("L1x" in run)))
                    dve.tensor_copy(KEEP[:, 1, :], MASK3[:])
                    dve.drain()
                    dve.tensor_scalar(KEEP[:, 0, :], KEEP[:, 1, :], 0.0, None, ALU.not_equal)
                    dve.drain()
                    dve.tensor_scalar(KEEP[:, 1, :], KEEP[:, 0, :], -NEG, NEG, ALU.mult, ALU.add)
                    dve.drain()
                if p in before_loop:
                    next_moments(p, BEFORE_LOOP)
                    next_normed(p, BEFORE_LOOP)
                if p == run[0]:
                    dve.wait_ge(rest_loaded, 32)
                if p in SMALL:
                    if kd_zeroed(p):
                        dve.wait_ge(kd_zero, kd_zeroed(p))
                    for g in range(HG):
                        keys(p, 0, g)
                    values(p, 0)
                    for g in range(HG):
                        queries(p, 0, g)
                    with dve.Fori(0, GROUPS - 1) as it:
                        small(p, it, True)
                    small(p, GROUPS - 1, False)
                    continue
                with dve.Fori(0, GROUPS) as it:
                    bodies[p](p, it)


def strips(a, heads=16, width=HD):
    a = a.reshape(*a.shape[:-1], heads, width)
    out = np.zeros((*a.shape[:-1], STRIP), a.dtype)
    out[..., :width] = a
    return out.reshape(*a.shape[:-2], heads * STRIP)


def chunks(a):
    n = a.shape[0] // P
    return a.reshape(n, P, a.shape[1]).transpose(1, 0, 2).reshape(P, -1)


def neighbours(a):
    return a.reshape(a.shape[0], -1, 2)[:, :, ::-1].reshape(a.shape)


def tables():
    k = np.zeros((P, K_ALL), np.float32)

    def put(name, a):
        k[:, K_AT[name][0]:K_AT[name][0] + P] = a

    put("ident", np.eye(P))
    put("tri", np.triu(np.ones((P, P))))
    half = 8
    inv = (1.0 / 10000.0 ** (np.arange(half, dtype=np.float32) / np.float32(half))).astype(np.float32)
    freqs = (np.arange(P, dtype=np.float32)[:, None] * inv[None, :]).astype(np.float32)
    cos, sin = np.zeros((P, P), np.float32), np.zeros((P, P), np.float32)
    for r in range(P):
        d = r % STRIP
        if d < 16:
            cos[r] = np.cos(freqs[:, d // 2])
            sin[r] = np.sin(freqs[:, d // 2]) * (-1.0 if d % 2 == 0 else 1.0)
    put("cos", cos)
    put("sin", sin)
    put("heads", np.kron(np.eye(H), np.ones((HD, HD))))
    return k


def lay_out(inp):
    a = {k: np.asarray(v) for k, v in inp.items()}
    parts = {}
    for p, t in (("L0a", "L0_attn"), ("L0x", "L0_xattn"), ("L1x", "L1_xattn")):
        parts[f"{p}.q"] = strips(a[f"{t}_Wq"].T)
        parts[f"{p}.k"] = strips(a[f"{t}_Wk"].T)
        parts[f"{p}.v"] = a[f"{t}_Wv"].T
    parts["L0a.o"] = a["L0_attn_Wp"].T
    table = np.zeros((4, STRIP, 2 * P), np.float32)
    for r in range(4):
        table[r, :HD, :] = a["L0_attn_pos_emb_k"][(np.arange(2 * P) - (P - 1) - r) % (2 * P)].T
    parts["L0a.pe"] = table.reshape(P, 2 * P)
    parts["L0f.gate"], parts["L0f.up"] = a["L0_ffn_w_gate"].T, a["L0_ffn_w_up"].T
    parts["L0f.down"] = chunks(a["L0_ffn_w_down"].T)
    for n in "qkv":
        parts[f"L1a.{n}"] = a[f"L1_attn_W{n}"].reshape(P, 1024)
    parts["L1a.o"] = chunks(a["L1_attn_Wo"].reshape(1024, P))
    parts["L1x.o"] = a["L1_xattn_Wo"].T
    parts["L1f.w1"], parts["L1f.w2"] = a["L1_ffn_w1"].T, chunks(a["L1_ffn_w2"].T)
    for n in "qk":
        t = a[f"L2_attn_W{n}"].T
        parts[f"L2a.{n}"], parts[f"L2a.{n}s"] = strips(t, 8, 16), strips(neighbours(t), 8, 16)
        parts[f"L2x.{n}"] = strips(a[f"L2_xattn_W{n}"])
    parts["L2a.v"], parts["L2a.o"] = a["L2_attn_Wv"].T, a["L2_attn_Wo"].T
    parts["L2a.gates"] = np.concatenate([a["L2_attn_Wbeta"].T, a["L2_attn_Walpha"].T], 1)
    parts["L2x.v"], parts["L2x.o"] = a["L2_xattn_Wv"], a["L2_xattn_Wo"]
    parts["L2f.sw1"], parts["L2f.sw3"], parts["L2f.sw2"] = a["L2_ffn_sw1"], a["L2_ffn_sw3"], chunks(a["L2_ffn_sw2"])
    parts["L2f.router"] = a["L2_ffn_router_w"].T
    for n in ("ew1", "ew2"):
        parts[f"L2f.{n}"] = a[f"L2_ffn_{n}"].transpose(1, 0, 2).reshape(P, -1)
    for n in "qkvgabo":
        parts[f"L3a.{n}"] = a[f"L3_attn_W{n}"]
    for n in "qkvo":
        parts[f"L3x.{n}"] = a[f"L3_xattn_W{n}"]
    parts["L3f.w1"], parts["L3f.w2"] = a["L3_ffn_w1"][0], chunks(a["L3_ffn_w2"][0])
    w = np.concatenate([parts[n] for n in W_AT], 1)

    c = {}
    for p in SMALL:
        for n in "qk":
            b = strips(a[f"{p[:2]}_xattn_b{n}"]) if p in ("L1x", "L2x") else np.zeros(H * STRIP, np.float32)
            c[f"{p}.b{n}"] = b.reshape(HG, P).T
    for n in "qk":
        c[f"L1a.b{n}"] = a[f"L1_attn_b{n}"].reshape(8, P).T
        c[f"L3x.b{n}"] = a[f"L3_xattn_b{n}"][:, None]
    for n in "qkvg":
        c[f"L3a.b{n}"] = a[f"L3_attn_b{n}"][:, None]
    c["L3a.scale"], c["L3a.bias"] = a["L3_attn_gn_scale"][:, None], a["L3_attn_gn_bias"][:, None]
    for n in "ab":
        c[f"L3a.b{n}"] = np.concatenate([a[f"L3_attn_b{n}"], np.zeros(P - H, np.float32)])[:, None]
    for n in "qkv":
        c[f"L3a.conv{n}"] = a[f"L3_attn_{n}_conv"]
    c["L3f.b1"] = a["L3_ffn_b1"][0].reshape(4, P).T
    cols = np.concatenate([c[n] for n in C_AT], 1)

    r = {"L1a.bv": a["L1_attn_bv"], "L2a.gates": np.concatenate([a["L2_attn_bbeta"], a["L2_attn_balpha"]]),
         "L2f.bias": a["L2_ffn_router_bias"], "L1f.b1": a["L1_ffn_b1"], "L1f.b2": a["L1_ffn_b2"],
         "L3f.b2": a["L3_ffn_b2"][0], "rank": np.arange(8, 0, -1, dtype=np.float32)}
    for p, t in (("L1a", "L1_attn"), ("L1x", "L1_xattn"), ("L2a", "L2_attn"), ("L2x", "L2_xattn"), ("L3a", "L3_attn"),
                 ("L3x", "L3_xattn"), ("L3f", "L3_ffn")):
        for n in ("bv", "bo", "gamma", "beta"):
            if f"{p}.{n}" in R_AT and f"{p}.{n}" not in r:
                r[f"{p}.{n}"] = a[f"{t}_{n}"]
    rows = np.concatenate([r[n].reshape(-1) for n in R_AT])[None, :]

    return {"x": a["x"], "ctx_t": a["ctx_1024"].transpose(2, 0, 1).reshape(P, B * P),
            "mask1": a["mask_Bx1xSxS2_bk1"], "mask3": a["mask_SxS2_ik0"],
            "w": w, "cols": cols, "rows": rows, "consts": tables()}


def build(nc, arrays, phases=PHASES):
    args = [nc.dram_tensor(f"in_{n}", a.shape, mybir.dt.from_np(a.dtype), kind="ExternalInput").ap() for n, a in arrays.items()]
    out = nc.dram_tensor("out", (B, P, P), F32, kind="ExternalOutput").ap()
    decoder(nc, *args, out, phases=phases)


def kernel(**inputs):
    import concourse.bacc as bacc
    from concourse.bass_utils import run_bass_kernel_spmd

    arrays = {n: np.ascontiguousarray(a) for n, a in lay_out(inputs).items()}
    nc = bacc.Bacc("TRN2", target_bir_lowering=False, num_devices=1)
    build(nc, arrays)
    r = run_bass_kernel_spmd(nc, [{f"in_{n}": a for n, a in arrays.items()}], core_ids=[0])
    return r.results[0]["out"]
```
